# Optimizing a Trainium2 kernel written in Bass

```python
import numpy as np
import jax
import jax.numpy as jnp

def _softmax(x, axis=-1):
    return jax.nn.softmax(x, axis=axis)

def _gelu(x):
    return jax.nn.gelu(x, approximate=True)

def _silu(x):
    return jax.nn.silu(x)

def _sigmoid(x):
    return jax.nn.sigmoid(x)

def _layernorm(x, axis=-1, eps=1e-05):
    m = jnp.mean(x, axis=axis, keepdims=True)
    v = jnp.var(x, axis=axis, keepdims=True)
    return (x - m) / jnp.sqrt(v + eps)

def _scatter_add(tgt, idx, src, axis=0):
    return tgt.at[idx].add(src)

def _segment_sum(src, seg, n):
    return jax.ops.segment_sum(src, seg, n)
kernel_name = 'mk_flamingo_gated_d2_seqx_r8_3d5a85'

def setup_inputs(seed: int=0):
    np.random.seed(seed)
    _w = jnp.asarray

    def _rec_inputs():
        import jax
        import jax.numpy as jnp
        _rk = jax.random.key(seed)
        x = -0.000929 + 1 * jax.random.normal(jax.random.fold_in(_rk, 1), (4, 512, 128), jnp.float32)
        _lenS = 512 - jax.random.randint(jax.random.fold_in(_rk, 7), (4,), 0, max(1, 512 // 4) + 1, jnp.int32)
        _lenS2 = 77 - jax.random.randint(jax.random.fold_in(_rk, 8), (4,), 0, max(1, 77 // 4) + 1, jnp.int32)
        _ctx_1024P = jax.random.normal(jax.random.fold_in(_rk, 11), (4, 16, 128), jnp.float32)
        _ctx_1024c = jax.random.dirichlet(jax.random.fold_in(_rk, 511), 0.3 * jnp.ones((16,), jnp.float32), (4, 77))
        _ctx_1024t = jnp.einsum('bsk,bkd->bsd', _ctx_1024c, _ctx_1024P)
        _ctx_1024t = _ctx_1024t * jax.lax.rsqrt(jnp.mean(jnp.square(_ctx_1024t)) + 1e-12) * 0.953939
        ctx_1024 = -1.52775e-05 + 0.999936 * (_ctx_1024t + 0.3 * jax.random.normal(jax.random.fold_in(_rk, 611), (4, 77, 128), jnp.float32))
        _g = jax.random.normal(jax.random.fold_in(_rk, 9001), (2, 2), jnp.float32)
        _g = jnp.sign(_g) * jnp.maximum(jnp.abs(_g), 1.0) + (_g == 0) * 1.0
        g_xattn = _g[0]
        g_ffn = _g[1]
        return (x, ctx_1024, g_xattn, g_ffn)
    x, ctx_1024, g_xattn, g_ffn = _rec_inputs()

    def _L0_xattn_setup():
        import jax, jax.numpy as jnp
        import numpy as np
        DIM = 128
        H = 16
        D = 64
        INNER = H * D
        EPS = 1e-05

        def layernorm(x, w, b):
            mu = jnp.mean(x, axis=-1, keepdims=True)
            var = jnp.var(x, axis=-1, keepdims=True)
            return (x - mu) * jax.lax.rsqrt(var + EPS) * w + b
        key = jax.random.key(seed)
        ks = jax.random.split(key, 8)
        B, N, S = (4, 32, 1024)
        s = 1.0 / np.sqrt(DIM)
        return {'latents': jax.random.normal(ks[0], (B, N, DIM), jnp.float32), 'context': jax.random.normal(ks[1], (B, S, DIM), jnp.float32), 'ln_l_w': jnp.ones((DIM,), jnp.float32), 'ln_l_b': jnp.zeros((DIM,), jnp.float32), 'ln_c_w': jnp.ones((DIM,), jnp.float32), 'ln_c_b': jnp.zeros((DIM,), jnp.float32), 'Wq': jax.random.normal(ks[2], (DIM, INNER), jnp.float32) * s, 'Wkv': jax.random.normal(ks[3], (DIM, 2 * INNER), jnp.float32) * s, 'Wo': jax.random.normal(ks[4], (INNER, DIM), jnp.float32) * (1.0 / np.sqrt(INNER)), 'bo': jnp.zeros((DIM,), jnp.float32)}
    _L0_xattn_all = _L0_xattn_setup()
    _L0_xattn_in = {k: v for k, v in _L0_xattn_all.items() if k in ('ln_l_w', 'ln_l_b', 'ln_c_w', 'ln_c_b', 'Wq', 'Wkv', 'Wo', 'bo')}
    del _L0_xattn_all

    def _L0_ffn_setup():
        import jax, jax.numpy as jnp
        import numpy as np
        DIM = 128
        E = 16
        TOPK = 2
        G = 4
        TOPK_G = 2
        INTER = 64
        N_SHARED = 2
        ROUTE_SCALE = 1.0

        def _gate(xf, gate_w, gate_b):
            scores = xf @ gate_w.T
            scores = jax.nn.softmax(scores.astype(jnp.float32), axis=-1)
            orig = scores
            scores = scores + gate_b
            T = xf.shape[0]
            sg = scores.reshape(T, G, E // G)
            group_scores = jax.lax.top_k(sg, 2)[0].sum(-1)
            _, gidx = jax.lax.top_k(group_scores, TOPK_G)
            keep = jax.nn.one_hot(gidx, G).sum(axis=1) > 0
            sg = jnp.where(keep[:, :, None], sg, -jnp.inf)
            scores = sg.reshape(T, E)
            _, idx = jax.lax.top_k(scores, TOPK)
            weights = jnp.take_along_axis(orig, idx, axis=1)
            weights = (weights * ROUTE_SCALE).astype(xf.dtype)
            return (weights, idx)
        key = jax.random.key(seed)
        ks = jax.random.split(key, 16)
        s = lambda fan_in: 1.0 / np.sqrt(fan_in)
        inp = {'x': jax.random.normal(ks[0], (4, 128, DIM), dtype=jnp.float32), 'gate_w': jax.random.normal(ks[1], (E, DIM), dtype=jnp.float32) * s(DIM), 'gate_b': jnp.zeros((E,), dtype=jnp.float32), 'We1': jax.random.normal(ks[2], (E, DIM, INTER), dtype=jnp.float32) * s(DIM), 'be1': jnp.zeros((E, INTER), dtype=jnp.float32), 'We2': jax.random.normal(ks[3], (E, INTER, DIM), dtype=jnp.float32) * s(INTER), 'be2': jnp.zeros((E, DIM), dtype=jnp.float32), 'We3': jax.random.normal(ks[4], (E, DIM, INTER), dtype=jnp.float32) * s(DIM), 'be3': jnp.zeros((E, INTER), dtype=jnp.float32), 'ws1': jax.random.normal(ks[5], (DIM, N_SHARED * INTER), dtype=jnp.float32) * s(DIM), 'bs1': jnp.zeros((N_SHARED * INTER,), dtype=jnp.float32), 'ws2': jax.random.normal(ks[6], (N_SHARED * INTER, DIM), dtype=jnp.float32) * s(N_SHARED * INTER), 'bs2': jnp.zeros((DIM,), dtype=jnp.float32), 'ws3': jax.random.normal(ks[7], (DIM, N_SHARED * INTER), dtype=jnp.float32) * s(DIM), 'bs3': jnp.zeros((N_SHARED * INTER,), dtype=jnp.float32)}
        return inp
    _L0_ffn_all = _L0_ffn_setup()
    _L0_ffn_in = {k: v for k, v in _L0_ffn_all.items() if k in ('gate_w', 'gate_b', 'We1', 'be1', 'We2', 'be2', 'We3', 'be3', 'ws1', 'bs1', 'ws2', 'bs2', 'ws3', 'bs3')}
    del _L0_ffn_all

    def _L1_xattn_setup():
        import jax, jax.numpy as jnp
        import numpy as np
        from jax import lax
        BIG = jnp.float32(1e+30)

        def _pairwise_euclidean(a, b):
            aa = jnp.sum(a * a, axis=-1)[:, None]
            bb = jnp.sum(b * b, axis=-1)[None, :]
            ab = a @ b.T
            return jnp.sqrt(jnp.maximum(aa + bb - 2.0 * ab, 0.0))

        def _dtw_cost(D):
            row0 = jnp.cumsum(D[0])

            def row_step(prev_row, d_row):
                first = d_row[0] + prev_row[0]

                def col_step(left, inp):
                    d_ij, up, diag = inp
                    r = d_ij + jnp.minimum(jnp.minimum(up, left), diag)
                    return (r, r)
                _, rest = lax.scan(col_step, first, (d_row[1:], prev_row[1:], prev_row[:-1]))
                row = jnp.concatenate([first[None], rest])
                return (row, row)
            _, rows = lax.scan(row_step, row0, D[1:])
            return jnp.concatenate([row0[None], rows], axis=0)

        def _backtrack(R, T1, T2):
            L = T1 + T2 - 1

            def step(carry, _):
                i, j, done = carry
                valid = jnp.logical_not(done)
                cd = jnp.where((i > 0) & (j > 0), R[jnp.maximum(i - 1, 0), jnp.maximum(j - 1, 0)], BIG)
                cu = jnp.where(i > 0, R[jnp.maximum(i - 1, 0), j], BIG)
                cl = jnp.where(j > 0, R[i, jnp.maximum(j - 1, 0)], BIG)
                choice = jnp.argmin(jnp.stack([cd, cu, cl]))
                ni = jnp.where(choice <= 1, i - 1, i)
                nj = jnp.where((choice == 0) | (choice == 2), j - 1, j)
                at_origin = (i == 0) & (j == 0)
                ni = jnp.where(at_origin, 0, ni)
                nj = jnp.where(at_origin, 0, nj)
                return ((ni, nj, done | at_origin), (i, j, valid))
            init = (jnp.int32(T1 - 1), jnp.int32(T2 - 1), jnp.bool_(False))
            _, (i_idx, j_idx, valid) = lax.scan(step, init, None, length=L)
            return (i_idx, j_idx, valid)

        def _align_one(small, large):
            T_small, d = small.shape
            T_large = large.shape[0]
            D = _pairwise_euclidean(small, large)
            R = _dtw_cost(D)
            i_idx, j_idx, valid = _backtrack(R, T_small, T_large)
            contrib = small[i_idx] * valid[:, None].astype(small.dtype)
            expanded = jnp.zeros((T_large, d), dtype=small.dtype).at[j_idx].add(contrib)
            return expanded
        key = jax.random.key(seed)
        k1, k2 = jax.random.split(key)
        teacher = jax.random.normal(k1, (16, 50, 128), dtype=jnp.float32)
        student = jax.random.normal(k2, (16, 75, 128), dtype=jnp.float32)
        return {'teacher_features': teacher, 'student_features': student}
    _L1_xattn_all = _L1_xattn_setup()
    _L1_xattn_in = {k: v for k, v in _L1_xattn_all.items() if k in ()}
    del _L1_xattn_all

    def _L1_ffn_setup():
        import jax, jax.numpy as jnp
        import numpy as np
        TOP_K = 2
        LN_EPS = 1e-05
        B, S, H, E, F = (2, 256, 128, 8, 512)

        def _layernorm(x, w, b):
            mu = jnp.mean(x, axis=-1, keepdims=True)
            var = jnp.mean(jnp.square(x - mu), axis=-1, keepdims=True)
            return (x - mu) * jax.lax.rsqrt(var + LN_EPS) * w + b
        key = jax.random.key(seed)
        ks = jax.random.split(key, 6)
        x = jax.random.normal(ks[0], (B, S, H), dtype=jnp.float32)
        Wg = jax.random.normal(ks[1], (H, E), dtype=jnp.float32) * 0.02
        alpha = jax.random.normal(ks[2], (E,), dtype=jnp.float32)
        ln_w = jnp.ones((E, H), dtype=jnp.float32)
        ln_b = jnp.zeros((E, H), dtype=jnp.float32)
        fc1_w = jax.random.normal(ks[3], (E, H, F), dtype=jnp.float32) * 0.02
        fc1_b = jnp.zeros((E, F), dtype=jnp.float32)
        fc2_w = jax.random.normal(ks[4], (E, F, H), dtype=jnp.float32) * 0.02
        fc2_b = jnp.zeros((E, H), dtype=jnp.float32)
        return {'x': x, 'Wg': Wg, 'alpha': alpha, 'ln_w': ln_w, 'ln_b': ln_b, 'fc1_w': fc1_w, 'fc1_b': fc1_b, 'fc2_w': fc2_w, 'fc2_b': fc2_b}
    _L1_ffn_all = _L1_ffn_setup()
    _L1_ffn_in = {k: v for k, v in _L1_ffn_all.items() if k in ('Wg', 'alpha', 'ln_w', 'ln_b', 'fc1_w', 'fc1_b', 'fc2_w', 'fc2_b')}
    del _L1_ffn_all
    return {'x': x, 'ctx_1024': ctx_1024, 'g_xattn': g_xattn, 'g_ffn': g_ffn, 'L0_xattn_ln_l_w': _L0_xattn_in['ln_l_w'], 'L0_xattn_ln_l_b': _L0_xattn_in['ln_l_b'], 'L0_xattn_ln_c_w': _L0_xattn_in['ln_c_w'], 'L0_xattn_ln_c_b': _L0_xattn_in['ln_c_b'], 'L0_xattn_Wq': _L0_xattn_in['Wq'], 'L0_xattn_Wkv': _L0_xattn_in['Wkv'], 'L0_xattn_Wo': _L0_xattn_in['Wo'], 'L0_xattn_bo': _L0_xattn_in['bo'], 'L0_ffn_gate_w': _L0_ffn_in['gate_w'], 'L0_ffn_gate_b': _L0_ffn_in['gate_b'], 'L0_ffn_We1': _L0_ffn_in['We1'], 'L0_ffn_be1': _L0_ffn_in['be1'], 'L0_ffn_We2': _L0_ffn_in['We2'], 'L0_ffn_be2': _L0_ffn_in['be2'], 'L0_ffn_We3': _L0_ffn_in['We3'], 'L0_ffn_be3': _L0_ffn_in['be3'], 'L0_ffn_ws1': _L0_ffn_in['ws1'], 'L0_ffn_bs1': _L0_ffn_in['bs1'], 'L0_ffn_ws2': _L0_ffn_in['ws2'], 'L0_ffn_bs2': _L0_ffn_in['bs2'], 'L0_ffn_ws3': _L0_ffn_in['ws3'], 'L0_ffn_bs3': _L0_ffn_in['bs3'], 'L1_ffn_Wg': _L1_ffn_in['Wg'], 'L1_ffn_alpha': _L1_ffn_in['alpha'], 'L1_ffn_ln_w': _L1_ffn_in['ln_w'], 'L1_ffn_ln_b': _L1_ffn_in['ln_b'], 'L1_ffn_fc1_w': _L1_ffn_in['fc1_w'], 'L1_ffn_fc1_b': _L1_ffn_in['fc1_b'], 'L1_ffn_fc2_w': _L1_ffn_in['fc2_w'], 'L1_ffn_fc2_b': _L1_ffn_in['fc2_b']}

def reference(x, ctx_1024, g_xattn, g_ffn, L0_xattn_ln_l_w, L0_xattn_ln_l_b, L0_xattn_ln_c_w, L0_xattn_ln_c_b, L0_xattn_Wq, L0_xattn_Wkv, L0_xattn_Wo, L0_xattn_bo, L0_ffn_gate_w, L0_ffn_gate_b, L0_ffn_We1, L0_ffn_be1, L0_ffn_We2, L0_ffn_be2, L0_ffn_We3, L0_ffn_be3, L0_ffn_ws1, L0_ffn_bs1, L0_ffn_ws2, L0_ffn_bs2, L0_ffn_ws3, L0_ffn_bs3, L1_ffn_Wg, L1_ffn_alpha, L1_ffn_ln_w, L1_ffn_ln_b, L1_ffn_fc1_w, L1_ffn_fc1_b, L1_ffn_fc2_w, L1_ffn_fc2_b):
    import jax
    import jax.numpy as jnp

    def _L0_xattn_ref(latents, context, ln_l_w, ln_l_b, ln_c_w, ln_c_b, Wq, Wkv, Wo, bo):
        import jax, jax.numpy as jnp
        import numpy as np
        DIM = 128
        H = 16
        D = 64
        INNER = H * D
        EPS = 1e-05

        def layernorm(x, w, b):
            mu = jnp.mean(x, axis=-1, keepdims=True)
            var = jnp.var(x, axis=-1, keepdims=True)
            return (x - mu) * jax.lax.rsqrt(var + EPS) * w + b
        b, n, _ = latents.shape
        s = context.shape[1]
        lat = layernorm(latents, ln_l_w, ln_l_b)
        ctx = layernorm(context, ln_c_w, ln_c_b)
        q = (lat @ Wq).reshape(b, n, H, D).transpose(0, 2, 1, 3)
        kv = ctx @ Wkv
        k, v = jnp.split(kv, 2, axis=-1)
        k = k.reshape(b, s, H, D).transpose(0, 2, 1, 3)
        v = v.reshape(b, s, H, D).transpose(0, 2, 1, 3)
        scale = D ** (-0.5)
        attn = jnp.einsum('bhnd,bhsd->bhns', q, k) * scale
        attn = jnp.clip(attn, -11.0, 11.0)
        attn = jax.nn.softmax(attn, axis=-1)
        out = jnp.einsum('bhns,bhsd->bhnd', attn, v)
        out = out.transpose(0, 2, 1, 3).reshape(b, n, INNER)
        return out @ Wo + bo

    def _L0_ffn_ref(x, gate_w, gate_b, We1, be1, We2, be2, We3, be3, ws1, bs1, ws2, bs2, ws3, bs3):
        import jax, jax.numpy as jnp
        import numpy as np
        DIM = 128
        E = 16
        TOPK = 2
        G = 4
        TOPK_G = 2
        INTER = 64
        N_SHARED = 2
        ROUTE_SCALE = 1.0

        def _gate(xf, gate_w, gate_b):
            scores = xf @ gate_w.T
            scores = jax.nn.softmax(scores.astype(jnp.float32), axis=-1)
            orig = scores
            scores = scores + gate_b
            T = xf.shape[0]
            sg = scores.reshape(T, G, E // G)
            group_scores = jax.lax.top_k(sg, 2)[0].sum(-1)
            _, gidx = jax.lax.top_k(group_scores, TOPK_G)
            keep = jax.nn.one_hot(gidx, G).sum(axis=1) > 0
            sg = jnp.where(keep[:, :, None], sg, -jnp.inf)
            scores = sg.reshape(T, E)
            _, idx = jax.lax.top_k(scores, TOPK)
            weights = jnp.take_along_axis(orig, idx, axis=1)
            weights = (weights * ROUTE_SCALE).astype(xf.dtype)
            return (weights, idx)
        shape = x.shape
        xf = x.reshape(-1, DIM)
        weights, idx = _gate(xf, gate_w, gate_b)
        combine = (jax.nn.one_hot(idx, E, dtype=xf.dtype) * weights[..., None]).sum(1)
        h1 = jnp.einsum('td,edi->tei', xf, We1) + be1
        h3 = jnp.einsum('td,edi->tei', xf, We3) + be3
        h = jax.nn.silu(h1) * h3
        yo = jnp.einsum('tei,eid->ted', h, We2) + be2
        y = jnp.einsum('te,ted->td', combine, yo)
        z = jax.nn.silu(xf @ ws1 + bs1) * (xf @ ws3 + bs3) @ ws2 + bs2
        return (y + z).reshape(shape)

    def _L1_xattn_ref(teacher_features, student_features):
        import jax, jax.numpy as jnp
        import numpy as np
        from jax import lax
        BIG = jnp.float32(1e+30)

        def _pairwise_euclidean(a, b):
            aa = jnp.sum(a * a, axis=-1)[:, None]
            bb = jnp.sum(b * b, axis=-1)[None, :]
            ab = a @ b.T
            return jnp.sqrt(jnp.maximum(aa + bb - 2.0 * ab, 0.0))

        def _dtw_cost(D):
            row0 = jnp.cumsum(D[0])

            def row_step(prev_row, d_row):
                first = d_row[0] + prev_row[0]

                def col_step(left, inp):
                    d_ij, up, diag = inp
                    r = d_ij + jnp.minimum(jnp.minimum(up, left), diag)
                    return (r, r)
                _, rest = lax.scan(col_step, first, (d_row[1:], prev_row[1:], prev_row[:-1]))
                row = jnp.concatenate([first[None], rest])
                return (row, row)
            _, rows = lax.scan(row_step, row0, D[1:])
            return jnp.concatenate([row0[None], rows], axis=0)

        def _backtrack(R, T1, T2):
            L = T1 + T2 - 1

            def step(carry, _):
                i, j, done = carry
                valid = jnp.logical_not(done)
                cd = jnp.where((i > 0) & (j > 0), R[jnp.maximum(i - 1, 0), jnp.maximum(j - 1, 0)], BIG)
                cu = jnp.where(i > 0, R[jnp.maximum(i - 1, 0), j], BIG)
                cl = jnp.where(j > 0, R[i, jnp.maximum(j - 1, 0)], BIG)
                choice = jnp.argmin(jnp.stack([cd, cu, cl]))
                ni = jnp.where(choice <= 1, i - 1, i)
                nj = jnp.where((choice == 0) | (choice == 2), j - 1, j)
                at_origin = (i == 0) & (j == 0)
                ni = jnp.where(at_origin, 0, ni)
                nj = jnp.where(at_origin, 0, nj)
                return ((ni, nj, done | at_origin), (i, j, valid))
            init = (jnp.int32(T1 - 1), jnp.int32(T2 - 1), jnp.bool_(False))
            _, (i_idx, j_idx, valid) = lax.scan(step, init, None, length=L)
            return (i_idx, j_idx, valid)

        def _align_one(small, large):
            T_small, d = small.shape
            T_large = large.shape[0]
            D = _pairwise_euclidean(small, large)
            R = _dtw_cost(D)
            i_idx, j_idx, valid = _backtrack(R, T_small, T_large)
            contrib = small[i_idx] * valid[:, None].astype(small.dtype)
            expanded = jnp.zeros((T_large, d), dtype=small.dtype).at[j_idx].add(contrib)
            return expanded
        return jax.vmap(_align_one)(teacher_features, student_features)

    def _L1_ffn_ref(x, Wg, alpha, ln_w, ln_b, fc1_w, fc1_b, fc2_w, fc2_b):
        import jax, jax.numpy as jnp
        import numpy as np
        TOP_K = 2
        LN_EPS = 1e-05
        B, S, H, E, F = (2, 256, 128, 8, 512)

        def _layernorm(x, w, b):
            mu = jnp.mean(x, axis=-1, keepdims=True)
            var = jnp.mean(jnp.square(x - mu), axis=-1, keepdims=True)
            return (x - mu) * jax.lax.rsqrt(var + LN_EPS) * w + b
        b, s, h = x.shape
        xf = x.reshape(-1, h)
        logits = xf @ Wg
        top_vals, top_idx = jax.lax.top_k(logits, TOP_K)
        gate_score = jax.nn.softmax(top_vals, axis=-1)
        one_hot = jax.nn.one_hot(top_idx, Wg.shape[1], dtype=xf.dtype)
        comb = jnp.einsum('tke,tk->te', one_hot, gate_score) * alpha
        out = jnp.zeros_like(xf)
        for e in range(Wg.shape[1]):
            hdn = _layernorm(xf, ln_w[e], ln_b[e])
            a = jax.nn.gelu(hdn @ fc1_w[e] + fc1_b[e], approximate=True)
            y = a @ fc2_w[e] + fc2_b[e]
            out = out + y * comb[:, e:e + 1]
        return out.reshape(b, s, h)
    x = x + jnp.tanh(g_xattn[0]) * _L0_xattn_ref(_layernorm(x, axis=-1), ctx_1024, L0_xattn_ln_l_w, L0_xattn_ln_l_b, L0_xattn_ln_c_w, L0_xattn_ln_c_b, L0_xattn_Wq, L0_xattn_Wkv, L0_xattn_Wo, L0_xattn_bo)
    x = x + jnp.tanh(g_ffn[0]) * _L0_ffn_ref(_layernorm(x, axis=-1), L0_ffn_gate_w, L0_ffn_gate_b, L0_ffn_We1, L0_ffn_be1, L0_ffn_We2, L0_ffn_be2, L0_ffn_We3, L0_ffn_be3, L0_ffn_ws1, L0_ffn_bs1, L0_ffn_ws2, L0_ffn_bs2, L0_ffn_ws3, L0_ffn_bs3)
    x = x + jnp.tanh(g_xattn[1]) * _L1_xattn_ref(ctx_1024, _layernorm(x, axis=-1))
    x = x + jnp.tanh(g_ffn[1]) * _L1_ffn_ref(_layernorm(x, axis=-1), L1_ffn_Wg, L1_ffn_alpha, L1_ffn_ln_w, L1_ffn_ln_b, L1_ffn_fc1_w, L1_ffn_fc1_b, L1_ffn_fc2_w, L1_ffn_fc2_b)
    return x

_drawn_inputs = setup_inputs


def setup_inputs(seed=0):
    import zlib

    import numpy as np

    out = dict(_drawn_inputs(seed))
    spreads = {'g_ffn': (-1.0, 0.6),
     'L0_xattn_ln_l_w': (1.0, 0.2),
     'L0_xattn_ln_l_b': (0.0, 0.464),
     'L0_xattn_ln_c_w': (1.0, 0.2),
     'L0_xattn_ln_c_b': (0.0, 0.1),
     'L0_xattn_bo': (0.0, 0.1),
     'L0_ffn_gate_b': (0.0, 0.1),
     'L0_ffn_be1': (0.0, 0.563),
     'L0_ffn_be2': (0.0, 0.521),
     'L0_ffn_be3': (0.0, 0.773),
     'L0_ffn_bs1': (0.0, 0.1),
     'L0_ffn_bs2': (0.0, 0.1),
     'L0_ffn_bs3': (0.0, 0.1),
     'L1_ffn_ln_w': (1.0, 0.6),
     'L1_ffn_ln_b': (0.0, 2.0),
     'L1_ffn_fc1_b': (0.0, 0.8),
     'L1_ffn_fc2_b': (0.0, 0.1)}
    factors = {}
    for name, (base, spread) in spreads.items():
        noise = np.random.default_rng([zlib.crc32(name.encode()), seed]).standard_normal(out[name].shape)
        drawn = base * np.exp(spread * noise) if base else spread * noise
        out[name] = jnp.asarray(drawn.astype(out[name].dtype))
    for name, factor in factors.items():
        out[name] = (out[name] * factor).astype(out[name].dtype)
    return out
```

```python
from contextlib import ExitStack

import concourse.bass as bass
from concourse import mybir

ALU = mybir.AluOpType
ACT = mybir.ActivationFunctionType
AX = mybir.AxisListType
F32 = mybir.dt.float32
BF16 = mybir.dt.bfloat16
U32 = mybir.dt.uint32

P = 128
B, N, D = 4, 512, 128
S = 77
W = 16
C = N // W
H, DH = 16, 64
HS = H * S
E0, F0 = 16, 64
E1, F1 = 8, 512
EPS = 1e-5
BIG = 1e30
KC = [128] * (HS // 128) + [HS % 128]
SCORE_HEADS = [6, 5, 5]
STEPS = S + C - 1
ROWW = W + 1
PADROWS = S + 2 * (C - 1)
E_HI, E_LO = 59874.14171519782, 1.670170079024566e-05
CHOICE = [(0, 27), (27, 54), (54, 81), (81, STEPS)]
R_COMB0, R_L0, R_EXP1, R_L1 = 22, 27, 6, 17
NROWS = 80

I_COLS, I_CT, I_CLT, I_WQ, I_K, I_V, I_A, I_BT, I_B = 0, 1, 2, 3, 5, 13, 21, 37, 53
N_PREP = I_B + 3 * B
BY_ACT = [n < I_A or n % 2 == 0 for n in range(N_PREP)]


def emptied(n):
    acts = sum(BY_ACT[:n + 1])
    return acts, n + 1 - acts


COL = {"ln_l_w": 0, "ln_l_b": 1, "ln_c_w": 2, "ln_c_b": 3, "bo": 4, "bs1": 5, "bs2": 6, "bs3": 7,
       "be1": 8, "be3": 16, "ln_w": 24, "ln_b": 32, "fc2_b": 40, "fc1_b": 48}


def build(nc, a, out, stage=9):
    ctx = ExitStack()
    with ctx:
        def sb(name, shape, dt=F32):
            return ctx.enter_context(nc.sbuf_tensor(name, shape, dt))

        def sem(name):
            return ctx.enter_context(nc.semaphore(name))

        X = sb("X", [P, W, D])
        Y = sb("Y", [P, W, D])
        Y2 = sb("Y2", [P, W, D])
        T1 = sb("T1", [P, W, P])
        T2 = sb("T2", [P, W, P])
        stats = sb("stats", [P, W, 6])
        lnw = sb("lnw", [P, 8, W])
        ident = sb("ident", [P, P])
        identb = sb("identb", [P, P], BF16)
        ones = sb("ones", [P, C])
        halfneg = sb("halfneg", [P, W])
        rows = sb("rows", [NROWS, P])
        gate_rows = sb("gate_rows", [E0, P])
        cols = sb("cols", [P, NROWS + E0])
        gains = sb("gains", [P, 4])
        tg = sb("tg", [P, 4])
        bs2g = sb("bs2g", [P, 1])
        gate_b = sb("gate_b", [P, E0])
        alpha = sb("alpha", [P, E1])
        wg1 = sb("wg1", [P, E1])
        cn = sb("cn", [S, B, D])
        cln = Y2[0:S, 0:B, :]
        cT = sb("cT", [P, B, S])
        clT = Y2[:, 4:7, :].rearrange("p w d -> p (w d)")[:, 0:B * S]
        csq = sb("csq", [P, B, S])
        R1 = sb("R1", [P, 4096])
        wkv = R1[:, 0:2048]
        wq = R1[:, 2048:3072]
        wqT = R1[:, 3072:4096]
        R2 = sb("R2", [P, 2 * 8 * B * S])
        kT = R2[:, 0:8 * B * S].rearrange("p (q s) -> p q s", q=8)
        vT = R2[:, 8 * B * S:16 * B * S].rearrange("p (q s) -> p q s", q=8)
        fc1 = R2[:, 0:E1 * F1].rearrange("p (e f) -> p e f", e=E1)
        fc2 = R1[:, 0:4096].rearrange("p (e f d) -> p e f d", e=E1, f=4)
        wo = sb("wo", [P, 8, D])
        A = sb("A", [P, B, HS])
        R3 = sb("R3", [P, B * HS])
        BT = R3[:, :].rearrange("p (b n) -> p b n", b=B)
        Et = BT
        Bc = sb("Bc", [P, B, len(KC), D])
        Bs = sb("Bs", [P, len(KC), D])
        R4 = sb("R4", [P, len(KC) * N])
        PT = R4[:, :].rearrange("p (k n) -> p k n", k=len(KC))
        latb = sb("latb", [P, B, P])
        sums = sb("sums", [P, 2, H])
        we1 = sb("we1", [P, E0, F0])
        we3 = sb("we3", [P, E0, F0])
        we2 = sb("we2", [P, E0 // 2, D])
        be2 = sb("be2", [E0, D])
        ws1 = sb("ws1", [P, D])
        ws2 = sb("ws2", [P, D])
        ws3 = sb("ws3", [P, D])
        R4o = [0]

        def r4(shape_free, dt=F32, parts=P):
            n = 1
            for q in shape_free:
                n *= q
            words = n if dt == F32 or dt == U32 else (n + 1) // 2
            v = R4[0:parts, R4o[0]:R4o[0] + words]
            R4o[0] += words
            if dt != F32:
                v = v.bitcast(dt)
            names = " ".join(f"a{k}" for k in range(len(shape_free)))
            if len(shape_free) > 1:
                v = v.rearrange(f"p ({names}) -> p {names}", **{f"a{k}": q for k, q in enumerate(shape_free)})
            return v

        pr = r4([W, E0])
        scr = r4([W, E0])
        t4 = r4([9, W * 4])
        beat = r4([W, 4, 4])
        beat2 = r4([W, 4, 4])
        top = r4([W, 8])
        topi = r4([W, 8], U32)
        topf = r4([W, 8])
        oh1 = r4([W, E0])
        oh2 = r4([W, E0])
        comb = r4([W, E0])
        rest = r4([W, E0])
        combs = r4([W, 3 * E0], BF16)
        small = r4([6, W])
        low = sb("low", [P, 4, 4])
        iota_e = sb("iota_e", [P, E0])
        combT = sb("combT", [E0, N * B])
        combST = sb("combST", [3 * E0, N * B], BF16)
        sel0 = sb("sel0", [3 * E0, E0 // 2, P], BF16)
        sel1 = sb("sel1", [3 * E1, E1, P], BF16)
        Av = A[:, :, :].rearrange("p b n -> p (b n)")
        silu = Av[:, 0:3 * N].rearrange("p (s n) -> p s n", s=3)
        glu = Av[:, 3 * N:6 * N].rearrange("p (s n) -> p s n", s=3)
        gelu = Av[:, 0:4 * N].rearrange("p (s n) -> p s n", s=4)
        cbs = Av[:, 4 * N:6 * N].rearrange("p (s n) -> p s n", s=2)
        yt = Av[:, 6 * N:8 * N].rearrange("p (s n) -> p s n", s=2)
        b1c = sb("b1c", [P, E1 * 4])
        R3o = [0]

        def r3(*shape_free, parts=P):
            n = 1
            for q in shape_free:
                n *= q
            v = R3[0:parts, R3o[0]:R3o[0] + n]
            R3o[0] += n
            if len(shape_free) > 1:
                names = " ".join(f"a{k}" for k in range(len(shape_free)))
                v = v.rearrange(f"p ({names}) -> p {names}", **{f"a{k}": q for k, q in enumerate(shape_free)})
            return v

        Dt = r3(S, ROWW)
        bb = r3(W)
        aab = r3(S)
        base = r3(W, S)
        Bcv = Bc[:, :, :, :].rearrange("p b k d -> p (b k d)")
        Dsk = Bcv[:, 0:STEPS * ROWW].rearrange("p (t w) -> p t w", w=ROWW)
        Rh = Bcv[:, 1900:1900 + (STEPS + 1) * (W + 2)].rearrange("p (t w) -> p t w", w=W + 2)
        mh = r3(STEPS, ROWW)
        du = R4[:, 0:STEPS * W].rearrange("p (t w) -> p t w", w=W)
        V = R4[:, STEPS * W:2 * STEPS * W].rearrange("p (t w) -> p t w", w=W)
        Vn_flat = base.rearrange("p w i -> p (w i)")
        Vn = Vn_flat.rearrange("p (i w) -> p i w", w=W)
        first = sb("first", [P, 1])
        block_last = sb("block_last", [P, 1])
        jj1 = sb("jj1", [P, W])
        jj2 = sb("jj2", [P, W])
        jrow = sb("jrow", [S, N])
        vals = sb("vals", [P, S + 1])
        pick = sb("pick", [P, W])
        pickm = sb("pickm", [P, 1])
        vcol = sb("vcol", [S, 2, P])
        Mb = Bcv[0:S, 0:4 * N].rearrange("p (b n) -> p b n", b=B)
        mge = R4[0:S, 0:4 * N].rearrange("p (b n) -> p b n", b=B)
        bigrow = Bcv[:, 4096:4096 + (C - 1) * ROWW]

        PS = ctx.enter_context(nc.psum_tensor("PS", [P, 8, 512], F32))

        def bank(k, n=512, parts=P, lo=0):
            return PS[0:parts, k, lo:lo + n]

        Dscr = nc.dram_tensor("Dscr", [P, PADROWS * ROWW], F32, kind="Internal").ap()
        Vscr = nc.dram_tensor("Vscr", [P, STEPS * W], F32, kind="Internal").ap()
        Dskew = bass.AP(Dscr.tensor, (C - 1) * ROWW,
                        [[C * PADROWS * ROWW, B], [(PADROWS - 1) * ROWW, C], [1, STEPS * ROWW]])
        Vskew = bass.AP(Vscr.tensor, 0, [[C * STEPS * W, B], [(STEPS + 1) * W, C], [1, S * W]])

        in_x, in_ctx, in_rows, in_wkv, in_wq, in_wo, in_small, in_e0, in_fc1, in_fc2 = map(sem, [
            "in_x", "in_ctx", "in_rows", "in_wkv", "in_wq", "in_wo", "in_small", "in_e0", "in_fc1", "in_fc2"])
        const0, consts, sel_ready, dve_consts = map(sem, ["const0", "consts", "sel_ready", "dve_consts"])
        ln_stats, ln_math, ln_var, ln_rstd, ln_out = map(sem, ["ln_stats", "ln_math", "ln_var", "ln_rstd", "ln_out"])
        t_done, t_evac = map(sem, ["t_done", "t_evac"])
        prep_done, prep_act, prep_dve, misc_act, misc_dve = map(sem, [
            "prep_done", "prep_act", "prep_dve", "misc_act", "misc_dve"])
        lat_slot, b_slot, score_done, exp_done, softmax_step, pt_done, pt_free, pv_done, pv_free = map(sem, [
            "lat_slot", "b_slot", "score_done", "exp_done", "softmax_step", "pt_done", "pt_free", "pv_done", "pv_free"])
        logits_done, route, route_exp, combT_done, comb_evac = map(sem, [
            "logits_done", "route", "route_exp", "combT_done", "comb_evac"])
        b1_done, b1_out, fc1_scaled = map(sem, ["b1_done", "b1_out", "fc1_scaled"])
        up0, silu0, glu0, cb0, scaled0, down0, acc0 = map(sem, ["up0", "silu0", "glu0", "cb0", "scaled0", "down0", "acc0"])
        aab_done, cost_mm, cost_step, cost_sqrt, sq_done = map(sem, [
            "aab_done", "cost_mm", "cost_step", "cost_sqrt", "sq_done"])
        choice_pool, al_evac, vcol_out = map(sem, ["choice_pool", "al_evac", "vcol_out"])
        d_stored, d_loaded, v_stored, v_loaded = map(sem, ["d_stored", "d_loaded", "v_stored", "v_loaded"])
        dtw_init, row_done, pre_done, choice = map(sem, ["dtw_init", "row_done", "pre_done", "choice"])
        back, vcol_done, mask_done, al_done = map(sem, ["back", "vcol_done", "mask_done", "al_done"])
        up1, gelu1, cb1, cbs1, y1, y1_used, acc1 = map(sem, ["up1", "gelu1", "cb1", "cbs1", "y1", "y1_used", "acc1"])
        stored = sem("stored")

        T_LAT, T_X1, T_E0, T_X2, T_DTW, T_X3, T_G1, T_E1, T_OUT = range(9)

        block = ctx.enter_context(nc.Block())

        xv = a["x"].rearrange("b (c w) d -> (b c) w d", w=W)
        ov = out.rearrange("b (c w) d -> (b c) w d", w=W)

        N_ROWS_DMA = len(COL)
        N_SMALL = 6
        N_CONSTS = 2 + 4 * B + 3

        COST_BANKS = [(0, 6), (6, 12), (12, 16)]
        B_GROUPS = [range(0, 4), range(4, 8), range(8, 10)]

        def combs_bank(g, parts):
            return PS[0:parts, 6 + g, :].bitcast(BF16)

        def prep_out(n, copy):
            k = 2 + n % 4
            if n == I_COLS:
                copy(cols[:, 0:NROWS], bank(k, NROWS))
                return copy(cols[:, NROWS:NROWS + E0], bank(k, E0, lo=NROWS))
            if n == I_CT:
                return copy(cT[:, :, :], bank(k, B * S).rearrange("p (b s) -> p b s", b=B))
            if n < I_K:
                return copy(wqT[:, 512 * (n - I_WQ):512 * (n - I_WQ) + 512], bank(k))
            if n < I_V:
                return copy(kT[:, n - I_K, :], bank(k, B * S))
            if n < I_A:
                return copy(vT[:, n - I_V, :], bank(k, B * S))
            if n < I_B:
                dst, h = (A, n - I_A) if n < I_BT else (BT, n - I_BT)
                return copy(dst[:, :, S * h:S * h + S], bank(k, B * S).rearrange("p (b s) -> p b s", b=B))
            b, g = (n - I_B) // 3, (n - I_B) % 3
            src = PS[:, k, :].rearrange("p (k d) -> p k d", k=4)
            if g < 2:
                return copy(Bc[:, b, 4 * g:4 * g + 4, :], src)
            copy(Bc[:, b, 8, :], src[:, 0, :])
            return copy(Bc[0:KC[9], b, 9, :], src[0:KC[9], 1, :])

        @block.sync
        def _(sp):
            sp.dma_start(cn[:, :, :], a["ctx_1024"].rearrange("b s d -> s b d")).then_inc(in_ctx, 16)
            for name, src, n in (("ln_l_w", "L0_xattn_ln_l_w", 0), ("ln_l_b", "L0_xattn_ln_l_b", 0),
                                 ("ln_c_w", "L0_xattn_ln_c_w", 0), ("ln_c_b", "L0_xattn_ln_c_b", 0),
                                 ("bo", "L0_xattn_bo", 0), ("bs1", "L0_ffn_bs1", 0), ("bs2", "L0_ffn_bs2", 0),
                                 ("bs3", "L0_ffn_bs3", 0), ("be1", "L0_ffn_be1", 8), ("be3", "L0_ffn_be3", 8),
                                 ("ln_w", "L1_ffn_ln_w", 8), ("ln_b", "L1_ffn_ln_b", 8),
                                 ("fc2_b", "L1_ffn_fc2_b", 8), ("fc1_b", "L1_ffn_fc1_b", 32)):
                v = a[src]
                if n == 0:
                    v = v.rearrange("(o d) -> o d", o=1)
                elif name in ("be1", "be3"):
                    v = v.rearrange("(q e) i -> q (e i)", e=2)
                elif name == "fc1_b":
                    v = v.rearrange("e (f i) -> (e f) i", i=P)
                sp.dma_start(rows[COL[name]:COL[name] + max(n, 1), :], v).then_inc(in_rows, 16)
            sp.dma_start(gate_rows[:, :], a["L0_ffn_gate_w"]).then_inc(in_small, 16)
            sp.dma_start(wq, a["L0_xattn_Wq"]).then_inc(in_wq, 16)
            sp.dma_start(we1[:, :, :], a["L0_ffn_We1"].rearrange("e d i -> d e i")).then_inc(in_e0, 16)
            sp.dma_start(we3[:, :, :], a["L0_ffn_We3"].rearrange("e d i -> d e i")).then_inc(in_e0, 16)
            sp.dma_start(we2[:, :, :], a["L0_ffn_We2"].rearrange("(q e) i d -> (e i) q d", e=2)).then_inc(in_e0, 16)
            sp.dma_start(be2[:, :], a["L0_ffn_be2"]).then_inc(in_e0, 16)
            sp.dma_start(ws1[:, :], a["L0_ffn_ws1"]).then_inc(in_e0, 16)
            sp.dma_start(ws2[:, :], a["L0_ffn_ws2"]).then_inc(in_e0, 16)
            sp.dma_start(ws3[:, :], a["L0_ffn_ws3"]).then_inc(in_e0, 16)
            sp.wait_ge(prep_done, N_PREP)
            sp.dma_start(fc1, a["L1_ffn_fc1_w"].rearrange("e d f -> d e f")).then_inc(in_fc1, 16)
            sp.dma_start(fc2, a["L1_ffn_fc2_w"].rearrange("e (f i) d -> i e f d", i=P)).then_inc(in_fc2, 16)
            sp.wait_ge(dtw_init, 1)
            sp.dma_start(Dscr[:, 0:(C - 1) * ROWW], bigrow).then_inc(d_stored, 16)
            sp.dma_start(Dscr[:, (C - 1 + S) * ROWW:PADROWS * ROWW], bigrow).then_inc(d_stored, 16)
            sp.wait_ge(cost_sqrt, 1)
            sp.dma_start(Dscr[:, (C - 1) * ROWW:(C - 1 + S) * ROWW],
                         Dt.rearrange("p t w -> p (t w)")).then_inc(d_stored, 16)
            sp.wait_ge(d_stored, 48)
            sp.dma_start(Dsk.rearrange("p t w -> p (t w)"), Dskew).then_inc(d_loaded, 16)
            for n, (lo, hi) in enumerate(CHOICE):
                sp.wait_ge(choice, n + 1)
                sp.dma_start(Vscr[:, lo * W:hi * W], V[:, lo:hi, :].rearrange("p t w -> p (t w)")).then_inc(v_stored, 16)
            sp.wait_ge(v_stored, 16 * len(CHOICE))
            sp.dma_start(Vn_flat, Vskew).then_inc(v_loaded, 16)
            for g in range(4):
                sp.wait_ge(t_evac, 4 * T_OUT + g + 1)
                sp.dma_start(ov[:, 4 * g:4 * g + 4, :], X[:, 4 * g:4 * g + 4, :]).then_inc(stored, 16)
            sp.wait_ge(stored, 64)

        @block.gpsimd
        def _(g):
            g.memset(ident[:, :], 0.0).then_inc(const0, 1)
            g.memset(identb[:, :], 0.0).then_inc(const0, 1)
            g.memset(ones[:, :], 1.0).then_inc(const0, 1)
            g.memset(halfneg[:, :], -0.5).then_inc(const0, 1)
            g.memset(first[:, :], BIG).then_inc(const0, 1)
            g.memset(block_last[:, :], 0.0).then_inc(const0, 1)
            g.memset(sel0[:, :, :], 0.0).then_inc(const0, 1)
            g.memset(sel1[:, :, :], 0.0).then_inc(const0, 1)
            g.memset(low[:, :, :], 1.0).then_inc(const0, 1)
            g.memset(Bc[:, :, len(KC) - 1, :], 0.0).then_inc(const0, 1)
            g.wait_ge(const0, 10)
            for m in (ident, identb):
                g.affine_select(out=m[:, :], in_=m[:, :], compare_op=ALU.not_equal, fill=1.0, base=0,
                                pattern=[[-1, P]], channel_multiplier=1).then_inc(consts, 1)

            def ln_power(k, n, parts=P):
                g.wait_ge(ln_var, k + 1)
                g.tensor_tensor(lnw[0:parts, 7, 0:n], lnw[0:parts, 6, 0:n], halfneg[0:parts, 0:n],
                                ALU.pow).then_inc(ln_rstd, 1)

            ln_power(0, B, S)
            ln_power(1, W)
            ln_power(2, W)
            for b in range(B):
                q = slice(C * b, C * b + C)
                if b == 0:
                    g.wait_ge(ln_rstd, 3)
                g.wait_ge(consts, 2 + 4 * b)
                g.affine_select(out=first[q, :], in_=first[q, :], compare_op=ALU.not_equal, fill=0.0, base=0,
                                pattern=[[0, 1]], channel_multiplier=1).then_inc(consts, 1)
                g.wait_ge(consts, 3 + 4 * b)
                g.affine_select(out=block_last[q, :], in_=block_last[q, :], compare_op=ALU.not_equal, fill=BIG,
                                base=-(C - 1), pattern=[[0, 1]], channel_multiplier=1).then_inc(consts, 1)
                g.wait_ge(consts, 4 + 4 * b)
                g.iota(jj1[q, :], pattern=[[2, W]], base=1, channel_multiplier=2 * W,
                       allow_small_or_imprecise_dtypes=True).then_inc(consts, 1)
                g.wait_ge(consts, 5 + 4 * b)
                g.iota(jj2[q, :], pattern=[[2, W]], base=2, channel_multiplier=2 * W,
                       allow_small_or_imprecise_dtypes=True).then_inc(consts, 1)
            g.wait_ge(consts, 2 + 4 * B)
            g.iota(jrow[:, :], pattern=[[2, N]], base=2, channel_multiplier=0,
                   allow_small_or_imprecise_dtypes=True).then_inc(consts, 1)
            g.iota(iota_e[:, :], pattern=[[1, E0]], base=0, channel_multiplier=0,
                   allow_small_or_imprecise_dtypes=True).then_inc(consts, 1)
            g.affine_select(out=low[:, :, :], in_=low[:, :, :], compare_op=ALU.is_gt, fill=0.0, base=0,
                            pattern=[[1, 4], [-1, 4]], channel_multiplier=0).then_inc(consts, 1)
            for part in range(3):
                v = sel0[:, :, :].rearrange("k q (e i) -> k q e i", e=2)
                if part:
                    g.wait_ge(sel_ready, 2 * part)
                g.affine_select(out=v, in_=v, compare_op=ALU.not_equal, fill=1.0, base=-E0 * part,
                                pattern=[[-2, E0 // 2], [-1, 2], [0, F0]], channel_multiplier=1).then_inc(sel_ready, 1)
                g.affine_select(out=sel1[:, :, :], in_=sel1[:, :, :], compare_op=ALU.not_equal, fill=1.0,
                                base=-E1 * part, pattern=[[-1, E1], [0, P]], channel_multiplier=1).then_inc(sel_ready, 1)

            def lat_copy(n, b, j):
                g.tensor_copy(latb[:, j, :].rearrange("p (w c) -> p w c", c=C),
                              T1[:, 4 * j:4 * j + 4, bass.ds(b * C, C)]).then_inc(lat_slot, 1)

            for j in range(4):
                g.wait_ge(t_evac, 4 * T_LAT + j + 1)
                lat_copy(j, 0, j)
            g.wait_ge(prep_act, emptied(N_PREP - 1)[0])
            g.wait_ge(prep_dve, emptied(N_PREP - 1)[1])
            g.tensor_copy(Bs[:, :, :], Bc[:, 0, :, :]).then_inc(b_slot, 1)
            with g.Fori(0, B - 1) as b:
                for j in range(4):
                    g.wait_ge(score_done, b * 12 + 3 * j + 3)
                    lat_copy(j, b + 1, j)
                g.wait_ge(pv_done, b + 2)
                g.tensor_copy(Bs[:, :, :], Bc[:, bass.ds(b + 1, 1), :, :].rearrange("p a k d -> p (a k) d")
                              ).then_inc(b_slot, 1)
            ln_power(3, W)
            g.wait_ge(b1_done, 1)
            for e in range(E1):
                g.tensor_scalar(fc1[:, e, :], fc1[:, e, :], cols[:, COL["ln_w"] + e:COL["ln_w"] + e + 1], 1.0,
                                ALU.mult, ALU.mult).then_inc(fc1_scaled, 1)
            ln_power(4, W)

            for n, (lo, hi) in enumerate(CHOICE):
                g.wait_ge(row_done, hi)
                r = slice(lo, hi)
                g.tensor_tensor(du[:, r, :], Rh[:, r, 1:1 + W], Rh[:, r, 0:W], ALU.subtract).then_inc(choice_pool, 1)
                g.tensor_tensor(V[:, r, :], Rh[:, lo + 1:hi + 1, 0:W], mh[:, r, 0:W], ALU.subtract).then_inc(choice_pool, 1)
                g.wait_ge(choice_pool, 5 * n + 2)
                g.tensor_scalar(du[:, r, :], du[:, r, :], 0.0, None, ALU.is_lt).then_inc(choice_pool, 1)
                g.tensor_scalar(V[:, r, :], V[:, r, :], 0.0, None, ALU.is_ge).then_inc(choice_pool, 1)
                g.wait_ge(choice_pool, 5 * n + 4)
                g.tensor_tensor(du[:, r, :], du[:, r, :], jj1[:, :].unsqueeze(1).to_broadcast([P, hi - lo, W]),
                                ALU.add).then_inc(choice_pool, 1)
                g.wait_ge(choice_pool, 5 * n + 5)
                g.tensor_tensor(V[:, r, :], V[:, r, :], du[:, r, :], ALU.mult).then_inc(choice, 1)
            ln_power(5, W)
            ln_power(6, W)

        @block.vector
        def _(v):
            v.memset(vals[:, S:S + 1], 2.0 * N).then_inc(dve_consts, 1)
            v.sem_inc(pv_free, 1)
            v.sem_inc(glu0, 3)
            v.sem_inc(cbs1, 2)
            v.sem_inc(y1_used, 2)

            def col(name, k=0):
                return cols[:, COL[name] + k:COL[name] + k + 1]

            def layer_norm(k, src, dst, n, ready, parts=P):
                for w in range(n):
                    ready(w)
                    ins = v.bn_stats(stats[0:parts, w, :], src[:, w, :])
                ins.then_inc(ln_stats, 1)
                v.wait_ge(ln_stats, k + 1)
                q = lnw[0:parts, :, 0:n]
                st = stats[0:parts, 0:n, :]
                v.tensor_tensor(q[:, 0, :], st[:, :, 1], st[:, :, 4], ALU.add)
                v.tensor_tensor(q[:, 1, :], st[:, :, 1], st[:, :, 4], ALU.subtract)
                v.tensor_tensor(q[:, 2, :], st[:, :, 2], st[:, :, 5], ALU.add).then_inc(ln_math, 1)
                v.wait_ge(ln_math, 3 * k + 1)
                v.tensor_scalar(q[:, 3, :], q[:, 0, :], 0.5, None, ALU.mult)
                v.scalar_tensor_tensor(out=q[:, 4, :], in0=q[:, 1, :], scalar=0.25, in1=q[:, 1, :],
                                       op0=ALU.mult, op1=ALU.mult).then_inc(ln_math, 1)
                v.wait_ge(ln_math, 3 * k + 2)
                v.scalar_tensor_tensor(out=q[:, 5, :], in0=q[:, 2, :], scalar=1.0 / D, in1=q[:, 4, :],
                                       op0=ALU.mult, op1=ALU.add).then_inc(ln_math, 1)
                v.wait_ge(ln_math, 3 * k + 3)
                v.tensor_scalar(q[:, 6, :], q[:, 5, :], EPS, None, ALU.add).then_inc(ln_var, 1)
                v.wait_ge(ln_rstd, k + 1)
                for w in range(n):
                    v.tensor_scalar(dst[:, w, :], src[:, w, :], q[:, 3, w:w + 1], lnw[0:parts, 7, w:w + 1],
                                    ALU.subtract, ALU.mult).then_inc(ln_out, 1)

            def ln_ready(k, w):
                return B + W * (k - 1) + w + 1

            def add_back(k):
                for g in range(4):
                    v.wait_ge(t_done, 4 * k + g + 1)
                    x4 = X[:, 4 * g:4 * g + 4, :]
                    v.tensor_tensor(x4, bank(g % 2).rearrange("p (w d) -> p w d", w=4), x4, ALU.add).then_inc(t_evac, 1)

            v.wait_ge(in_ctx, 16)
            layer_norm(0, cn[:, :, :], cln, B, lambda w: None, S)
            v.wait_ge(in_x, 16)
            layer_norm(1, X, Y, W, lambda w: None)
            layer_norm(2, Y, Y, W, lambda w: v.wait_ge(ln_out, ln_ready(1, w)))
            v.wait_ge(prep_act, 1)
            for g in range(4):
                v.wait_ge(t_done, 4 * T_LAT + g + 1)
                v.tensor_scalar(T1[:, 4 * g:4 * g + 4, :], bank(g % 2).rearrange("p (w n) -> p w n", w=4),
                                col("ln_l_w"), col("ln_l_b"), ALU.mult, ALU.add).then_inc(t_evac, 1)
            for n in range(I_A, N_PREP):
                if not BY_ACT[n]:
                    v.wait_ge(prep_done, n + 1)
                    prep_out(n, lambda o, i: v.tensor_copy(o, i)).then_inc(prep_dve, 1)
            v.wait_ge(misc_act, 1)
            v.tensor_tensor(bs2g[:, :], col("bs2"), tg[:, 2:3], ALU.mult).then_inc(misc_dve, 1)

            def softmax(n, j):
                e = Et[:, j, :]
                eh = e.rearrange("p (h s) -> p h s", h=H)
                v.wait_ge(exp_done, 3 * n + 3)
                v.tensor_scalar(e, e, E_HI, E_LO, ALU.min, ALU.max).then_inc(softmax_step, 1)
                v.wait_ge(softmax_step, 4 * n + 1)
                v.tensor_reduce(sums[:, 0, :], eh, AX.X, ALU.add).then_inc(softmax_step, 1)
                v.wait_ge(softmax_step, 4 * n + 2)
                v.reciprocal(sums[:, 1, :], sums[:, 0, :]).then_inc(softmax_step, 1)
                v.wait_ge(softmax_step, 4 * n + 3)
                v.tensor_tensor(eh, eh, sums[:, 1, :].unsqueeze(2).to_broadcast([P, H, S]), ALU.mult
                                ).then_inc(softmax_step, 1)

            def attention(b, last):
                softmax(4 * b + 2, 2)
                softmax(4 * b + 3, 3)
                if not last:
                    softmax(4 * b + 4, 0)
                    softmax(4 * b + 5, 1)
                v.wait_ge(pv_done, b + 2)
                v.tensor_scalar(T2[:, :, bass.ds(b * C, C)], bank(6).rearrange("p (w c) -> p w c", w=W),
                                col("bo"), tg[:, 0:1], ALU.add, ALU.mult).then_inc(pv_free, 1)

            softmax(0, 0)
            softmax(1, 1)
            with v.Fori(0, B - 1) as b:
                attention(b, False)
            attention(B - 1, True)
            v.memset(mh[:, :, W:ROWW], BIG)
            v.memset(Rh[:, 0, :], BIG)
            v.memset(Rh[:, 1, 0:1], BIG)
            v.memset(bigrow, BIG).then_inc(dtw_init, 1)
            add_back(T_X1)

            layer_norm(3, X, Y, W, lambda w: v.wait_ge(t_evac, 4 * T_X1 + w // 4 + 1))
            r = [0]

            def did(ins):
                ins.then_inc(route, 1)
                r[0] += 1

            def so_far():
                v.wait_ge(route, r[0])

            def per_token(x, n):
                return x.unsqueeze(2).to_broadcast([P, W, n])

            def top_two(values, n):
                for w in range(W):
                    ins = v.max(top[:, w, :], values[:, w, :])
                did(ins)
                so_far()
                for w in range(W):
                    ins = v.max_index(topi[:, w, :], top[:, w, :], values[:, w, :])
                did(ins)
                so_far()
                did(v.tensor_copy(topf, topi))
                so_far()
                ie = iota_e[:, 0:n].unsqueeze(1).to_broadcast([P, W, n])
                v.tensor_tensor(oh1[:, :, 0:n], ie, per_token(topf[:, :, 0], n), ALU.is_equal)
                did(v.tensor_tensor(oh2[:, :, 0:n], ie, per_token(topf[:, :, 1], n), ALU.is_equal))
                so_far()

            def split(c, n):
                did(v.tensor_copy(combs[:, :, 0:n], c))
                so_far()
                did(v.tensor_tensor(rest[:, :, 0:n], c, combs[:, :, 0:n], ALU.subtract))
                so_far()
                did(v.tensor_copy(combs[:, :, n:2 * n], rest[:, :, 0:n]))
                so_far()
                did(v.tensor_tensor(scr[:, :, 0:n], rest[:, :, 0:n], combs[:, :, n:2 * n], ALU.subtract))
                so_far()
                did(v.tensor_copy(combs[:, :, 2 * n:3 * n], scr[:, :, 0:n]))

            v.wait_ge(consts, N_CONSTS)
            v.wait_ge(in_small, 16 * N_SMALL)
            v.wait_ge(logits_done, 1)
            lg = bank(7, W * E0).rearrange("p (w e) -> p w e", w=W)
            did(v.tensor_reduce(small[:, 0, :], lg, AX.X, ALU.max))
            so_far()
            did(v.tensor_tensor(scr, lg, per_token(small[:, 0, :], E0), ALU.subtract))
            v.wait_ge(route_exp, 1)
            did(v.tensor_reduce(small[:, 1, :], pr, AX.X, ALU.add))
            so_far()
            did(v.reciprocal(small[:, 2, :], small[:, 1, :]))
            so_far()
            did(v.tensor_tensor(pr, pr, per_token(small[:, 2, :], E0), ALU.mult))
            so_far()
            did(v.tensor_tensor(scr, pr, gate_b[:, :].unsqueeze(1).to_broadcast([P, W, E0]), ALU.add))
            so_far()
            q4 = scr.rearrange("p w (g k) -> p (w g) k", k=4)
            hi1, lo1, hi2, lo2, m1, mlo, mhi, m2, gs = (t4[:, k, :] for k in range(9))
            v.tensor_tensor(hi1, q4[:, :, 0], q4[:, :, 1], ALU.max)
            v.tensor_tensor(lo1, q4[:, :, 0], q4[:, :, 1], ALU.min)
            v.tensor_tensor(hi2, q4[:, :, 2], q4[:, :, 3], ALU.max)
            did(v.tensor_tensor(lo2, q4[:, :, 2], q4[:, :, 3], ALU.min))
            so_far()
            v.tensor_tensor(m1, hi1, hi2, ALU.max)
            v.tensor_tensor(mlo, hi1, hi2, ALU.min)
            did(v.tensor_tensor(mhi, lo1, lo2, ALU.max))
            so_far()
            did(v.tensor_tensor(m2, mlo, mhi, ALU.max))
            so_far()
            did(v.tensor_tensor(gs, m1, m2, ALU.add))
            so_far()
            gw = gs.rearrange("p (w g) -> p w g", g=4)
            mine = gw.unsqueeze(3).to_broadcast([P, W, 4, 4])
            other = gw.unsqueeze(2).to_broadcast([P, W, 4, 4])
            v.tensor_tensor(beat, other, mine, ALU.is_gt)
            did(v.tensor_tensor(beat2, other, mine, ALU.is_equal))
            so_far()
            did(v.tensor_tensor(beat2, beat2, low[:, :, :].unsqueeze(1).to_broadcast([P, W, 4, 4]), ALU.mult))
            so_far()
            did(v.tensor_tensor(beat, beat, beat2, ALU.add))
            so_far()
            did(v.tensor_reduce(hi1, beat.rearrange("p w g o -> p (w g) o"), AX.X, ALU.add))
            so_far()
            did(v.tensor_scalar(lo1, hi1, 2.0, -BIG, ALU.is_ge, ALU.mult))
            so_far()
            did(v.tensor_tensor(q4, q4, lo1.unsqueeze(2).to_broadcast([P, W * 4, 4]), ALU.add))
            so_far()
            top_two(scr, E0)
            did(v.tensor_tensor(oh1, oh1, oh2, ALU.add))
            so_far()
            did(v.tensor_tensor(comb, oh1, pr, ALU.mult))
            so_far()
            split(comb, E0)
            v.wait_ge(b1_done, 1)
            v.tensor_tensor(b1c[:, :], bank(5, 32, lo=128), cols[:, COL["fc1_b"]:COL["fc1_b"] + 32], ALU.add
                            ).then_inc(b1_out, 1)

            def hidden0(b, u):
                n = 9 * b + u
                v.wait_ge(silu0, n + 1)
                v.scalar_tensor_tensor(out=glu[:, u % 3, :], in0=bank(3 + u % 3),
                                       scalar=col("be3", u - 1) if u else col("bs3"), in1=silu[:, u % 3, :],
                                       op0=ALU.add, op1=ALU.mult).then_inc(glu0, 1)
                if u:
                    v.wait_ge(cb0, 8 * b + u)
                    v.wait_ge(glu0, n + 4)
                    v.tensor_tensor(glu[:, u % 3, :], glu[:, u % 3, :], bank(7), ALU.mult).then_inc(scaled0, 1)

            with v.Fori(0, B) as b:
                for u in range(9):
                    hidden0(b, u)
            add_back(T_X2)

            layer_norm(4, X, Y, W, lambda w: v.wait_ge(t_evac, 4 * T_X2 + w // 4 + 1))
            v.wait_ge(aab_done, 1)
            v.tensor_copy(aab, bank(5, S)).then_inc(cost_step, 1)
            v.wait_ge(sq_done, 1)
            v.tensor_reduce(bb, Y2[:, :, :], AX.X, ALU.add).then_inc(cost_step, 1)
            v.wait_ge(cost_step, 2)
            v.tensor_tensor(base, aab.unsqueeze(1).to_broadcast([P, W, S]), bb.unsqueeze(2).to_broadcast([P, W, S]),
                            ALU.add).then_inc(cost_step, 1)
            v.wait_ge(cost_step, 3)
            v.tensor_copy(Dt[:, :, W:ROWW], block_last[:, :].unsqueeze(1).to_broadcast([P, S, 1]))
            for k, (lo, hi) in enumerate(COST_BANKS):
                v.wait_ge(cost_mm, k + 1)
                v.scalar_tensor_tensor(out=Dt[:, :, lo:hi].rearrange("p i w -> p w i"),
                                       in0=bank(2 + k, (hi - lo) * S).rearrange("p (w i) -> p w i", i=S), scalar=-2.0,
                                       in1=base[:, lo:hi, :], op0=ALU.mult, op1=ALU.add).then_inc(cost_step, 1)
            v.wait_ge(cost_step, 6)
            v.tensor_scalar(Dt[:, :, 0:W], Dt[:, :, 0:W], 0.0, None, ALU.max).then_inc(cost_step, 1)

            v.wait_ge(dve_consts, 1)
            v.wait_ge(dtw_init, 1)
            v.wait_ge(d_loaded, 16)
            shift = [C - 1] + list(range(C - 1))
            for t in range(STEPS):
                if t:
                    v.wait_ge(row_done, t)
                    v.stream_shuffle(Rh[:, t + 1, 0:1], Rh[:, t, W + 1:W + 2], shift)
                v.tensor_tensor(mh[:, t, 0:W], Rh[:, t, 1:1 + W], Rh[:, t, 0:W], ALU.min).then_inc(pre_done, 1)
                v.wait_ge(pre_done, t + 1)
                v.tensor_tensor_scan(Rh[:, t + 1, 1:2 + W], mh[:, t, :], Dsk[:, t, :],
                                     Rh[:, t + 1, 0:1] if t else first[:, :], ALU.min, ALU.add).then_inc(row_done, 1)

            v.wait_ge(v_loaded, 16)
            for n, i in enumerate(range(S - 1, -1, -1)):
                v.scalar_tensor_tensor(out=pick[:, :], in0=jj2[:, :], scalar=vals[:, i + 1:i + 2], in1=Vn[:, i, :],
                                       op0=ALU.is_le, op1=ALU.mult).then_inc(back, 1)
                v.wait_ge(back, 3 * n + 1)
                v.tensor_reduce(pickm[:, :], pick[:, :], AX.X, ALU.max).then_inc(back, 1)
                v.wait_ge(back, 3 * n + 2)
                v.tensor_reduce(vals[:, i:i + 1], pickm[:, :].to_broadcast([P, C]), AX.X, ALU.max,
                                apply_transpose=True).then_inc(back, 1)
                v.wait_ge(back, 3 * n + 3)
            v.wait_ge(vcol_done, 1)
            v.tensor_copy(vcol[:, :, :], bank(2, 2 * P, S).rearrange("p (k n) -> p k n", k=2)).then_inc(vcol_out, 1)
            v.wait_ge(vcol_out, 1)
            for b in range(B):
                v.tensor_scalar(mge[:, b, :], jrow[:, :], vcol[:, 0, C * b:C * b + 1], None, ALU.is_ge).then_inc(vcol_out, 1)
                v.wait_ge(vcol_out, 2 + b)
                v.scalar_tensor_tensor(out=Mb[:, b, :], in0=jrow[:, :], scalar=vcol[:, 1, C * b:C * b + 1],
                                       in1=mge[:, b, :], op0=ALU.is_le, op1=ALU.mult).then_inc(mask_done, 1)
            add_back(T_X3)

            layer_norm(5, X, Y, W, lambda w: v.wait_ge(t_evac, 4 * T_X3 + w // 4 + 1))
            layer_norm(6, Y, Y2, W, lambda w: v.wait_ge(ln_out, ln_ready(5, w)))
            v.wait_ge(logits_done, 2)
            lg1 = scr[:, :, 0:E1]
            did(v.tensor_copy(lg1, bank(7, W * E1).rearrange("p (w e) -> p w e", w=W)))
            so_far()
            top_two(lg1, E1)
            did(v.tensor_tensor(small[:, 0, :], top[:, :, 1], top[:, :, 0], ALU.subtract))
            v.wait_ge(route_exp, 2)
            did(v.tensor_scalar(small[:, 2, :], small[:, 1, :], 1.0, None, ALU.add))
            so_far()
            did(v.reciprocal(small[:, 3, :], small[:, 2, :]))
            so_far()
            did(v.tensor_tensor(small[:, 4, :], small[:, 1, :], small[:, 3, :], ALU.mult))
            so_far()
            v.tensor_tensor(oh1[:, :, 0:E1], oh1[:, :, 0:E1], per_token(small[:, 3, :], E1), ALU.mult)
            did(v.tensor_tensor(oh2[:, :, 0:E1], oh2[:, :, 0:E1], per_token(small[:, 4, :], E1), ALU.mult))
            so_far()
            did(v.tensor_tensor(oh1[:, :, 0:E1], oh1[:, :, 0:E1], oh2[:, :, 0:E1], ALU.add))
            so_far()
            did(v.tensor_tensor(comb[:, :, 0:E1], oh1[:, :, 0:E1],
                                alpha[:, :].unsqueeze(1).to_broadcast([P, W, E1]), ALU.mult))
            so_far()
            split(comb[:, :, 0:E1], E1)
            assert r[0] == R_L0 + R_L1, r[0]

            with v.Fori(0, B) as b:
                acc = T1[:, bass.ds(4 * b, 4), :].rearrange("p w n -> p (w n)")
                for e in range(E1):
                    n = E1 * b + e
                    v.wait_ge(cb1, n + 1)
                    v.tensor_copy(cbs[:, e % 2, :], bank(6 + e % 2)).then_inc(cbs1, 1)
                    v.wait_ge(y1, n + 1)
                    v.wait_ge(cbs1, n + 3)
                    v.scalar_tensor_tensor(out=yt[:, e % 2, :] if e else acc, in0=bank(4 + e % 2), scalar=col("fc2_b", e),
                                           in1=cbs[:, e % 2, :], op0=ALU.add, op1=ALU.mult).then_inc(y1_used, 1)
                    if e:
                        v.wait_ge(y1_used, n + 3)
                        if e > 1:
                            v.wait_ge(acc1, 7 * b + e - 1)
                        v.tensor_tensor(acc, acc, yt[:, e % 2, :], ALU.add).then_inc(acc1, 1)
            for g in range(4):
                v.wait_ge(t_done, 4 * T_OUT + g + 1)
                x4 = X[:, 4 * g:4 * g + 4, :]
                v.scalar_tensor_tensor(out=x4, in0=bank(g % 2).rearrange("p (w d) -> p w d", w=4), scalar=tg[:, 3:4],
                                       in1=x4, op0=ALU.mult, op1=ALU.add).then_inc(t_evac, 1)

        @block.scalar
        def _(s):
            s.dma_start(X[:, :, :], xv).then_inc(in_x, 16)
            s.dma_start(wkv, a["L0_xattn_Wkv"]).then_inc(in_wkv, 16)
            s.dma_start(gains[:, 0:2], a["g_xattn"].partition_broadcast(P)).then_inc(in_small, 16)
            s.dma_start(gains[:, 2:4], a["g_ffn"].partition_broadcast(P)).then_inc(in_small, 16)
            s.dma_start(gate_b[:, :], a["L0_ffn_gate_b"].partition_broadcast(P)).then_inc(in_small, 16)
            s.dma_start(alpha[:, :], a["L1_ffn_alpha"].partition_broadcast(P)).then_inc(in_small, 16)
            s.dma_start(wg1[:, :], a["L1_ffn_Wg"]).then_inc(in_small, 16)
            s.dma_start(wo[:, :, :], a["L0_xattn_Wo"].rearrange("(q i) d -> i q d", i=P)).then_inc(in_wo, 16)
            s.sem_inc(pt_free, 2)
            s.sem_inc(acc0, 1)
            s.sem_inc(gelu1, 4)

            def col(name, k=0):
                return cols[:, COL[name] + k:COL[name] + k + 1]

            s.wait_ge(in_small, 16 * N_SMALL)
            s.activation(tg[:, :], gains[:, :], ACT.Tanh).then_inc(misc_act, 1)
            for n in range(N_PREP):
                if BY_ACT[n]:
                    s.wait_ge(prep_done, n + 1)
                    if n == I_CLT:
                        s.wait_ge(prep_act, 1)
                        s.activation(clT, bank(2 + n % 4, B * S), ACT.Identity, bias=col("ln_c_b"),
                                     scale=col("ln_c_w")).then_inc(prep_act, 1)
                    else:
                        prep_out(n, lambda o, i: s.activation(o, i, ACT.Copy)).then_inc(prep_act, 1)
                if n == I_CLT:
                    s.wait_ge(prep_act, 2)
                    s.activation(csq[:, :, :], cT[:, :, :], ACT.Square).then_inc(misc_act, 1)

            def exps(n, jj):
                s.wait_ge(pt_done, 3 * n + 3)
                h0 = 0
                for k, nh in enumerate(SCORE_HEADS):
                    s.wait_ge(score_done, 3 * n + k + 1)
                    s.activation(Et[:, jj % 4, h0 * S:(h0 + nh) * S], bank(2 + (3 * jj + k) % 4, nh * S), ACT.Exp,
                                 scale=DH ** -0.5).then_inc(exp_done, 1)
                    h0 += nh

            def weights_out(n, b, j):
                for g in range(3):
                    s.wait_ge(pt_done, 12 + 3 * n + g + 1)
                    if j == 0 and g == 0:
                        s.wait_ge(pv_done, b + 1)
                    k0 = 4 * g
                    src = PS[:, (3 * j + g) % 2, :].rearrange("p (k n) -> p k n", k=4)
                    if g < 2:
                        s.activation(PT[:, k0:k0 + 4, P * j:P * j + P], src, ACT.Copy).then_inc(pt_free, 1)
                    else:
                        s.activation(PT[:, 8, P * j:P * j + P], src[:, 0, :], ACT.Copy)
                        s.activation(PT[0:KC[9], 9, P * j:P * j + P], src[0:KC[9], 1, :], ACT.Copy).then_inc(pt_free, 1)

            exps(0, 0)
            exps(1, 1)

            def attention(b, last):
                for j in range(4):
                    if not (last and j > 1):
                        exps(4 * b + j + 2, j + 2)
                    weights_out(4 * b + j, b, j)

            with s.Fori(0, B - 1) as b:
                attention(b, False)
            attention(B - 1, True)

            def t_copy(k, dst):
                for g in range(4):
                    s.wait_ge(t_done, 4 * k + g + 1)
                    s.activation(dst[:, 4 * g:4 * g + 4, :], bank(g % 2).rearrange("p (w n) -> p w n", w=4),
                                 ACT.Copy).then_inc(t_evac, 1)

            t_copy(T_E0, T1)
            s.wait_ge(route, 2)
            s.activation(pr, scr, ACT.Exp).then_inc(route_exp, 1)
            for g in range(4):
                s.wait_ge(combT_done, g + 1)
                s.activation(combT[:, 512 * g:512 * g + 512], bank(2 + g if g < 3 else 1, 512, E0), ACT.Copy).then_inc(comb_evac, 1)
            for g in range(2):
                s.wait_ge(combT_done, 5 + g)
                s.activation(combST[:, 1024 * g:1024 * g + 1024], combs_bank(g, 3 * E0), ACT.Copy).then_inc(comb_evac, 1)

            def silu_unit(b, u):
                s.wait_ge(up0, 9 * b + u + 1)
                u = u % 9
                s.activation(silu[:, u % 3, :], bank(u % 3), ACT.Silu,
                             bias=col("be1", u - 1) if u else col("bs1")).then_inc(silu0, 1)

            def block0(b, last):
                for u in range(9):
                    if not (last and u == 8):
                        silu_unit(b, u + 1)
                s.wait_ge(down0, b + 1)
                s.activation(T2[:, bass.ds(4 * b, 4), :], bank(6).rearrange("p (w n) -> p w n", w=4), ACT.Identity,
                             bias=bs2g[:, :], scale=tg[:, 2:3]).then_inc(acc0, 1)

            s.wait_ge(misc_dve, 1)
            silu_unit(0, 0)
            with s.Fori(0, B - 1) as b:
                block0(b, False)
            block0(B - 1, True)

            t_copy(T_DTW, T1)
            s.wait_ge(ln_out, B + W * 4)
            s.activation(Y2[:, :, :], Y[:, :, :], ACT.Square).then_inc(sq_done, 1)
            s.wait_ge(cost_step, 7)
            s.activation(Dt[:, :, 0:W], Dt[:, :, 0:W], ACT.Sqrt).then_inc(cost_sqrt, 1)

            for b in range(B):
                s.wait_ge(al_done, b + 1)
                s.activation(T2[:, :, C * b:C * b + C], bank(3 + b).rearrange("p (c w) -> p w c", w=W), ACT.Identity,
                             scale=tg[:, 1:2]).then_inc(al_evac, 1)
            t_copy(T_G1, T1)
            t_copy(T_E1, T2)
            s.wait_ge(route, R_L0 + R_EXP1)
            s.activation(small[:, 1, :], small[:, 0, :], ACT.Exp).then_inc(route_exp, 1)
            for g in range(2):
                s.wait_ge(combT_done, 7 + g)
                s.activation(combST[0:3 * E1, 1024 * g:1024 * g + 1024], combs_bank(g, 3 * E1), ACT.Copy).then_inc(comb_evac, 1)

            def gelu_unit(b, u):
                s.wait_ge(up1, 32 * b + u + 1)
                u = u % 32
                s.activation(gelu[:, u % 4, :], bank(u % 4), ACT.Gelu_apprx_tanh, bias=b1c[:, u:u + 1]).then_inc(gelu1, 1)

            s.wait_ge(b1_out, 1)
            gelu_unit(0, 0)
            with s.Fori(0, B - 1) as b:
                for u in range(32):
                    gelu_unit(b, u + 1)
            for u in range(31):
                gelu_unit(B - 1, u + 1)

        @block.tensor
        def _(pe):
            pe.sem_inc(pt_done, 12)
            pe.sem_inc(pv_done, 1)

            def t_set(k, src, ready):
                for g in range(4):
                    n = 4 * k + g
                    if n > 1:
                        pe.wait_ge(t_evac, n - 1)
                    for w in range(4 * g, 4 * g + 4):
                        ready(w)
                        ins = pe.transpose(bank(g % 2, P, lo=P * (w % 4)), src[:, w, :], ident[:, :])
                    ins.then_inc(t_done, 1)

            def ln_wait(k):
                return lambda w: pe.wait_ge(ln_out, B + W * (k - 1) + w + 1)

            def item(n):
                if n >= 4:
                    q = emptied(n - 4)
                    pe.wait_ge(prep_act if BY_ACT[n - 4] else prep_dve, q[0] if BY_ACT[n - 4] else q[1])
                return 2 + n % 4

            def have(n):
                q = emptied(n)
                pe.wait_ge(prep_act, q[0])
                if q[1]:
                    pe.wait_ge(prep_dve, q[1])

            pe.wait_ge(consts, 2)
            pe.wait_ge(in_rows, 16 * N_ROWS_DMA)
            pe.wait_ge(in_small, 16 * N_SMALL)
            pe.transpose(bank(2, NROWS), rows[:, :], ident[0:NROWS, 0:NROWS])
            pe.transpose(bank(2, E0, lo=NROWS), gate_rows[:, :], ident[0:E0, 0:E0]).then_inc(prep_done, 1)
            pe.wait_ge(in_ctx, 16)
            for b in range(B):
                ins = pe.transpose(bank(3, S, lo=S * b), cn[:, b, :], ident[0:S, 0:S])
            ins.then_inc(prep_done, 1)
            pe.wait_ge(ln_out, B)
            for b in range(B):
                ins = pe.transpose(bank(4, S, lo=S * b), cln[:, b, :], ident[0:S, 0:S])
            ins.then_inc(prep_done, 1)
            pe.wait_ge(in_wq, 16)
            for g in range(2):
                k = item(I_WQ + g)
                for q in range(4):
                    ins = pe.transpose(bank(k, P, lo=P * q), wq[:, P * (4 * g + q):P * (4 * g + q + 1)], ident[:, :])
                ins.then_inc(prep_done, 1)
            pe.wait_ge(in_wkv, 16)
            have(I_CLT)
            for q in range(16):
                k = item(I_K + q)
                pe.matmul(bank(k, B * S), wkv[:, P * q:P * q + P], clT, start=True, stop=True).then_inc(prep_done, 1)
            t_set(T_LAT, Y, ln_wait(2))
            have(I_V - 1)
            for h in range(H):
                k = item(I_A + h)
                r = slice(DH * (h % 2), DH * (h % 2) + DH)
                pe.matmul(bank(k, B * S), wqT[r, P * (h // 2):P * (h // 2) + P], kT[r, h // 2, :],
                          start=True, stop=True).then_inc(prep_done, 1)
            pe.wait_ge(in_wo, 16)
            have(I_A - 1)
            for h in range(H):
                k = item(I_BT + h)
                r = slice(DH * (h % 2), DH * (h % 2) + DH)
                pe.matmul(bank(k, B * S), wo[r, h // 2, :], vT[r, h // 2, :], start=True, stop=True).then_inc(prep_done, 1)
            have(I_B - 1)
            for b in range(B):
                for g, ks in enumerate(B_GROUPS):
                    k = item(I_B + 3 * b + g)
                    for q in ks:
                        ins = pe.transpose(bank(k, P, KC[q], P * (q % 4)), BT[:, b, P * q:P * q + KC[q]], ident[:, :])
                    ins.then_inc(prep_done, 1)
            have(N_PREP - 1)

            def scores(n, b, jj):
                pe.wait_ge(lat_slot, n + 1)
                h0 = 0
                for k, nh in enumerate(SCORE_HEADS):
                    m = 3 * jj + k
                    if jj >= 2:
                        pe.wait_ge(exp_done, 3 * n + k - 3)
                    elif m >= 4:
                        pe.wait_ge(exp_done, m - 3)
                    rhs = A[:, bass.ds(b, 1), h0 * S:(h0 + nh) * S].rearrange("p b n -> p (b n)")
                    pe.matmul(bank(2 + m % 4, nh * S), latb[:, jj % 4, :], rhs, start=True, stop=True).then_inc(score_done, 1)
                    h0 += nh

            def transpose_weights(n, j):
                pe.wait_ge(softmax_step, 4 * n + 4)
                for g, ks in enumerate(B_GROUPS):
                    pe.wait_ge(pt_free, 3 * n + g + 1)
                    for q in ks:
                        ins = pe.transpose(bank((3 * j + g) % 2, P, KC[q], P * (q % 4)),
                                           Et[:, j, P * q:P * q + KC[q]], ident[:, :])
                    ins.then_inc(pt_done, 1)

            def attention(b, last):
                for j in range(4):
                    if not (last and j > 1):
                        scores(4 * b + j + 2, b if j < 2 else b + 1, j + 2)
                    transpose_weights(4 * b + j, j)
                pe.wait_ge(b_slot, b + 1)
                pe.wait_ge(pv_free, b + 1)
                pe.wait_ge(pt_free, 2 + 3 * (4 * b + 3) + 3)
                for q, kc in enumerate(KC):
                    ins = pe.matmul(bank(6), Bs[0:kc, q, :], PT[0:kc, q, :], start=(q == 0), stop=(q == len(KC) - 1))
                ins.then_inc(pv_done, 1)

            pe.wait_ge(t_evac, 4 * T_LAT + 4)
            scores(0, 0, 0)
            scores(1, 0, 1)
            with pe.Fori(0, B - 1) as b:
                attention(b, False)
            attention(B - 1, True)
            pe.wait_ge(pv_free, 1 + B)
            t_set(T_X1, T2, lambda w: None)

            t_set(T_E0, Y, ln_wait(3))
            gwT = cols[:, NROWS:NROWS + E0]
            for w in range(W):
                if w % 4 == 0:
                    pe.wait_ge(t_evac, 4 * T_E0 + w // 4 + 1)
                ins = pe.matmul(bank(7, E0, lo=E0 * w), T1[:, w, :], gwT, start=True, stop=True)
            ins.then_inc(logits_done, 1)
            pe.wait_ge(in_fc1, 16)
            for e in range(E1):
                for f in range(4):
                    ins = pe.matmul(bank(5, 1, lo=128 + 4 * e + f), fc1[:, e, P * f:P * f + P],
                                    cols[:, COL["ln_b"] + e:COL["ln_b"] + e + 1], start=True, stop=True)
            ins.then_inc(b1_done, 1)
            pe.wait_ge(route, R_COMB0)
            for g in range(4):
                for q in range(4):
                    ins = pe.transpose(bank(2 + g if g < 3 else 1, P, E0, P * q), comb[:, 4 * g + q, :], ident[:, :])
                ins.then_inc(combT_done, 1)
            pe.wait_ge(route, R_L0)
            for g in range(2):
                for q in range(8):
                    ins = pe.transpose(combs_bank(g, 3 * E0)[:, P * q:P * q + P], combs[:, 8 * g + q, :], identb[:, :])
                ins.then_inc(combT_done, 1)
            pe.wait_ge(comb_evac, 6)
            pe.wait_ge(sel_ready, 6)
            pe.wait_ge(in_e0, 16 * 7)
            pe.wait_ge(b1_out, 1)

            def up_unit0(b, u):
                n = 9 * b + u
                if u == 9:
                    b, u = b + 1, 0
                rhs = T1[:, bass.ds(4 * b, 4), :].rearrange("p w n -> p (w n)")
                pe.wait_ge(glu0, n + 1)
                w1 = we1[:, 2 * u - 2:2 * u, :].rearrange("p e i -> p (e i)") if u else ws1[:, :]
                w3 = we3[:, 2 * u - 2:2 * u, :].rearrange("p e i -> p (e i)") if u else ws3[:, :]
                pe.matmul(bank(3 + u % 3), w3, rhs, start=True, stop=True)
                pe.matmul(bank(u % 3), w1, rhs, start=True, stop=True).then_inc(up0, 1)

            def block0(b, last):
                cols_b = bass.ds(b * N, N)
                for u in range(9):
                    if u == 0:
                        pe.wait_ge(acc0, b + 1)
                    if not (last and u == 8):
                        up_unit0(b, u + 1)
                    if u == 0:
                        pe.matmul(bank(6), be2[:, :], combT[:, cols_b], start=True, stop=False)
                        pe.wait_ge(glu0, 9 * b + 4)
                    else:
                        pe.wait_ge(scaled0, 8 * b + u)
                    ins = pe.matmul(bank(6), we2[:, u - 1, :] if u else ws2[:, :], glu[:, u % 3, :],
                                    start=False, stop=(u == 8))
                    if u == 8:
                        ins.then_inc(down0, 1)
                    else:
                        pe.matmul(bank(7), sel0[:, u, :], combST[:, cols_b], start=True, stop=True).then_inc(cb0, 1)

            up_unit0(0, 0)
            with pe.Fori(0, B - 1) as b:
                block0(b, False)
            block0(B - 1, True)
            pe.wait_ge(acc0, 1 + B)
            t_set(T_X2, T2, lambda w: None)

            pe.wait_ge(misc_act, 2)
            for b in range(B):
                ins = pe.matmul(PS[C * b:C * b + C, 5, 0:S], ones[:, :], csq[:, b, :], start=True, stop=True)
            ins.then_inc(aab_done, 1)
            t_set(T_DTW, Y, ln_wait(4))
            pe.wait_ge(t_evac, 4 * T_DTW + 4)
            for k, (lo, hi) in enumerate(COST_BANKS):
                for w in range(lo, hi):
                    for b in range(B):
                        ins = pe.matmul(PS[C * b:C * b + C, 2 + k, S * (w - lo):S * (w - lo) + S],
                                        T1[:, w, C * b:C * b + C], cT[:, b, :], start=True, stop=True)
                ins.then_inc(cost_mm, 1)

            pe.wait_ge(back, 3 * S)
            pe.wait_ge(dve_consts, 1)
            pe.transpose(bank(2, P, S), vals[:, 0:S], ident[:, :])
            pe.transpose(bank(2, P, S, P), vals[:, 1:S + 1], ident[:, :]).then_inc(vcol_done, 1)
            for b in range(B):
                pe.wait_ge(mask_done, b + 1)
                pe.matmul(bank(3 + b), cn[:, b, :], Mb[:, b, :], start=True, stop=True).then_inc(al_done, 1)
            pe.wait_ge(al_evac, B)
            t_set(T_X3, T2, lambda w: None)

            t_set(T_G1, Y, ln_wait(5))
            for w in range(W):
                if w % 4 == 0:
                    pe.wait_ge(t_evac, 4 * T_G1 + w // 4 + 1)
                ins = pe.matmul(bank(7, E1, lo=E1 * w), T1[:, w, :], wg1[:, :], start=True, stop=True)
            ins.then_inc(logits_done, 1)
            t_set(T_E1, Y2, ln_wait(6))
            pe.wait_ge(route, R_L0 + R_L1)
            for g in range(2):
                for q in range(8):
                    ins = pe.transpose(combs_bank(g, 3 * E1)[:, P * q:P * q + P], combs[:, 8 * g + q, 0:3 * E1], identb[:, :])
                ins.then_inc(combT_done, 1)
            pe.wait_ge(comb_evac, 8)
            pe.wait_ge(t_evac, 4 * T_E1 + 4)
            pe.wait_ge(in_fc2, 16)
            pe.wait_ge(fc1_scaled, E1)

            def up_unit1(b, u):
                n = 32 * b + u
                if u == 32:
                    b, u = b + 1, 0
                pe.wait_ge(gelu1, n + 1)
                pe.matmul(bank(u % 4), fc1[:, u // 4, P * (u % 4):P * (u % 4) + P],
                          T2[:, bass.ds(4 * b, 4), :].rearrange("p w n -> p (w n)"), start=True, stop=True).then_inc(up1, 1)

            def block1(b, last):
                for u in range(32):
                    e, f = u // 4, u % 4
                    if f == 0:
                        pe.wait_ge(cbs1, E1 * b + e + 1)
                    if not (last and u == 31):
                        up_unit1(b, u + 1)
                    if f == 0:
                        pe.matmul(bank(6 + e % 2), sel1[:, e, :], combST[0:3 * E1, bass.ds(b * N, N)],
                                  start=True, stop=True).then_inc(cb1, 1)
                        pe.wait_ge(y1_used, E1 * b + e + 1)
                    pe.wait_ge(gelu1, 32 * b + u + 5)
                    ins = pe.matmul(bank(4 + e % 2), fc2[:, e, f, :], gelu[:, f, :], start=(f == 0), stop=(f == 3))
                    if f == 3:
                        ins.then_inc(y1, 1)

            up_unit1(0, 0)
            with pe.Fori(0, B - 1) as b:
                block1(b, False)
            block1(B - 1, True)
            pe.wait_ge(acc1, 7 * B)
            t_set(T_OUT, T1, lambda w: None)


_INS = ["x", "ctx_1024", "g_xattn", "g_ffn",
        "L0_xattn_ln_l_w", "L0_xattn_ln_l_b", "L0_xattn_ln_c_w", "L0_xattn_ln_c_b", "L0_xattn_Wq", "L0_xattn_Wkv",
        "L0_xattn_Wo", "L0_xattn_bo", "L0_ffn_gate_w", "L0_ffn_gate_b", "L0_ffn_We1", "L0_ffn_be1", "L0_ffn_We2",
        "L0_ffn_be2", "L0_ffn_We3", "L0_ffn_be3", "L0_ffn_ws1", "L0_ffn_bs1", "L0_ffn_ws2", "L0_ffn_bs2",
        "L0_ffn_ws3", "L0_ffn_bs3", "L1_ffn_Wg", "L1_ffn_alpha", "L1_ffn_ln_w", "L1_ffn_ln_b", "L1_ffn_fc1_w",
        "L1_ffn_fc1_b", "L1_ffn_fc2_w", "L1_ffn_fc2_b"]


def kernel(**inputs):
    import numpy as _np
    import concourse.bacc as _bacc
    from concourse import mybir as _mybir
    from concourse.bass_utils import run_bass_kernel_spmd as _run

    nc = _bacc.Bacc("TRN2", target_bir_lowering=False, num_devices=1)
    arrays, args = {}, {}
    for name in _INS:
        v = _np.ascontiguousarray(inputs[name])
        arrays[f"in_{name}"] = v
        args[name] = nc.dram_tensor(f"in_{name}", v.shape, _mybir.dt.from_np(v.dtype), kind="ExternalInput").ap()
    out = nc.dram_tensor("out_0", (B, N, D), F32, kind="ExternalOutput").ap()
    build(nc, args, out)
    r = _run(nc, [arrays], core_ids=[0])
    return r.results[0]["out_0"]
```

```python
from contextlib import ExitStack

import concourse.bass as bass
from concourse import mybir

ALU = mybir.AluOpType
ACT = mybir.ActivationFunctionType
AX = mybir.AxisListType
F32 = mybir.dt.float32
BF16 = mybir.dt.bfloat16
U32 = mybir.dt.uint32
F32R = mybir.dt.float32r

P = 128
B, N, D = 4, 512, 128
S = 77
W = 16
C = N // W
H, DH = 16, 64
HS = H * S
E0, F0 = 16, 64
E1, F1 = 8, 512
EPS = 1e-5
BIG = 1e30
KC = [128] * (HS // 128) + [HS % 128]
SCORE_HEADS = [6, 5, 5]
STEPS = S + C - 1
ROWW = W + 1
PADROWS = S + 2 * (C - 1)
E_HI, E_LO = 59874.14171519782, 1.670170079024566e-05
CHOICE = [(0, 27), (27, 54), (54, 81), (81, STEPS)]
R_COMB0, R_L0, R_EXP1, R_L1 = 22, 27, 6, 17
NROWS = 80

I_COLS, I_CT, I_CLT, I_WQ, I_K, I_V, I_A, I_BT, I_B = 0, 1, 2, 3, 5, 13, 21, 37, 53
N_PREP = I_B + 3 * B
BY_ACT = [n < I_A or n % 2 == 0 for n in range(N_PREP)]


def emptied(n):
    acts = sum(BY_ACT[:n + 1])
    return acts, n + 1 - acts


COL = {"ln_l_w": 0, "ln_l_b": 1, "ln_c_w": 2, "ln_c_b": 3, "bo": 4, "bs1": 5, "bs2": 6, "bs3": 7,
       "be1": 8, "be3": 16, "ln_w": 24, "ln_b": 32, "fc2_b": 40, "fc1_b": 48}


def build(nc, a, out, stage=9):
    ctx = ExitStack()
    with ctx:
        at = {}

        def sb(name, shape, dt=F32):
            at[name] = (nc.sbuf_base + 31) // 32 * 32
            return ctx.enter_context(nc.sbuf_tensor(name, shape, dt))

        def part(name, region, words, shape):
            return nc.alloc_sbuf_tensor_at(name, shape, F32R, offset=at[region] + 4 * words)

        def sem(name):
            return ctx.enter_context(nc.semaphore(name))

        X = sb("X", [P, W, D])
        Y = sb("Y", [P, W, D])
        Y2 = sb("Y2", [P, W, D])
        T1 = sb("T1", [P, W, P])
        T2 = sb("T2", [P, W, P])
        stats = sb("stats", [P, W, 6])
        lnw = sb("lnw", [P, 8, W])
        ident = sb("ident", [P, P])
        identb = sb("identb", [P, P], BF16)
        ones = sb("ones", [P, C])
        halfneg = sb("halfneg", [P, W])
        rows = sb("rows", [NROWS, P])
        gate_rows = sb("gate_rows", [E0, P])
        cols = sb("cols", [P, NROWS + E0])
        gains = sb("gains", [P, 4])
        tg = sb("tg", [P, 4])
        bs2g = sb("bs2g", [P, 1])
        gate_b = sb("gate_b", [P, E0])
        alpha = sb("alpha", [P, E1])
        wg1 = sb("wg1", [P, E1])
        cn = sb("cn", [S, B, D])
        cln = Y2[0:S, 0:B, :]
        cT = sb("cT", [P, B, S])
        clT = Y2[:, 4:7, :].rearrange("p w d -> p (w d)")[:, 0:B * S]
        csq = sb("csq", [P, B, S])
        R1 = sb("R1", [P, 4096])
        wkv = R1[:, 0:2048]
        wq = R1[:, 2048:3072]
        wqT = R1[:, 3072:4096]
        R2 = sb("R2", [P, 2 * 8 * B * S])
        kT = R2[:, 0:8 * B * S].rearrange("p (q s) -> p q s", q=8)
        vT = R2[:, 8 * B * S:16 * B * S].rearrange("p (q s) -> p q s", q=8)
        fc1 = R2[:, 0:E1 * F1].rearrange("p (e f) -> p e f", e=E1)
        fc2 = R1[:, 0:4096].rearrange("p (e f d) -> p e f d", e=E1, f=4)
        wo = sb("wo", [P, 8, D])
        A = sb("A", [P, B, HS])
        R3 = sb("R3", [P, B * HS])
        BT = R3[:, :].rearrange("p (b n) -> p b n", b=B)
        Et = BT
        Bc = sb("Bc", [P, B, len(KC), D])
        Bs = sb("Bs", [P, len(KC), D])
        R4 = sb("R4", [P, len(KC) * N])
        PT = R4[:, :].rearrange("p (k n) -> p k n", k=len(KC))
        latb = sb("latb", [P, B, P])
        sums = sb("sums", [P, 2, H])
        we1 = sb("we1", [P, E0, F0])
        we3 = sb("we3", [P, E0, F0])
        we2 = sb("we2", [P, E0 // 2, D])
        be2 = sb("be2", [E0, D])
        ws1 = sb("ws1", [P, D])
        ws2 = sb("ws2", [P, D])
        ws3 = sb("ws3", [P, D])
        R4o = [0]

        def r4(shape_free, dt=F32, parts=P):
            n = 1
            for q in shape_free:
                n *= q
            words = n if dt == F32 or dt == U32 else (n + 1) // 2
            v = R4[0:parts, R4o[0]:R4o[0] + words]
            R4o[0] += words
            if dt != F32:
                v = v.bitcast(dt)
            names = " ".join(f"a{k}" for k in range(len(shape_free)))
            if len(shape_free) > 1:
                v = v.rearrange(f"p ({names}) -> p {names}", **{f"a{k}": q for k, q in enumerate(shape_free)})
            return v

        pr = r4([W, E0])
        scr = r4([W, E0])
        t4 = r4([9, W * 4])
        beat = r4([W, 4, 4])
        beat2 = r4([W, 4, 4])
        top = r4([W, 8])
        topi = r4([W, 8], U32)
        topf = r4([W, 8])
        oh1 = r4([W, E0])
        oh2 = r4([W, E0])
        comb = r4([W, E0])
        rest = r4([W, E0])
        combs = r4([W, 3 * E0], BF16)
        small = r4([6, W])
        low = sb("low", [P, 4, 4])
        iota_e = sb("iota_e", [P, E0])
        combT = sb("combT", [E0, N * B])
        combST = sb("combST", [3 * E0, N * B], BF16)
        sel0 = sb("sel0", [3 * E0, E0 // 2, P], BF16)
        sel1 = sb("sel1", [3 * E1, E1, P], BF16)
        Av = A[:, :, :].rearrange("p b n -> p (b n)")
        def slots(region, lo, n):
            return region[:, lo:lo + n * N].rearrange("p (s n) -> p s n", s=n)

        silu = slots(Av, 0, 3)
        glu = slots(Av, 3 * N, 3)
        glu_hi = part("glu_hi", "A", 6 * N, [P, 3, N])
        glu_lo = part("glu_lo", "R4", 0, [P, 3, N])
        we1_hi = part("we1_hi", "R3", 0, [P, E0, F0])
        we3_hi = part("we3_hi", "R3", E0 * F0, [P, E0, F0])
        we2_hi = part("we2_hi", "R3", 2 * E0 * F0, [P, E0 // 2, D])
        ws1_hi, ws2_hi, ws3_hi = (part(f"ws{k + 1}_hi", "R3", 3 * E0 * F0 + k * D, [P, D]) for k in range(3))
        we1_lo, we3_lo = (part(f"{k}_lo", k, 0, [P, E0, F0]) for k in ("we1", "we3"))
        we2_lo = part("we2_lo", "we2", 0, [P, E0 // 2, D])
        ws1_lo, ws2_lo, ws3_lo = (part(f"{k}_lo", k, 0, [P, D]) for k in ("ws1", "ws2", "ws3"))
        x0_hi = part("x0_hi", "Bc", 0, [P, W, P])
        x0_lo = part("x0_lo", "Bc", W * P, [P, W, P])
        fc1_hi = part("fc1_hi", "A", 0, [P, E1, F1])
        fc2_hi = part("fc2_hi", "Bc", 0, [P, E1, 4, D])
        fc1_lo = part("fc1_lo", "R2", 0, [P, E1, F1])
        fc2_lo = part("fc2_lo", "R1", 0, [P, E1, 4, D])
        x1_hi = part("x1_hi", "Y", 0, [P, W, P])
        x1_lo = part("x1_lo", "T2", 0, [P, W, P])
        gelu = slots(R3, 0, 4)
        yt = slots(R3, 4 * N, 2)
        cbs = slots(R3, 6 * N, 2)
        gelu_hi = part("gelu_hi", "R4", 0, [P, 4, N])
        gelu_lo = part("gelu_lo", "R4", 4 * N, [P, 4, N])
        b1c = sb("b1c", [P, E1 * 4])
        R3o = [0]

        def r3(*shape_free, parts=P):
            n = 1
            for q in shape_free:
                n *= q
            v = R3[0:parts, R3o[0]:R3o[0] + n]
            R3o[0] += n
            if len(shape_free) > 1:
                names = " ".join(f"a{k}" for k in range(len(shape_free)))
                v = v.rearrange(f"p ({names}) -> p {names}", **{f"a{k}": q for k, q in enumerate(shape_free)})
            return v

        Dt = r3(S, ROWW)
        bb = r3(W)
        aab = r3(S)
        base = r3(W, S)
        Bcv = Bc[:, :, :, :].rearrange("p b k d -> p (b k d)")
        Dsk = Bcv[:, 0:STEPS * ROWW].rearrange("p (t w) -> p t w", w=ROWW)
        Rh = Bcv[:, 1900:1900 + (STEPS + 1) * (W + 2)].rearrange("p (t w) -> p t w", w=W + 2)
        MH0 = R3o[0]
        mh = r3(STEPS, ROWW)
        du = R4[:, 0:STEPS * W].rearrange("p (t w) -> p t w", w=W)
        V = R4[:, STEPS * W:2 * STEPS * W].rearrange("p (t w) -> p t w", w=W)
        Vn_flat = base.rearrange("p w i -> p (w i)")
        Vn = Vn_flat.rearrange("p (i w) -> p i w", w=W)
        first = sb("first", [P, 1])
        block_last = sb("block_last", [P, 1])
        jj1 = sb("jj1", [P, W])
        jj2 = sb("jj2", [P, W])
        jrow = sb("jrow", [S, N])
        vals = sb("vals", [P, S + 1])
        pick = sb("pick", [P, W])
        pickm = sb("pickm", [P, 1])
        vcol = sb("vcol", [S, 2, P])
        Mb = R3[0:S, MH0:MH0 + 4 * N].rearrange("p (b n) -> p b n", b=B)
        mge = R4[0:S, 0:4 * N].rearrange("p (b n) -> p b n", b=B)
        bigrow = Bcv[:, 4096:4096 + (C - 1) * ROWW]

        PS = ctx.enter_context(nc.psum_tensor("PS", [P, 8, 512], F32))

        def bank(k, n=512, parts=P, lo=0):
            return PS[0:parts, k, lo:lo + n]

        Dscr = nc.dram_tensor("Dscr", [P, PADROWS * ROWW], F32, kind="Internal").ap()
        Vscr = nc.dram_tensor("Vscr", [P, STEPS * W], F32, kind="Internal").ap()
        Dskew = bass.AP(Dscr.tensor, (C - 1) * ROWW,
                        [[C * PADROWS * ROWW, B], [(PADROWS - 1) * ROWW, C], [1, STEPS * ROWW]])
        Vskew = bass.AP(Vscr.tensor, 0, [[C * STEPS * W, B], [(STEPS + 1) * W, C], [1, S * W]])

        in_x, in_ctx, in_rows, in_wkv, in_wq, in_wo, in_small, in_e0, in_fc1, in_fc2 = map(sem, [
            "in_x", "in_ctx", "in_rows", "in_wkv", "in_wq", "in_wo", "in_small", "in_e0", "in_fc1", "in_fc2"])
        const0, consts, sel_ready, dve_consts = map(sem, ["const0", "consts", "sel_ready", "dve_consts"])
        ln_stats, ln_math, ln_var, ln_rstd, ln_out = map(sem, ["ln_stats", "ln_math", "ln_var", "ln_rstd", "ln_out"])
        t_done, t_evac = map(sem, ["t_done", "t_evac"])
        prep_done, prep_act, prep_dve, misc_act, misc_dve = map(sem, [
            "prep_done", "prep_act", "prep_dve", "misc_act", "misc_dve"])
        lat_slot, b_slot, score_done, exp_done, softmax_step, pt_done, pt_free, pv_done, pv_free = map(sem, [
            "lat_slot", "b_slot", "score_done", "exp_done", "softmax_step", "pt_done", "pt_free", "pv_done", "pv_free"])
        logits_done, route, route_exp, combT_done, comb_evac = map(sem, [
            "logits_done", "route", "route_exp", "combT_done", "comb_evac"])
        b1_done, b1_out, fc1_scaled = map(sem, ["b1_done", "b1_out", "fc1_scaled"])
        up0, silu0, glu0, cb0, scaled0, glu_hi_done, glu_lo_done, down0, acc0 = map(sem, [
            "up0", "silu0", "glu0", "cb0", "scaled0", "glu_hi_done", "glu_lo_done", "down0", "acc0"])
        w0_hi, w0_lo, x0_hi_done, x0_lo_done = map(sem, ["w0_hi", "w0_lo", "x0_hi_done", "x0_lo_done"])
        fc_hi, fc_lo, x1_hi_done, x1_lo_done = map(sem, ["fc_hi", "fc_lo", "x1_hi_done", "x1_lo_done"])
        aab_done, cost_mm, cost_step, cost_sqrt, sq_done = map(sem, [
            "aab_done", "cost_mm", "cost_step", "cost_sqrt", "sq_done"])
        choice_pool, al_evac, vcol_out = map(sem, ["choice_pool", "al_evac", "vcol_out"])
        d_stored, d_loaded, v_stored, v_loaded = map(sem, ["d_stored", "d_loaded", "v_stored", "v_loaded"])
        dtw_init, row_done, pre_done, choice = map(sem, ["dtw_init", "row_done", "pre_done", "choice"])
        back, vcol_done, mask_done, al_done = map(sem, ["back", "vcol_done", "mask_done", "al_done"])
        up1, gelu1, cb1, cbs1, gelu_hi_done, gelu_lo_done, down1, y1_used, acc1 = map(sem, [
            "up1", "gelu1", "cb1", "cbs1", "gelu_hi_done", "gelu_lo_done", "down1", "y1_used", "acc1"])
        stored = sem("stored")

        T_LAT, T_X1, T_E0, T_X2, T_DTW, T_X3, T_G1, T_E1, T_OUT = range(9)

        block = ctx.enter_context(nc.Block())

        xv = a["x"].rearrange("b (c w) d -> (b c) w d", w=W)
        ov = out.rearrange("b (c w) d -> (b c) w d", w=W)

        N_ROWS_DMA = len(COL)
        N_SMALL = 6
        N_CONSTS = 2 + 4 * B + 3

        COST_BANKS = [(0, 6), (6, 12), (12, 16)]
        B_GROUPS = [range(0, 4), range(4, 8), range(8, 10)]

        def combs_bank(g, parts):
            return PS[0:parts, 6 + g, :].bitcast(BF16)

        SPLIT0 = [(w[:, :], w_hi[:, :], w_lo[:, :])
                  for w, w_hi, w_lo in ((ws1, ws1_hi, ws1_lo), (ws3, ws3_hi, ws3_lo), (ws2, ws2_hi, ws2_lo))]
        SPLIT0 += [(w[:, :, :], w_hi[:, :, :], w_lo[:, :, :])
                   for w, w_hi, w_lo in ((we1, we1_hi, we1_lo), (we3, we3_hi, we3_lo), (we2, we2_hi, we2_lo))]

        def prep_out(n, copy):
            k = 2 + n % 4
            if n == I_COLS:
                copy(cols[:, 0:NROWS], bank(k, NROWS))
                return copy(cols[:, NROWS:NROWS + E0], bank(k, E0, lo=NROWS))
            if n == I_CT:
                return copy(cT[:, :, :], bank(k, B * S).rearrange("p (b s) -> p b s", b=B))
            if n < I_K:
                return copy(wqT[:, 512 * (n - I_WQ):512 * (n - I_WQ) + 512], bank(k))
            if n < I_V:
                return copy(kT[:, n - I_K, :], bank(k, B * S))
            if n < I_A:
                return copy(vT[:, n - I_V, :], bank(k, B * S))
            if n < I_B:
                dst, h = (A, n - I_A) if n < I_BT else (BT, n - I_BT)
                return copy(dst[:, :, S * h:S * h + S], bank(k, B * S).rearrange("p (b s) -> p b s", b=B))
            b, g = (n - I_B) // 3, (n - I_B) % 3
            src = PS[:, k, :].rearrange("p (k d) -> p k d", k=4)
            if g < 2:
                return copy(Bc[:, b, 4 * g:4 * g + 4, :], src)
            copy(Bc[:, b, 8, :], src[:, 0, :])
            return copy(Bc[0:KC[9], b, 9, :], src[0:KC[9], 1, :])

        @block.sync
        def _(sp):
            sp.dma_start(cn[:, :, :], a["ctx_1024"].rearrange("b s d -> s b d")).then_inc(in_ctx, 16)
            for name, src, n in (("ln_l_w", "L0_xattn_ln_l_w", 0), ("ln_l_b", "L0_xattn_ln_l_b", 0),
                                 ("ln_c_w", "L0_xattn_ln_c_w", 0), ("ln_c_b", "L0_xattn_ln_c_b", 0),
                                 ("bo", "L0_xattn_bo", 0), ("bs1", "L0_ffn_bs1", 0), ("bs2", "L0_ffn_bs2", 0),
                                 ("bs3", "L0_ffn_bs3", 0), ("be1", "L0_ffn_be1", 8), ("be3", "L0_ffn_be3", 8),
                                 ("ln_w", "L1_ffn_ln_w", 8), ("ln_b", "L1_ffn_ln_b", 8),
                                 ("fc2_b", "L1_ffn_fc2_b", 8), ("fc1_b", "L1_ffn_fc1_b", 32)):
                v = a[src]
                if n == 0:
                    v = v.rearrange("(o d) -> o d", o=1)
                elif name in ("be1", "be3"):
                    v = v.rearrange("(q e) i -> q (e i)", e=2)
                elif name == "fc1_b":
                    v = v.rearrange("e (f i) -> (e f) i", i=P)
                sp.dma_start(rows[COL[name]:COL[name] + max(n, 1), :], v).then_inc(in_rows, 16)
            sp.dma_start(gate_rows[:, :], a["L0_ffn_gate_w"]).then_inc(in_small, 16)
            sp.dma_start(wq, a["L0_xattn_Wq"]).then_inc(in_wq, 16)
            sp.dma_start(we1[:, :, :], a["L0_ffn_We1"].rearrange("e d i -> d e i")).then_inc(in_e0, 16)
            sp.dma_start(we3[:, :, :], a["L0_ffn_We3"].rearrange("e d i -> d e i")).then_inc(in_e0, 16)
            sp.dma_start(we2[:, :, :], a["L0_ffn_We2"].rearrange("(q e) i d -> (e i) q d", e=2)).then_inc(in_e0, 16)
            sp.dma_start(be2[:, :], a["L0_ffn_be2"]).then_inc(in_e0, 16)
            sp.dma_start(ws1[:, :], a["L0_ffn_ws1"]).then_inc(in_e0, 16)
            sp.dma_start(ws2[:, :], a["L0_ffn_ws2"]).then_inc(in_e0, 16)
            sp.dma_start(ws3[:, :], a["L0_ffn_ws3"]).then_inc(in_e0, 16)
            sp.wait_ge(prep_done, N_PREP)
            sp.dma_start(fc1, a["L1_ffn_fc1_w"].rearrange("e d f -> d e f")).then_inc(in_fc1, 16)
            sp.dma_start(fc2, a["L1_ffn_fc2_w"].rearrange("e (f i) d -> i e f d", i=P)).then_inc(in_fc2, 16)
            sp.wait_ge(dtw_init, 1)
            sp.dma_start(Dscr[:, 0:(C - 1) * ROWW], bigrow).then_inc(d_stored, 16)
            sp.dma_start(Dscr[:, (C - 1 + S) * ROWW:PADROWS * ROWW], bigrow).then_inc(d_stored, 16)
            sp.wait_ge(cost_sqrt, 1)
            sp.dma_start(Dscr[:, (C - 1) * ROWW:(C - 1 + S) * ROWW],
                         Dt.rearrange("p t w -> p (t w)")).then_inc(d_stored, 16)
            sp.wait_ge(d_stored, 48)
            sp.dma_start(Dsk.rearrange("p t w -> p (t w)"), Dskew).then_inc(d_loaded, 16)
            for n, (lo, hi) in enumerate(CHOICE):
                sp.wait_ge(choice, n + 1)
                sp.dma_start(Vscr[:, lo * W:hi * W], V[:, lo:hi, :].rearrange("p t w -> p (t w)")).then_inc(v_stored, 16)
            sp.wait_ge(v_stored, 16 * len(CHOICE))
            sp.dma_start(Vn_flat, Vskew).then_inc(v_loaded, 16)
            for g in range(4):
                sp.wait_ge(t_evac, 4 * T_OUT + g + 1)
                sp.dma_start(ov[:, 4 * g:4 * g + 4, :], X[:, 4 * g:4 * g + 4, :]).then_inc(stored, 16)
            sp.wait_ge(stored, 64)

        @block.gpsimd
        def _(g):
            g.memset(ident[:, :], 0.0).then_inc(const0, 1)
            g.memset(identb[:, :], 0.0).then_inc(const0, 1)
            g.memset(ones[:, :], 1.0).then_inc(const0, 1)
            g.memset(halfneg[:, :], -0.5).then_inc(const0, 1)
            g.memset(first[:, :], BIG).then_inc(const0, 1)
            g.memset(block_last[:, :], 0.0).then_inc(const0, 1)
            g.memset(sel0[:, :, :], 0.0).then_inc(const0, 1)
            g.memset(sel1[:, :, :], 0.0).then_inc(const0, 1)
            g.memset(low[:, :, :], 1.0).then_inc(const0, 1)
            g.memset(Bc[:, :, len(KC) - 1, :], 0.0).then_inc(const0, 1)
            g.wait_ge(const0, 10)
            for m in (ident, identb):
                g.affine_select(out=m[:, :], in_=m[:, :], compare_op=ALU.not_equal, fill=1.0, base=0,
                                pattern=[[-1, P]], channel_multiplier=1).then_inc(consts, 1)

            def ln_power(k, n, parts=P):
                g.wait_ge(ln_var, k + 1)
                g.tensor_tensor(lnw[0:parts, 7, 0:n], lnw[0:parts, 6, 0:n], halfneg[0:parts, 0:n],
                                ALU.pow).then_inc(ln_rstd, 1)

            ln_power(0, B, S)
            ln_power(1, W)
            ln_power(2, W)
            for b in range(B):
                q = slice(C * b, C * b + C)
                if b == 0:
                    g.wait_ge(ln_rstd, 3)
                g.wait_ge(consts, 2 + 4 * b)
                g.affine_select(out=first[q, :], in_=first[q, :], compare_op=ALU.not_equal, fill=0.0, base=0,
                                pattern=[[0, 1]], channel_multiplier=1).then_inc(consts, 1)
                g.wait_ge(consts, 3 + 4 * b)
                g.affine_select(out=block_last[q, :], in_=block_last[q, :], compare_op=ALU.not_equal, fill=BIG,
                                base=-(C - 1), pattern=[[0, 1]], channel_multiplier=1).then_inc(consts, 1)
                g.wait_ge(consts, 4 + 4 * b)
                g.iota(jj1[q, :], pattern=[[2, W]], base=1, channel_multiplier=2 * W,
                       allow_small_or_imprecise_dtypes=True).then_inc(consts, 1)
                g.wait_ge(consts, 5 + 4 * b)
                g.iota(jj2[q, :], pattern=[[2, W]], base=2, channel_multiplier=2 * W,
                       allow_small_or_imprecise_dtypes=True).then_inc(consts, 1)
            g.wait_ge(consts, 2 + 4 * B)
            g.iota(jrow[:, :], pattern=[[2, N]], base=2, channel_multiplier=0,
                   allow_small_or_imprecise_dtypes=True).then_inc(consts, 1)
            g.iota(iota_e[:, :], pattern=[[1, E0]], base=0, channel_multiplier=0,
                   allow_small_or_imprecise_dtypes=True).then_inc(consts, 1)
            g.affine_select(out=low[:, :, :], in_=low[:, :, :], compare_op=ALU.is_gt, fill=0.0, base=0,
                            pattern=[[1, 4], [-1, 4]], channel_multiplier=0).then_inc(consts, 1)
            for part in range(3):
                v = sel0[:, :, :].rearrange("k q (e i) -> k q e i", e=2)
                if part:
                    g.wait_ge(sel_ready, 2 * part)
                g.affine_select(out=v, in_=v, compare_op=ALU.not_equal, fill=1.0, base=-E0 * part,
                                pattern=[[-2, E0 // 2], [-1, 2], [0, F0]], channel_multiplier=1).then_inc(sel_ready, 1)
                g.affine_select(out=sel1[:, :, :], in_=sel1[:, :, :], compare_op=ALU.not_equal, fill=1.0,
                                base=-E1 * part, pattern=[[-1, E1], [0, P]], channel_multiplier=1).then_inc(sel_ready, 1)

            def lat_copy(n, b, j):
                g.tensor_copy(latb[:, j, :].rearrange("p (w c) -> p w c", c=C),
                              T1[:, 4 * j:4 * j + 4, bass.ds(b * C, C)]).then_inc(lat_slot, 1)

            for j in range(4):
                g.wait_ge(t_evac, 4 * T_LAT + j + 1)
                lat_copy(j, 0, j)
            g.wait_ge(prep_act, emptied(N_PREP - 1)[0])
            g.wait_ge(prep_dve, emptied(N_PREP - 1)[1])
            g.tensor_copy(Bs[:, :, :], Bc[:, 0, :, :]).then_inc(b_slot, 1)
            with g.Fori(0, B - 1) as b:
                for j in range(4):
                    g.wait_ge(score_done, b * 12 + 3 * j + 3)
                    lat_copy(j, b + 1, j)
                g.wait_ge(pv_done, b + 2)
                g.tensor_copy(Bs[:, :, :], Bc[:, bass.ds(b + 1, 1), :, :].rearrange("p a k d -> p (a k) d")
                              ).then_inc(b_slot, 1)
            ln_power(3, W)
            for n, (w, w_hi, w_lo) in enumerate(SPLIT0):
                g.wait_ge(w0_hi, n + 1)
                g.tensor_tensor(w_lo, w, w_hi.bitcast(F32), ALU.subtract).then_inc(w0_lo, 1)
            for k in range(4):
                r = slice(4 * k, 4 * k + 4)
                g.wait_ge(x0_hi_done, k + 1)
                g.tensor_tensor(x0_lo[:, r, :], T1[:, r, :], x0_hi[:, r, :].bitcast(F32), ALU.subtract).then_inc(x0_lo_done, 1)
            g.wait_ge(b1_done, 1)
            for e in range(E1):
                g.tensor_scalar(fc1[:, e, :], fc1[:, e, :], cols[:, COL["ln_w"] + e:COL["ln_w"] + e + 1], 1.0,
                                ALU.mult, ALU.mult).then_inc(fc1_scaled, 1)
            ln_power(4, W)
            for e in range(E1):
                g.wait_ge(fc_hi, e + 1)
                g.tensor_tensor(fc1_lo[:, e, :], fc1[:, e, :], fc1_hi[:, e, :].bitcast(F32), ALU.subtract).then_inc(fc_lo, 1)

            for n, (lo, hi) in enumerate(CHOICE):
                g.wait_ge(row_done, hi)
                r = slice(lo, hi)
                g.tensor_tensor(du[:, r, :], Rh[:, r, 1:1 + W], Rh[:, r, 0:W], ALU.subtract).then_inc(choice_pool, 1)
                g.tensor_tensor(V[:, r, :], Rh[:, lo + 1:hi + 1, 0:W], mh[:, r, 0:W], ALU.subtract).then_inc(choice_pool, 1)
                g.wait_ge(choice_pool, 5 * n + 2)
                g.tensor_scalar(du[:, r, :], du[:, r, :], 0.0, None, ALU.is_lt).then_inc(choice_pool, 1)
                g.tensor_scalar(V[:, r, :], V[:, r, :], 0.0, None, ALU.is_ge).then_inc(choice_pool, 1)
                g.wait_ge(choice_pool, 5 * n + 4)
                g.tensor_tensor(du[:, r, :], du[:, r, :], jj1[:, :].unsqueeze(1).to_broadcast([P, hi - lo, W]),
                                ALU.add).then_inc(choice_pool, 1)
                g.wait_ge(choice_pool, 5 * n + 5)
                g.tensor_tensor(V[:, r, :], V[:, r, :], du[:, r, :], ALU.mult).then_inc(choice, 1)
            for e in range(E1):
                g.wait_ge(fc_hi, E1 + e + 1)
                g.tensor_tensor(fc2_lo[:, e, :, :], fc2[:, e, :, :], fc2_hi[:, e, :, :].bitcast(F32),
                                ALU.subtract).then_inc(fc_lo, 1)
            ln_power(5, W)
            ln_power(6, W)
            for k in range(4):
                r = slice(4 * k, 4 * k + 4)
                g.wait_ge(x1_hi_done, k + 1)
                g.tensor_tensor(x1_lo[:, r, :], T2[:, r, :], x1_hi[:, r, :].bitcast(F32), ALU.subtract).then_inc(x1_lo_done, 1)

        @block.vector
        def _(v):
            v.memset(vals[:, S:S + 1], 2.0 * N).then_inc(dve_consts, 1)
            v.sem_inc(pv_free, 1)
            v.sem_inc(glu0, 3)
            v.sem_inc(gelu_lo_done, 4)
            v.sem_inc(y1_used, 2)

            def col(name, k=0):
                return cols[:, COL[name] + k:COL[name] + k + 1]

            def layer_norm(k, src, dst, n, ready, parts=P):
                for w in range(n):
                    ready(w)
                    ins = v.bn_stats(stats[0:parts, w, :], src[:, w, :])
                ins.then_inc(ln_stats, 1)
                v.wait_ge(ln_stats, k + 1)
                q = lnw[0:parts, :, 0:n]
                st = stats[0:parts, 0:n, :]
                v.tensor_tensor(q[:, 0, :], st[:, :, 1], st[:, :, 4], ALU.add)
                v.tensor_tensor(q[:, 1, :], st[:, :, 1], st[:, :, 4], ALU.subtract)
                v.tensor_tensor(q[:, 2, :], st[:, :, 2], st[:, :, 5], ALU.add).then_inc(ln_math, 1)
                v.wait_ge(ln_math, 3 * k + 1)
                v.tensor_scalar(q[:, 3, :], q[:, 0, :], 0.5, None, ALU.mult)
                v.scalar_tensor_tensor(out=q[:, 4, :], in0=q[:, 1, :], scalar=0.25, in1=q[:, 1, :],
                                       op0=ALU.mult, op1=ALU.mult).then_inc(ln_math, 1)
                v.wait_ge(ln_math, 3 * k + 2)
                v.scalar_tensor_tensor(out=q[:, 5, :], in0=q[:, 2, :], scalar=1.0 / D, in1=q[:, 4, :],
                                       op0=ALU.mult, op1=ALU.add).then_inc(ln_math, 1)
                v.wait_ge(ln_math, 3 * k + 3)
                v.tensor_scalar(q[:, 6, :], q[:, 5, :], EPS, None, ALU.add).then_inc(ln_var, 1)
                v.wait_ge(ln_rstd, k + 1)
                for w in range(n):
                    v.tensor_scalar(dst[:, w, :], src[:, w, :], q[:, 3, w:w + 1], lnw[0:parts, 7, w:w + 1],
                                    ALU.subtract, ALU.mult).then_inc(ln_out, 1)

            def ln_ready(k, w):
                return B + W * (k - 1) + w + 1

            def add_back(k):
                for g in range(4):
                    v.wait_ge(t_done, 4 * k + g + 1)
                    x4 = X[:, 4 * g:4 * g + 4, :]
                    v.tensor_tensor(x4, bank(g % 2).rearrange("p (w d) -> p w d", w=4), x4, ALU.add).then_inc(t_evac, 1)

            v.wait_ge(in_ctx, 16)
            layer_norm(0, cn[:, :, :], cln, B, lambda w: None, S)
            v.wait_ge(in_x, 16)
            layer_norm(1, X, Y, W, lambda w: None)
            layer_norm(2, Y, Y, W, lambda w: v.wait_ge(ln_out, ln_ready(1, w)))
            v.wait_ge(prep_act, 1)
            for g in range(4):
                v.wait_ge(t_done, 4 * T_LAT + g + 1)
                v.tensor_scalar(T1[:, 4 * g:4 * g + 4, :], bank(g % 2).rearrange("p (w n) -> p w n", w=4),
                                col("ln_l_w"), col("ln_l_b"), ALU.mult, ALU.add).then_inc(t_evac, 1)
            for n in range(I_A, N_PREP):
                if not BY_ACT[n]:
                    v.wait_ge(prep_done, n + 1)
                    prep_out(n, lambda o, i: v.tensor_copy(o, i)).then_inc(prep_dve, 1)
            v.wait_ge(misc_act, 1)
            v.tensor_tensor(bs2g[:, :], col("bs2"), tg[:, 2:3], ALU.mult).then_inc(misc_dve, 1)

            def softmax(n, j):
                e = Et[:, j, :]
                eh = e.rearrange("p (h s) -> p h s", h=H)
                v.wait_ge(exp_done, 3 * n + 3)
                v.tensor_scalar(e, e, E_HI, E_LO, ALU.min, ALU.max).then_inc(softmax_step, 1)
                v.wait_ge(softmax_step, 4 * n + 1)
                v.tensor_reduce(sums[:, 0, :], eh, AX.X, ALU.add).then_inc(softmax_step, 1)
                v.wait_ge(softmax_step, 4 * n + 2)
                v.reciprocal(sums[:, 1, :], sums[:, 0, :]).then_inc(softmax_step, 1)
                v.wait_ge(softmax_step, 4 * n + 3)
                v.tensor_tensor(eh, eh, sums[:, 1, :].unsqueeze(2).to_broadcast([P, H, S]), ALU.mult
                                ).then_inc(softmax_step, 1)

            def attention(b, last):
                softmax(4 * b + 2, 2)
                softmax(4 * b + 3, 3)
                if not last:
                    softmax(4 * b + 4, 0)
                    softmax(4 * b + 5, 1)
                v.wait_ge(pv_done, b + 2)
                v.tensor_scalar(T2[:, :, bass.ds(b * C, C)], bank(6).rearrange("p (w c) -> p w c", w=W),
                                col("bo"), tg[:, 0:1], ALU.add, ALU.mult).then_inc(pv_free, 1)

            softmax(0, 0)
            softmax(1, 1)
            with v.Fori(0, B - 1) as b:
                attention(b, False)
            attention(B - 1, True)
            add_back(T_X1)

            layer_norm(3, X, Y, W, lambda w: v.wait_ge(t_evac, 4 * T_X1 + w // 4 + 1))
            r = [0]

            def did(ins):
                ins.then_inc(route, 1)
                r[0] += 1

            def so_far():
                v.wait_ge(route, r[0])

            def per_token(x, n):
                return x.unsqueeze(2).to_broadcast([P, W, n])

            def top_two(values, n):
                for w in range(W):
                    ins = v.max(top[:, w, :], values[:, w, :])
                did(ins)
                so_far()
                for w in range(W):
                    ins = v.max_index(topi[:, w, :], top[:, w, :], values[:, w, :])
                did(ins)
                so_far()
                did(v.tensor_copy(topf, topi))
                so_far()
                ie = iota_e[:, 0:n].unsqueeze(1).to_broadcast([P, W, n])
                v.tensor_tensor(oh1[:, :, 0:n], ie, per_token(topf[:, :, 0], n), ALU.is_equal)
                did(v.tensor_tensor(oh2[:, :, 0:n], ie, per_token(topf[:, :, 1], n), ALU.is_equal))
                so_far()

            def split(c, n):
                did(v.tensor_copy(combs[:, :, 0:n], c))
                so_far()
                did(v.tensor_tensor(rest[:, :, 0:n], c, combs[:, :, 0:n], ALU.subtract))
                so_far()
                did(v.tensor_copy(combs[:, :, n:2 * n], rest[:, :, 0:n]))
                so_far()
                did(v.tensor_tensor(scr[:, :, 0:n], rest[:, :, 0:n], combs[:, :, n:2 * n], ALU.subtract))
                so_far()
                did(v.tensor_copy(combs[:, :, 2 * n:3 * n], scr[:, :, 0:n]))

            v.wait_ge(consts, N_CONSTS)
            v.wait_ge(in_small, 16 * N_SMALL)
            v.wait_ge(logits_done, 1)
            lg = bank(7, W * E0).rearrange("p (w e) -> p w e", w=W)
            did(v.tensor_reduce(small[:, 0, :], lg, AX.X, ALU.max))
            so_far()
            did(v.tensor_tensor(scr, lg, per_token(small[:, 0, :], E0), ALU.subtract))
            v.wait_ge(route_exp, 1)
            did(v.tensor_reduce(small[:, 1, :], pr, AX.X, ALU.add))
            so_far()
            did(v.reciprocal(small[:, 2, :], small[:, 1, :]))
            so_far()
            did(v.tensor_tensor(pr, pr, per_token(small[:, 2, :], E0), ALU.mult))
            so_far()
            did(v.tensor_tensor(scr, pr, gate_b[:, :].unsqueeze(1).to_broadcast([P, W, E0]), ALU.add))
            so_far()
            q4 = scr.rearrange("p w (g k) -> p (w g) k", k=4)
            hi1, lo1, hi2, lo2, m1, mlo, mhi, m2, gs = (t4[:, k, :] for k in range(9))
            v.tensor_tensor(hi1, q4[:, :, 0], q4[:, :, 1], ALU.max)
            v.tensor_tensor(lo1, q4[:, :, 0], q4[:, :, 1], ALU.min)
            v.tensor_tensor(hi2, q4[:, :, 2], q4[:, :, 3], ALU.max)
            did(v.tensor_tensor(lo2, q4[:, :, 2], q4[:, :, 3], ALU.min))
            so_far()
            v.tensor_tensor(m1, hi1, hi2, ALU.max)
            v.tensor_tensor(mlo, hi1, hi2, ALU.min)
            did(v.tensor_tensor(mhi, lo1, lo2, ALU.max))
            so_far()
            did(v.tensor_tensor(m2, mlo, mhi, ALU.max))
            so_far()
            did(v.tensor_tensor(gs, m1, m2, ALU.add))
            so_far()
            gw = gs.rearrange("p (w g) -> p w g", g=4)
            mine = gw.unsqueeze(3).to_broadcast([P, W, 4, 4])
            other = gw.unsqueeze(2).to_broadcast([P, W, 4, 4])
            v.tensor_tensor(beat, other, mine, ALU.is_gt)
            did(v.tensor_tensor(beat2, other, mine, ALU.is_equal))
            so_far()
            did(v.tensor_tensor(beat2, beat2, low[:, :, :].unsqueeze(1).to_broadcast([P, W, 4, 4]), ALU.mult))
            so_far()
            did(v.tensor_tensor(beat, beat, beat2, ALU.add))
            so_far()
            did(v.tensor_reduce(hi1, beat.rearrange("p w g o -> p (w g) o"), AX.X, ALU.add))
            so_far()
            did(v.tensor_scalar(lo1, hi1, 2.0, -BIG, ALU.is_ge, ALU.mult))
            so_far()
            did(v.tensor_tensor(q4, q4, lo1.unsqueeze(2).to_broadcast([P, W * 4, 4]), ALU.add))
            so_far()
            top_two(scr, E0)
            did(v.tensor_tensor(oh1, oh1, oh2, ALU.add))
            so_far()
            did(v.tensor_tensor(comb, oh1, pr, ALU.mult))
            so_far()
            split(comb, E0)
            v.wait_ge(b1_done, 1)
            v.tensor_tensor(b1c[:, :], bank(5, 32, lo=128), cols[:, COL["fc1_b"]:COL["fc1_b"] + 32], ALU.add
                            ).then_inc(b1_out, 1)

            def glu_unit(b, u):
                n = 9 * b + u
                u = u % 9
                v.wait_ge(silu0, n + 1)
                v.scalar_tensor_tensor(out=glu[:, u % 3, :], in0=bank(3 + u % 3),
                                       scalar=col("be3", u - 1) if u else col("bs3"), in1=silu[:, u % 3, :],
                                       op0=ALU.add, op1=ALU.mult).then_inc(glu0, 1)

            def block0(b, last):
                for u in range(9):
                    if u:
                        v.wait_ge(cb0, 8 * b + u)
                        v.wait_ge(glu0, 9 * b + u + 4)
                        v.tensor_tensor(glu[:, u % 3, :], glu[:, u % 3, :], bank(7), ALU.mult).then_inc(scaled0, 1)
                    if not (last and u == 8):
                        glu_unit(b, u + 1)
                    v.wait_ge(glu_hi_done, 9 * b + u + 1)
                    v.tensor_tensor(glu_lo[:, u % 3, :], glu[:, u % 3, :], glu_hi[:, u % 3, :].bitcast(F32),
                                    ALU.subtract).then_inc(glu_lo_done, 1)

            glu_unit(0, 0)
            with v.Fori(0, B - 1) as b:
                block0(b, False)
            block0(B - 1, True)
            add_back(T_X2)
            v.memset(mh[:, :, W:ROWW], BIG)
            v.memset(Rh[:, 0, :], BIG)
            v.memset(Rh[:, 1, 0:1], BIG)
            v.memset(bigrow, BIG).then_inc(dtw_init, 1)

            layer_norm(4, X, Y, W, lambda w: v.wait_ge(t_evac, 4 * T_X2 + w // 4 + 1))
            v.wait_ge(aab_done, 1)
            v.tensor_copy(aab, bank(5, S)).then_inc(cost_step, 1)
            v.wait_ge(sq_done, 1)
            v.tensor_reduce(bb, Y2[:, :, :], AX.X, ALU.add).then_inc(cost_step, 1)
            v.wait_ge(cost_step, 2)
            v.tensor_tensor(base, aab.unsqueeze(1).to_broadcast([P, W, S]), bb.unsqueeze(2).to_broadcast([P, W, S]),
                            ALU.add).then_inc(cost_step, 1)
            v.wait_ge(cost_step, 3)
            v.tensor_copy(Dt[:, :, W:ROWW], block_last[:, :].unsqueeze(1).to_broadcast([P, S, 1]))
            for k, (lo, hi) in enumerate(COST_BANKS):
                v.wait_ge(cost_mm, k + 1)
                v.scalar_tensor_tensor(out=Dt[:, :, lo:hi].rearrange("p i w -> p w i"),
                                       in0=bank(2 + k, (hi - lo) * S).rearrange("p (w i) -> p w i", i=S), scalar=-2.0,
                                       in1=base[:, lo:hi, :], op0=ALU.mult, op1=ALU.add).then_inc(cost_step, 1)
            v.wait_ge(cost_step, 6)
            v.tensor_scalar(Dt[:, :, 0:W], Dt[:, :, 0:W], 0.0, None, ALU.max).then_inc(cost_step, 1)

            v.wait_ge(dve_consts, 1)
            v.wait_ge(dtw_init, 1)
            v.wait_ge(d_loaded, 16)
            shift = [C - 1] + list(range(C - 1))
            for t in range(STEPS):
                if t:
                    v.wait_ge(row_done, t)
                    v.stream_shuffle(Rh[:, t + 1, 0:1], Rh[:, t, W + 1:W + 2], shift)
                v.tensor_tensor(mh[:, t, 0:W], Rh[:, t, 1:1 + W], Rh[:, t, 0:W], ALU.min).then_inc(pre_done, 1)
                v.wait_ge(pre_done, t + 1)
                v.tensor_tensor_scan(Rh[:, t + 1, 1:2 + W], mh[:, t, :], Dsk[:, t, :],
                                     Rh[:, t + 1, 0:1] if t else first[:, :], ALU.min, ALU.add).then_inc(row_done, 1)

            v.wait_ge(v_loaded, 16)
            for n, i in enumerate(range(S - 1, -1, -1)):
                v.scalar_tensor_tensor(out=pick[:, :], in0=jj2[:, :], scalar=vals[:, i + 1:i + 2], in1=Vn[:, i, :],
                                       op0=ALU.is_le, op1=ALU.mult).then_inc(back, 1)
                v.wait_ge(back, 3 * n + 1)
                v.tensor_reduce(pickm[:, :], pick[:, :], AX.X, ALU.max).then_inc(back, 1)
                v.wait_ge(back, 3 * n + 2)
                v.tensor_reduce(vals[:, i:i + 1], pickm[:, :].to_broadcast([P, C]), AX.X, ALU.max,
                                apply_transpose=True).then_inc(back, 1)
                v.wait_ge(back, 3 * n + 3)
            v.wait_ge(vcol_done, 1)
            v.tensor_copy(vcol[:, :, :], bank(2, 2 * P, S).rearrange("p (k n) -> p k n", k=2)).then_inc(vcol_out, 1)
            v.wait_ge(vcol_out, 1)
            for b in range(B):
                v.tensor_scalar(mge[:, b, :], jrow[:, :], vcol[:, 0, C * b:C * b + 1], None, ALU.is_ge).then_inc(vcol_out, 1)
                v.wait_ge(vcol_out, 2 + b)
                v.scalar_tensor_tensor(out=Mb[:, b, :], in0=jrow[:, :], scalar=vcol[:, 1, C * b:C * b + 1],
                                       in1=mge[:, b, :], op0=ALU.is_le, op1=ALU.mult).then_inc(mask_done, 1)
            add_back(T_X3)

            layer_norm(5, X, Y, W, lambda w: v.wait_ge(t_evac, 4 * T_X3 + w // 4 + 1))
            layer_norm(6, Y, Y2, W, lambda w: v.wait_ge(ln_out, ln_ready(5, w)))
            v.wait_ge(logits_done, 2)
            lg1 = scr[:, :, 0:E1]
            did(v.tensor_copy(lg1, bank(7, W * E1).rearrange("p (w e) -> p w e", w=W)))
            so_far()
            top_two(lg1, E1)
            did(v.tensor_tensor(small[:, 0, :], top[:, :, 1], top[:, :, 0], ALU.subtract))
            v.wait_ge(route_exp, 2)
            did(v.tensor_scalar(small[:, 2, :], small[:, 1, :], 1.0, None, ALU.add))
            so_far()
            did(v.reciprocal(small[:, 3, :], small[:, 2, :]))
            so_far()
            did(v.tensor_tensor(small[:, 4, :], small[:, 1, :], small[:, 3, :], ALU.mult))
            so_far()
            v.tensor_tensor(oh1[:, :, 0:E1], oh1[:, :, 0:E1], per_token(small[:, 3, :], E1), ALU.mult)
            did(v.tensor_tensor(oh2[:, :, 0:E1], oh2[:, :, 0:E1], per_token(small[:, 4, :], E1), ALU.mult))
            so_far()
            did(v.tensor_tensor(oh1[:, :, 0:E1], oh1[:, :, 0:E1], oh2[:, :, 0:E1], ALU.add))
            so_far()
            did(v.tensor_tensor(comb[:, :, 0:E1], oh1[:, :, 0:E1],
                                alpha[:, :].unsqueeze(1).to_broadcast([P, W, E1]), ALU.mult))
            so_far()
            split(comb[:, :, 0:E1], E1)
            assert r[0] == R_L0 + R_L1, r[0]

            def gelu_low(b, u):
                n = 32 * b + u
                v.wait_ge(gelu_hi_done, n + 1)
                v.tensor_tensor(gelu_lo[:, u % 4, :], gelu[:, u % 4, :], gelu_hi[:, u % 4, :].bitcast(F32),
                                ALU.subtract).then_inc(gelu_lo_done, 1)

            def block1(b, last):
                acc = T1[:, bass.ds(4 * b, 4), :].rearrange("p w n -> p (w n)")
                for u in range(3, 35):
                    if not (last and u > 31):
                        gelu_low(b, u)
                    e, step = (u - 4) // 4, u % 4
                    n = E1 * b + e
                    if u > 3 and step == 0:
                        v.wait_ge(cb1, n + 1)
                        v.tensor_copy(cbs[:, e % 2, :], bank(6 + e % 2)).then_inc(cbs1, 1)
                    if u > 3 and step == 1:
                        v.wait_ge(cbs1, n + 1)
                        v.wait_ge(down1, 4 * n + 8)
                        v.scalar_tensor_tensor(out=yt[:, e % 2, :] if e else acc, in0=bank(4 + e % 2),
                                               scalar=col("fc2_b", e), in1=cbs[:, e % 2, :],
                                               op0=ALU.add, op1=ALU.mult).then_inc(y1_used, 1)
                    if step == 2 and e:
                        v.wait_ge(y1_used, n + 3)
                        if e > 1:
                            v.wait_ge(acc1, 7 * b + e - 1)
                        v.tensor_tensor(acc, acc, yt[:, e % 2, :], ALU.add).then_inc(acc1, 1)

            for u in range(3):
                gelu_low(0, u)
            with v.Fori(0, B - 1) as b:
                block1(b, False)
            block1(B - 1, True)
            for g in range(4):
                v.wait_ge(t_done, 4 * T_OUT + g + 1)
                x4 = X[:, 4 * g:4 * g + 4, :]
                v.scalar_tensor_tensor(out=x4, in0=bank(g % 2).rearrange("p (w d) -> p w d", w=4), scalar=tg[:, 3:4],
                                       in1=x4, op0=ALU.mult, op1=ALU.add).then_inc(t_evac, 1)

        @block.scalar
        def _(s):
            s.dma_start(X[:, :, :], xv).then_inc(in_x, 16)
            s.dma_start(wkv, a["L0_xattn_Wkv"]).then_inc(in_wkv, 16)
            s.dma_start(gains[:, 0:2], a["g_xattn"].partition_broadcast(P)).then_inc(in_small, 16)
            s.dma_start(gains[:, 2:4], a["g_ffn"].partition_broadcast(P)).then_inc(in_small, 16)
            s.dma_start(gate_b[:, :], a["L0_ffn_gate_b"].partition_broadcast(P)).then_inc(in_small, 16)
            s.dma_start(alpha[:, :], a["L1_ffn_alpha"].partition_broadcast(P)).then_inc(in_small, 16)
            s.dma_start(wg1[:, :], a["L1_ffn_Wg"]).then_inc(in_small, 16)
            s.dma_start(wo[:, :, :], a["L0_xattn_Wo"].rearrange("(q i) d -> i q d", i=P)).then_inc(in_wo, 16)
            s.sem_inc(pt_free, 2)
            s.sem_inc(acc0, 1)
            s.sem_inc(gelu1, 4)

            def col(name, k=0):
                return cols[:, COL[name] + k:COL[name] + k + 1]

            s.wait_ge(in_small, 16 * N_SMALL)
            s.activation(tg[:, :], gains[:, :], ACT.Tanh).then_inc(misc_act, 1)
            for n in range(N_PREP):
                if BY_ACT[n]:
                    s.wait_ge(prep_done, n + 1)
                    if n == I_CLT:
                        s.wait_ge(prep_act, 1)
                        s.activation(clT, bank(2 + n % 4, B * S), ACT.Identity, bias=col("ln_c_b"),
                                     scale=col("ln_c_w")).then_inc(prep_act, 1)
                    else:
                        prep_out(n, lambda o, i: s.activation(o, i, ACT.Copy)).then_inc(prep_act, 1)
                if n == I_CLT:
                    s.wait_ge(prep_act, 2)
                    s.activation(csq[:, :, :], cT[:, :, :], ACT.Square).then_inc(misc_act, 1)

            def exps(n, jj):
                s.wait_ge(pt_done, 3 * n + 3)
                h0 = 0
                for k, nh in enumerate(SCORE_HEADS):
                    s.wait_ge(score_done, 3 * n + k + 1)
                    s.activation(Et[:, jj % 4, h0 * S:(h0 + nh) * S], bank(2 + (3 * jj + k) % 4, nh * S), ACT.Exp,
                                 scale=DH ** -0.5).then_inc(exp_done, 1)
                    h0 += nh

            def weights_out(n, b, j):
                for g in range(3):
                    s.wait_ge(pt_done, 12 + 3 * n + g + 1)
                    if j == 0 and g == 0:
                        s.wait_ge(pv_done, b + 1)
                    k0 = 4 * g
                    src = PS[:, (3 * j + g) % 2, :].rearrange("p (k n) -> p k n", k=4)
                    if g < 2:
                        s.activation(PT[:, k0:k0 + 4, P * j:P * j + P], src, ACT.Copy).then_inc(pt_free, 1)
                    else:
                        s.activation(PT[:, 8, P * j:P * j + P], src[:, 0, :], ACT.Copy)
                        s.activation(PT[0:KC[9], 9, P * j:P * j + P], src[0:KC[9], 1, :], ACT.Copy).then_inc(pt_free, 1)

            exps(0, 0)
            exps(1, 1)

            def attention(b, last):
                for j in range(4):
                    if not (last and j > 1):
                        exps(4 * b + j + 2, j + 2)
                    weights_out(4 * b + j, b, j)

            with s.Fori(0, B - 1) as b:
                attention(b, False)
            attention(B - 1, True)

            def t_copy(k, dst):
                for g in range(4):
                    s.wait_ge(t_done, 4 * k + g + 1)
                    s.activation(dst[:, 4 * g:4 * g + 4, :], bank(g % 2).rearrange("p (w n) -> p w n", w=4),
                                 ACT.Copy).then_inc(t_evac, 1)

            s.wait_ge(in_e0, 16 * 7)
            for w, w_hi, _ in SPLIT0:
                s.activation(w_hi, w, ACT.Copy).then_inc(w0_hi, 1)
            s.wait_ge(b_slot, B)
            t_copy(T_E0, T1)
            for k in range(4):
                r = slice(4 * k, 4 * k + 4)
                s.wait_ge(t_evac, 4 * T_E0 + k + 1)
                s.activation(x0_hi[:, r, :], T1[:, r, :], ACT.Copy).then_inc(x0_hi_done, 1)
            s.wait_ge(route, 2)
            s.activation(pr, scr, ACT.Exp).then_inc(route_exp, 1)
            for g in range(4):
                s.wait_ge(combT_done, g + 1)
                s.activation(combT[:, 512 * g:512 * g + 512], bank(2 + g if g < 3 else 1, 512, E0), ACT.Copy).then_inc(comb_evac, 1)
            for g in range(2):
                s.wait_ge(combT_done, 5 + g)
                s.activation(combST[:, 1024 * g:1024 * g + 1024], combs_bank(g, 3 * E0), ACT.Copy).then_inc(comb_evac, 1)

            def silu_unit(b, u):
                s.wait_ge(up0, 9 * b + u + 1)
                u = u % 9
                s.activation(silu[:, u % 3, :], bank(u % 3), ACT.Silu,
                             bias=col("be1", u - 1) if u else col("bs1")).then_inc(silu0, 1)

            def glu_high(b, u):
                n = 9 * b + u
                if u % 9:
                    s.wait_ge(scaled0, 8 * b + u)
                else:
                    s.wait_ge(glu0, n + 4)
                s.wait_ge(down0, n + 1)
                s.activation(glu_hi[:, u % 3, :], glu[:, u % 3, :], ACT.Copy).then_inc(glu_hi_done, 1)

            def block0(b, last):
                for u in range(1, 9):
                    if not (last and u == 8):
                        silu_unit(b, u + 1)
                    glu_high(b, u)
                if not last:
                    silu_unit(b, 10)
                s.wait_ge(down0, 9 * b + 12)
                s.activation(T2[:, bass.ds(4 * b, 4), :], bank(6).rearrange("p (w n) -> p w n", w=4), ACT.Identity,
                             bias=bs2g[:, :], scale=tg[:, 2:3]).then_inc(acc0, 1)
                if not last:
                    glu_high(b, 9)

            s.wait_ge(misc_dve, 1)
            silu_unit(0, 0)
            silu_unit(0, 1)
            glu_high(0, 0)
            with s.Fori(0, B - 1) as b:
                block0(b, False)
            block0(B - 1, True)

            s.wait_ge(fc1_scaled, E1)
            for e in range(E1):
                s.activation(fc1_hi[:, e, :], fc1[:, e, :], ACT.Copy).then_inc(fc_hi, 1)
            t_copy(T_DTW, T1)
            s.wait_ge(ln_out, B + W * 4)
            s.activation(Y2[:, :, :], Y[:, :, :], ACT.Square).then_inc(sq_done, 1)
            s.wait_ge(cost_step, 7)
            s.activation(Dt[:, :, 0:W], Dt[:, :, 0:W], ACT.Sqrt).then_inc(cost_sqrt, 1)

            s.wait_ge(in_fc2, 16)
            s.wait_ge(choice, len(CHOICE))
            for e in range(E1):
                s.activation(fc2_hi[:, e, :, :], fc2[:, e, :, :], ACT.Copy).then_inc(fc_hi, 1)
            for b in range(B):
                s.wait_ge(al_done, b + 1)
                s.activation(T2[:, :, C * b:C * b + C], bank(3 + b).rearrange("p (c w) -> p w c", w=W), ACT.Identity,
                             scale=tg[:, 1:2]).then_inc(al_evac, 1)
            t_copy(T_G1, T1)
            t_copy(T_E1, T2)
            for k in range(4):
                r = slice(4 * k, 4 * k + 4)
                s.wait_ge(t_evac, 4 * T_E1 + k + 1)
                s.activation(x1_hi[:, r, :], T2[:, r, :], ACT.Copy).then_inc(x1_hi_done, 1)
            s.wait_ge(route, R_L0 + R_EXP1)
            s.activation(small[:, 1, :], small[:, 0, :], ACT.Exp).then_inc(route_exp, 1)
            for g in range(2):
                s.wait_ge(combT_done, 7 + g)
                s.activation(combST[0:3 * E1, 1024 * g:1024 * g + 1024], combs_bank(g, 3 * E1), ACT.Copy).then_inc(comb_evac, 1)

            def gelu_unit(b, u):
                n = 32 * b + u
                s.wait_ge(up1, n + 1)
                s.wait_ge(gelu_lo_done, n + 1)
                s.activation(gelu[:, u % 4, :], bank(u % 4), ACT.Gelu_apprx_tanh, bias=b1c[:, u:u + 1]).then_inc(gelu1, 1)

            def gelu_high(b, u):
                n = 32 * b + u
                s.wait_ge(gelu1, n + 5)
                s.wait_ge(down1, n + 1)
                s.activation(gelu_hi[:, u % 4, :], gelu[:, u % 4, :], ACT.Copy).then_inc(gelu_hi_done, 1)

            s.wait_ge(b1_out, 1)
            with s.Fori(0, B) as b:
                for u in range(32):
                    gelu_unit(b, u)
                    gelu_high(b, u)

        @block.tensor
        def _(pe):
            pe.sem_inc(pt_done, 12)
            pe.sem_inc(pv_done, 1)
            pe.sem_inc(down0, 3)
            pe.sem_inc(down1, 4)

            def t_set(k, src, ready):
                for g in range(4):
                    n = 4 * k + g
                    if n > 1:
                        pe.wait_ge(t_evac, n - 1)
                    for w in range(4 * g, 4 * g + 4):
                        ready(w)
                        ins = pe.transpose(bank(g % 2, P, lo=P * (w % 4)), src[:, w, :], ident[:, :])
                    ins.then_inc(t_done, 1)

            def ln_wait(k):
                return lambda w: pe.wait_ge(ln_out, B + W * (k - 1) + w + 1)

            def item(n):
                if n >= 4:
                    q = emptied(n - 4)
                    pe.wait_ge(prep_act if BY_ACT[n - 4] else prep_dve, q[0] if BY_ACT[n - 4] else q[1])
                return 2 + n % 4

            def have(n):
                q = emptied(n)
                pe.wait_ge(prep_act, q[0])
                if q[1]:
                    pe.wait_ge(prep_dve, q[1])

            pe.wait_ge(consts, 2)
            pe.wait_ge(in_rows, 16 * N_ROWS_DMA)
            pe.wait_ge(in_small, 16 * N_SMALL)
            pe.transpose(bank(2, NROWS), rows[:, :], ident[0:NROWS, 0:NROWS])
            pe.transpose(bank(2, E0, lo=NROWS), gate_rows[:, :], ident[0:E0, 0:E0]).then_inc(prep_done, 1)
            pe.wait_ge(in_ctx, 16)
            for b in range(B):
                ins = pe.transpose(bank(3, S, lo=S * b), cn[:, b, :], ident[0:S, 0:S])
            ins.then_inc(prep_done, 1)
            pe.wait_ge(ln_out, B)
            for b in range(B):
                ins = pe.transpose(bank(4, S, lo=S * b), cln[:, b, :], ident[0:S, 0:S])
            ins.then_inc(prep_done, 1)
            pe.wait_ge(in_wq, 16)
            for g in range(2):
                k = item(I_WQ + g)
                for q in range(4):
                    ins = pe.transpose(bank(k, P, lo=P * q), wq[:, P * (4 * g + q):P * (4 * g + q + 1)], ident[:, :])
                ins.then_inc(prep_done, 1)
            pe.wait_ge(in_wkv, 16)
            have(I_CLT)
            for q in range(16):
                k = item(I_K + q)
                pe.matmul(bank(k, B * S), wkv[:, P * q:P * q + P], clT, start=True, stop=True).then_inc(prep_done, 1)
            t_set(T_LAT, Y, ln_wait(2))
            have(I_V - 1)
            for h in range(H):
                k = item(I_A + h)
                r = slice(DH * (h % 2), DH * (h % 2) + DH)
                pe.matmul(bank(k, B * S), wqT[r, P * (h // 2):P * (h // 2) + P], kT[r, h // 2, :],
                          start=True, stop=True).then_inc(prep_done, 1)
            pe.wait_ge(in_wo, 16)
            have(I_A - 1)
            for h in range(H):
                k = item(I_BT + h)
                r = slice(DH * (h % 2), DH * (h % 2) + DH)
                pe.matmul(bank(k, B * S), wo[r, h // 2, :], vT[r, h // 2, :], start=True, stop=True).then_inc(prep_done, 1)
            have(I_B - 1)
            for b in range(B):
                for g, ks in enumerate(B_GROUPS):
                    k = item(I_B + 3 * b + g)
                    for q in ks:
                        ins = pe.transpose(bank(k, P, KC[q], P * (q % 4)), BT[:, b, P * q:P * q + KC[q]], ident[:, :])
                    ins.then_inc(prep_done, 1)
            have(N_PREP - 1)

            def scores(n, b, jj):
                pe.wait_ge(lat_slot, n + 1)
                h0 = 0
                for k, nh in enumerate(SCORE_HEADS):
                    m = 3 * jj + k
                    if jj >= 2:
                        pe.wait_ge(exp_done, 3 * n + k - 3)
                    elif m >= 4:
                        pe.wait_ge(exp_done, m - 3)
                    rhs = A[:, bass.ds(b, 1), h0 * S:(h0 + nh) * S].rearrange("p b n -> p (b n)")
                    pe.matmul(bank(2 + m % 4, nh * S), latb[:, jj % 4, :], rhs, start=True, stop=True).then_inc(score_done, 1)
                    h0 += nh

            def transpose_weights(n, j):
                pe.wait_ge(softmax_step, 4 * n + 4)
                for g, ks in enumerate(B_GROUPS):
                    pe.wait_ge(pt_free, 3 * n + g + 1)
                    for q in ks:
                        ins = pe.transpose(bank((3 * j + g) % 2, P, KC[q], P * (q % 4)),
                                           Et[:, j, P * q:P * q + KC[q]], ident[:, :])
                    ins.then_inc(pt_done, 1)

            def attention(b, last):
                for j in range(4):
                    if not (last and j > 1):
                        scores(4 * b + j + 2, b if j < 2 else b + 1, j + 2)
                    transpose_weights(4 * b + j, j)
                pe.wait_ge(b_slot, b + 1)
                pe.wait_ge(pv_free, b + 1)
                pe.wait_ge(pt_free, 2 + 3 * (4 * b + 3) + 3)
                for q, kc in enumerate(KC):
                    ins = pe.matmul(bank(6), Bs[0:kc, q, :], PT[0:kc, q, :], start=(q == 0), stop=(q == len(KC) - 1))
                ins.then_inc(pv_done, 1)

            pe.wait_ge(t_evac, 4 * T_LAT + 4)
            scores(0, 0, 0)
            scores(1, 0, 1)
            with pe.Fori(0, B - 1) as b:
                attention(b, False)
            attention(B - 1, True)
            pe.wait_ge(pv_free, 1 + B)
            t_set(T_X1, T2, lambda w: None)

            t_set(T_E0, Y, ln_wait(3))
            gwT = cols[:, NROWS:NROWS + E0]
            for w in range(W):
                if w % 4 == 0:
                    pe.wait_ge(t_evac, 4 * T_E0 + w // 4 + 1)
                ins = pe.matmul(bank(7, E0, lo=E0 * w), T1[:, w, :], gwT, start=True, stop=True)
            ins.then_inc(logits_done, 1)
            pe.wait_ge(in_fc1, 16)
            for e in range(E1):
                for f in range(4):
                    ins = pe.matmul(bank(5, 1, lo=128 + 4 * e + f), fc1[:, e, P * f:P * f + P],
                                    cols[:, COL["ln_b"] + e:COL["ln_b"] + e + 1], start=True, stop=True)
            ins.then_inc(b1_done, 1)
            pe.wait_ge(route, R_COMB0)
            for g in range(4):
                for q in range(4):
                    ins = pe.transpose(bank(2 + g if g < 3 else 1, P, E0, P * q), comb[:, 4 * g + q, :], ident[:, :])
                ins.then_inc(combT_done, 1)
            pe.wait_ge(route, R_L0)
            for g in range(2):
                for q in range(8):
                    ins = pe.transpose(combs_bank(g, 3 * E0)[:, P * q:P * q + P], combs[:, 8 * g + q, :], identb[:, :])
                ins.then_inc(combT_done, 1)
            pe.wait_ge(comb_evac, 6)
            pe.wait_ge(sel_ready, 6)
            pe.wait_ge(in_e0, 16 * 7)
            pe.wait_ge(b1_out, 1)

            def split_product(dst, w_hi, w_lo, x_hi, x_lo, start=True, stop=True, before_last=None):
                pe.matmul(dst, w_lo, x_hi, start=start, stop=False)
                pe.matmul(dst, w_hi, x_lo, start=False, stop=False)
                if before_last is not None:
                    pe.wait_ge(*before_last)
                return pe.matmul(dst, w_hi, x_hi, start=False, stop=stop)

            def up_unit0(b, u, before_last=None):
                n = 9 * b + u
                if u > 8:
                    b, u = b + 1, u - 9
                x_hi, x_lo = (q[:, bass.ds(4 * b, 4), :].rearrange("p w n -> p (w n)") for q in (x0_hi, x0_lo))
                pe.wait_ge(glu0, n + 1)
                w1_hi, w1_lo, w3_hi, w3_lo = (
                    (q[:, 2 * u - 2:2 * u, :].rearrange("p e i -> p (e i)") if u else shared[:, :])
                    for q, shared in ((we1_hi, ws1_hi), (we1_lo, ws1_lo), (we3_hi, ws3_hi), (we3_lo, ws3_lo)))
                split_product(bank(3 + u % 3), w3_hi, w3_lo, x_hi, x_lo)
                split_product(bank(u % 3), w1_hi, w1_lo, x_hi, x_lo, before_last=before_last).then_inc(up0, 1)

            def block0(b, last):
                cols_b = bass.ds(b * N, N)
                for u in range(9):
                    free = (acc0, b + 1) if u == 0 else (scaled0, 8 * b + u)
                    if not (last and u > 6):
                        up_unit0(b, u + 2, free)
                    if u == 0:
                        pe.matmul(bank(6), be2[:, :], combT[:, cols_b], start=True, stop=False)
                    if u < 8 and not (last and u > 6):
                        pe.matmul(bank(7), sel0[:, u, :], combST[:, cols_b], start=True, stop=True).then_inc(cb0, 1)
                    pe.wait_ge(glu_lo_done, 9 * b + u + 1)
                    split_product(bank(6), *((we2_hi[:, u - 1, :], we2_lo[:, u - 1, :]) if u else (ws2_hi[:, :], ws2_lo[:, :])),
                                  glu_hi[:, u % 3, :], glu_lo[:, u % 3, :], start=False, stop=(u == 8)).then_inc(down0, 1)
                    if last and u == 7:
                        pe.matmul(bank(7), sel0[:, u, :], combST[:, cols_b], start=True, stop=True).then_inc(cb0, 1)

            pe.wait_ge(w0_lo, len(SPLIT0))
            pe.wait_ge(x0_lo_done, 4)
            up_unit0(0, 0)
            up_unit0(0, 1)
            with pe.Fori(0, B - 1) as b:
                block0(b, False)
            block0(B - 1, True)
            pe.wait_ge(acc0, 1 + B)
            t_set(T_X2, T2, lambda w: None)

            pe.wait_ge(misc_act, 2)
            for b in range(B):
                ins = pe.matmul(PS[C * b:C * b + C, 5, 0:S], ones[:, :], csq[:, b, :], start=True, stop=True)
            ins.then_inc(aab_done, 1)
            t_set(T_DTW, Y, ln_wait(4))
            pe.wait_ge(t_evac, 4 * T_DTW + 4)
            for k, (lo, hi) in enumerate(COST_BANKS):
                for w in range(lo, hi):
                    for b in range(B):
                        ins = pe.matmul(PS[C * b:C * b + C, 2 + k, S * (w - lo):S * (w - lo) + S],
                                        T1[:, w, C * b:C * b + C], cT[:, b, :], start=True, stop=True)
                ins.then_inc(cost_mm, 1)

            pe.wait_ge(back, 3 * S)
            pe.wait_ge(dve_consts, 1)
            pe.transpose(bank(2, P, S), vals[:, 0:S], ident[:, :])
            pe.transpose(bank(2, P, S, P), vals[:, 1:S + 1], ident[:, :]).then_inc(vcol_done, 1)
            for b in range(B):
                pe.wait_ge(mask_done, b + 1)
                pe.matmul(bank(3 + b), cn[:, b, :], Mb[:, b, :], start=True, stop=True).then_inc(al_done, 1)
            pe.wait_ge(al_evac, B)
            t_set(T_X3, T2, lambda w: None)

            t_set(T_G1, Y, ln_wait(5))
            for w in range(W):
                if w % 4 == 0:
                    pe.wait_ge(t_evac, 4 * T_G1 + w // 4 + 1)
                ins = pe.matmul(bank(7, E1, lo=E1 * w), T1[:, w, :], wg1[:, :], start=True, stop=True)
            ins.then_inc(logits_done, 1)
            t_set(T_E1, Y2, ln_wait(6))
            pe.wait_ge(route, R_L0 + R_L1)
            for g in range(2):
                for q in range(8):
                    ins = pe.transpose(combs_bank(g, 3 * E1)[:, P * q:P * q + P], combs[:, 8 * g + q, 0:3 * E1], identb[:, :])
                ins.then_inc(combT_done, 1)
            pe.wait_ge(comb_evac, 8)
            pe.wait_ge(t_evac, 4 * T_E1 + 4)
            pe.wait_ge(fc_lo, 2 * E1)
            pe.wait_ge(x1_lo_done, 4)

            def up_unit1(b, u, before_last=None):
                n = 32 * b + u
                if u > 31:
                    b, u = b + 1, u - 32
                e, f = u // 4, slice(P * (u % 4), P * (u % 4) + P)
                x_hi, x_lo = (q[:, bass.ds(4 * b, 4), :].rearrange("p w n -> p (w n)") for q in (x1_hi, x1_lo))
                pe.wait_ge(gelu1, n + 1)
                split_product(bank(u % 4), fc1_hi[:, e, f], fc1_lo[:, e, f], x_hi, x_lo, before_last=before_last
                              ).then_inc(up1, 1)

            def block1(b, last):
                for u in range(32):
                    e, f = u // 4, u % 4
                    free = (y1_used, E1 * b + e + 1) if f == 0 else None
                    if not (last and u > 29):
                        up_unit1(b, u + 2, free)
                    if f == 0:
                        pe.matmul(bank(6 + e % 2), sel1[:, e, :], combST[0:3 * E1, bass.ds(b * N, N)],
                                  start=True, stop=True).then_inc(cb1, 1)
                    pe.wait_ge(gelu_lo_done, 32 * b + u + 5)
                    split_product(bank(4 + e % 2), fc2_hi[:, e, f, :], fc2_lo[:, e, f, :], gelu_hi[:, f, :],
                                  gelu_lo[:, f, :], start=(f == 0), stop=(f == 3)).then_inc(down1, 1)

            up_unit1(0, 0)
            up_unit1(0, 1)
            with pe.Fori(0, B - 1) as b:
                block1(b, False)
            block1(B - 1, True)
            pe.wait_ge(acc1, 7 * B)
            t_set(T_OUT, T1, lambda w: None)


_INS = ["x", "ctx_1024", "g_xattn", "g_ffn",
        "L0_xattn_ln_l_w", "L0_xattn_ln_l_b", "L0_xattn_ln_c_w", "L0_xattn_ln_c_b", "L0_xattn_Wq", "L0_xattn_Wkv",
        "L0_xattn_Wo", "L0_xattn_bo", "L0_ffn_gate_w", "L0_ffn_gate_b", "L0_ffn_We1", "L0_ffn_be1", "L0_ffn_We2",
        "L0_ffn_be2", "L0_ffn_We3", "L0_ffn_be3", "L0_ffn_ws1", "L0_ffn_bs1", "L0_ffn_ws2", "L0_ffn_bs2",
        "L0_ffn_ws3", "L0_ffn_bs3", "L1_ffn_Wg", "L1_ffn_alpha", "L1_ffn_ln_w", "L1_ffn_ln_b", "L1_ffn_fc1_w",
        "L1_ffn_fc1_b", "L1_ffn_fc2_w", "L1_ffn_fc2_b"]


def kernel(**inputs):
    import numpy as _np
    import concourse.bacc as _bacc
    from concourse import mybir as _mybir
    from concourse.bass_utils import run_bass_kernel_spmd as _run

    nc = _bacc.Bacc("TRN2", target_bir_lowering=False, num_devices=1)
    arrays, args = {}, {}
    for name in _INS:
        v = _np.ascontiguousarray(inputs[name])
        arrays[f"in_{name}"] = v
        args[name] = nc.dram_tensor(f"in_{name}", v.shape, _mybir.dt.from_np(v.dtype), kind="ExternalInput").ap()
    out = nc.dram_tensor("out_0", (B, N, D), F32, kind="ExternalOutput").ap()
    build(nc, args, out)
    r = _run(nc, [arrays], core_ids=[0])
    return r.results[0]["out_0"]
```

```python
from contextlib import ExitStack

import concourse.bass as bass
from concourse import mybir

ALU = mybir.AluOpType
ACT = mybir.ActivationFunctionType
AX = mybir.AxisListType
F32 = mybir.dt.float32
U32 = mybir.dt.uint32
F32R = mybir.dt.float32r

P = 128
B, N, D = 4, 512, 128
S = 77
W = 16
C = N // W
H, DH = 16, 64
HS = H * S
E0, F0 = 16, 64
E1, F1 = 8, 512
EPS = 1e-5
BIG = 1e30
KC = [128] * (HS // 128) + [HS % 128]
SCORE_HEADS = [6, 6, 4]
STEPS = S + C - 1
ROWW = W + 1
PADROWS = S + 2 * (C - 1)
E_HI, E_LO = 59874.14171519782, 1.670170079024566e-05
CHOICE = [(0, 32), (32, 64), (64, 92), (92, STEPS)]
R_COMB0, R_EXP1, R_L1 = 22, 6, 12
LO = 32
NROWS = 78

I_CT, I_CLT, I_K, I_V, I_WQ, I_COLS, I_A, I_BT, I_B = 0, 1, 2, 10, 18, 20, 21, 37, 53
N_PREP = I_B + 3 * B
BY_ACT = [n < I_A or n % 2 == 0 for n in range(N_PREP)]


def emptied(n):
    acts = sum(BY_ACT[:n + 1])
    return acts, n + 1 - acts


COL = {"ln_l_w": 0, "ln_l_b": 1, "bo": 2, "bs1": 3, "bs2": 4, "bs3": 5,
       "be1": 6, "be3": 14, "ln_w": 22, "ln_b": 30, "fc2_b": 38, "fc1_b": 46}


def build(nc, a, out, stage=9):
    ctx = ExitStack()
    with ctx:
        at = {}

        def sb(name, shape, dt=F32):
            at[name] = (nc.sbuf_base + 31) // 32 * 32
            return ctx.enter_context(nc.sbuf_tensor(name, shape, dt))

        def part(name, region, words, shape):
            return nc.alloc_sbuf_tensor_at(name, shape, F32R, offset=at[region] + 4 * words)

        def sem(name):
            return ctx.enter_context(nc.semaphore(name))

        X = sb("X", [P, W, D])
        Y = sb("Y", [P, W, D])
        Y2 = sb("Y2", [P, W, D])
        T1 = sb("T1", [P, W, P])
        T2 = sb("T2", [P, W, P])
        stats = sb("stats", [P, W, 6])
        lnw = sb("lnw", [P, 13, W])
        eps_col = sb("eps_col", [P, 1])
        unused = sb("unused", [P, 16])
        ident = sb("ident", [P, P])
        ones = sb("ones", [P, C])
        rows = sb("rows", [NROWS, P])
        ln_c_rows = sb("ln_c_rows", [2, P])
        ln_c = sb("ln_c", [P, 2])
        gate_rows = sb("gate_rows", [E0, P])
        cols = sb("cols", [P, NROWS + E0])
        gains = sb("gains", [P, 4])
        tg = sb("tg", [P, 4])
        bs2g = sb("bs2g", [P, 1])
        gate_b = sb("gate_b", [P, E0])
        alpha = sb("alpha", [P, E1])
        wg1 = sb("wg1", [P, E1])
        cn = sb("cn", [S, B, D])
        cln = Y2[0:S, 0:B, :]
        cT = sb("cT", [P, B, S])
        clT = Y2[:, 4:7, :].rearrange("p w d -> p (w d)")[:, 0:B * S]
        csq = sb("csq", [P, B, S])
        R1 = sb("R1", [P, 4096])
        wkv = R1[:, 0:2048]
        wq = R1[:, 2048:3072]
        wqT = R1[:, 3072:4096]
        R2 = sb("R2", [P, 2 * 8 * B * S])
        kT = R2[:, 0:8 * B * S].rearrange("p (q s) -> p q s", q=8)
        vT = R2[:, 8 * B * S:16 * B * S].rearrange("p (q s) -> p q s", q=8)
        fc1 = R2[:, 0:E1 * F1].rearrange("p (e f) -> p e f", e=E1)
        fc2 = R1[:, 0:4096].rearrange("p (e f d) -> p e f d", e=E1, f=4)
        wo = sb("wo", [P, 8, D])
        A = sb("A", [P, B, HS])
        R3 = sb("R3", [P, B * HS])
        BT = R3[:, :].rearrange("p (b n) -> p b n", b=B)
        Et = BT
        Bc = sb("Bc", [P, B, len(KC), D])
        Bs = sb("Bs", [P, len(KC), D])
        R4 = sb("R4", [P, len(KC) * N])
        PT = R4[:, :].rearrange("p (k n) -> p k n", k=len(KC))
        latb_hi = sb("latb_hi", [P, B, P], F32R)
        sums = sb("sums", [P, 2, H])
        we1 = sb("we1", [P, E0, F0])
        we3 = sb("we3", [P, E0, F0])
        we2 = sb("we2", [P, E0 // 2, D])
        be2 = sb("be2", [LO + E0, D])
        ws1 = sb("ws1", [P, D])
        ws2 = sb("ws2", [P, D])
        ws3 = sb("ws3", [P, D])
        R4o = [0]

        def r4(shape_free, dt=F32, parts=P):
            n = 1
            for q in shape_free:
                n *= q
            words = n if dt == F32 or dt == U32 else (n + 1) // 2
            v = R4[0:parts, R4o[0]:R4o[0] + words]
            R4o[0] += words
            if dt != F32:
                v = v.bitcast(dt)
            names = " ".join(f"a{k}" for k in range(len(shape_free)))
            if len(shape_free) > 1:
                v = v.rearrange(f"p ({names}) -> p {names}", **{f"a{k}": q for k, q in enumerate(shape_free)})
            return v

        pr = r4([W, E0])
        scr = r4([W, E0])
        t4 = r4([9, W * 4])
        beat = r4([W, 4, 4])
        beat2 = r4([W, 4, 4])
        top = r4([W, 8])
        topi = r4([W, 8], U32)
        topf = r4([W, 8])
        oh1 = r4([W, E0])
        oh2 = r4([W, E0])
        comb = r4([W, E0])
        small = r4([6, W])
        low = sb("low", [P, 4, 4])
        iota_e = sb("iota_e", [P, E0])
        def rounded(name, shape):
            return sb(name + "_words", shape), part(name, name + "_words", 0, shape)

        combT_words, combT = rounded("combT", [LO + E0, N * B])
        sel0_words, sel0 = rounded("sel0", [LO + E0, E0 // 2, P])
        sel1_words, sel1 = rounded("sel1", [LO + E0, E1, P])
        be2_hi_words, be2_hi = rounded("be2_hi", [LO + E0, D])
        be2_lo_words, be2_lo = rounded("be2_lo", [LO + E0, D])
        Av = A[:, :, :].rearrange("p b n -> p (b n)")
        def slots(region, lo, n):
            return region[:, lo:lo + n * N].rearrange("p (s n) -> p s n", s=n)

        silu = slots(Av, 0, 3)
        glu = slots(Av, 3 * N, 3)
        A_hi = part("A_hi", "R1", 0, [P, B, HS])
        A_lo = part("A_lo", "A", 0, [P, B, HS])
        latb_lo = part("latb_lo", "Y", 0, [P, B, P])
        latb = Y[:, B:2 * B, :]
        glu_hi = part("glu_hi", "A", 6 * N, [P, 3, N])
        glu_lo = part("glu_lo", "R4", 0, [P, 3, N])
        we1_hi = part("we1_hi", "R3", 0, [P, E0, F0])
        we3_hi = part("we3_hi", "R3", E0 * F0, [P, E0, F0])
        we2_hi = part("we2_hi", "R3", 2 * E0 * F0, [P, E0 // 2, D])
        ws1_hi, ws2_hi, ws3_hi = (part(f"ws{k + 1}_hi", "R3", 3 * E0 * F0 + k * D, [P, D]) for k in range(3))
        we1_lo, we3_lo = (part(f"{k}_lo", k, 0, [P, E0, F0]) for k in ("we1", "we3"))
        we2_lo = part("we2_lo", "we2", 0, [P, E0 // 2, D])
        ws1_lo, ws2_lo, ws3_lo = (part(f"{k}_lo", k, 0, [P, D]) for k in ("ws1", "ws2", "ws3"))
        x0_hi = part("x0_hi", "Bc", 0, [P, W, P])
        x0_lo = part("x0_lo", "Bc", W * P, [P, W, P])
        fc1_hi = part("fc1_hi", "A", 0, [P, E1, F1])
        fc2_hi = part("fc2_hi", "Bc", 0, [P, E1, 4, D])
        fc1_lo = part("fc1_lo", "R2", 0, [P, E1, F1])
        fc2_lo = part("fc2_lo", "R1", 0, [P, E1, 4, D])
        x1_hi = part("x1_hi", "Y", 0, [P, W, P])
        x1_lo = part("x1_lo", "T2", 0, [P, W, P])
        gelu = slots(R3, 0, 4)
        yt = slots(R3, 4 * N, 2)
        cbs = slots(R3, 6 * N, 2)
        gelu_hi = part("gelu_hi", "R4", 0, [P, 4, N])
        gelu_lo = part("gelu_lo", "R4", 4 * N, [P, 4, N])
        b1c = sb("b1c", [P, E1 * 4])
        R3o = [0]

        def r3(*shape_free, parts=P):
            n = 1
            for q in shape_free:
                n *= q
            v = R3[0:parts, R3o[0]:R3o[0] + n]
            R3o[0] += n
            if len(shape_free) > 1:
                names = " ".join(f"a{k}" for k in range(len(shape_free)))
                v = v.rearrange(f"p ({names}) -> p {names}", **{f"a{k}": q for k, q in enumerate(shape_free)})
            return v

        Dt = r3(S, ROWW)
        bb = r3(W)
        aab = r3(S)
        base = r3(W, S)
        Bcv = Bc[:, :, :, :].rearrange("p b k d -> p (b k d)")
        Dsk = Bcv[:, 0:STEPS * ROWW].rearrange("p (t w) -> p t w", w=ROWW)
        Rh = Bcv[:, 1900:1900 + (STEPS + 1) * (W + 2)].rearrange("p (t w) -> p t w", w=W + 2)
        MH0 = R3o[0]
        mh = r3(STEPS, ROWW)
        du = R4[:, 0:STEPS * W].rearrange("p (t w) -> p t w", w=W)
        V = R4[:, STEPS * W:2 * STEPS * W].rearrange("p (t w) -> p t w", w=W)
        Vn_flat = base.rearrange("p w i -> p (w i)")
        Vn = Vn_flat.rearrange("p (i w) -> p i w", w=W)
        first = sb("first", [P, 1])
        block_last = sb("block_last", [P, 1])
        jj1 = sb("jj1", [P, W])
        jj2 = sb("jj2", [P, W])
        jrow = sb("jrow", [S, N])
        vals = sb("vals", [P, S + 1])
        pick = sb("pick", [P, W])
        pickm = sb("pickm", [P, 1])
        run_max = sb("run_max", [P, 2, 1 + W])
        rises = sb("rises", [P, 2, W])
        vcol = sb("vcol", [S, 2, B])
        Mb = R3[0:S, MH0:MH0 + 4 * N].rearrange("p (b n) -> p b n", b=B)
        away = R4[0:S, 0:4 * N].rearrange("p (b n) -> p b n", b=B)
        span = sb("span", [S, 2, B])
        bigrow = Bcv[:, 4096:4096 + (C - 1) * ROWW]

        PS = ctx.enter_context(nc.psum_tensor("PS", [P, 8, 512], F32))

        def bank(k, n=512, parts=P, lo=0):
            return PS[0:parts, k, lo:lo + n]

        Dscr = nc.dram_tensor("Dscr", [P, PADROWS * ROWW], F32, kind="Internal").ap()
        Vscr = nc.dram_tensor("Vscr", [P, STEPS * W], F32, kind="Internal").ap()
        Dskew = bass.AP(Dscr.tensor, (C - 1) * ROWW,
                        [[C * PADROWS * ROWW, B], [(PADROWS - 1) * ROWW, C], [1, STEPS * ROWW]])
        Vskew = bass.AP(Vscr.tensor, 0, [[C * STEPS * W, B], [(STEPS + 1) * W, C], [1, S * W]])

        in_x, in_ctx, in_rows, in_wkv, in_wq, in_wo, in_small, in_e0, in_fc1, in_fc2 = map(sem, [
            "in_x", "in_ctx", "in_rows", "in_wkv", "in_wq", "in_wo", "in_small", "in_e0", "in_fc1", "in_fc2"])
        const0, consts, sel_ready, dve_consts = map(sem, ["const0", "consts", "sel_ready", "dve_consts"])
        ln_math, ln_var, ln_sqrt, ln_shift, ln_dve, ln_act = map(sem, [
            "ln_math", "ln_var", "ln_sqrt", "ln_shift", "ln_dve", "ln_act"])
        t_done, t_evac = map(sem, ["t_done", "t_evac"])
        prep_done, prep_act, prep_dve, misc_act, misc_dve = map(sem, [
            "prep_done", "prep_act", "prep_dve", "misc_act", "misc_dve"])
        lat_slot, b_slot, score_done, exp_done, softmax_step, pt_done, pt_free, pv_done, pv_free = map(sem, [
            "lat_slot", "b_slot", "score_done", "exp_done", "softmax_step", "pt_done", "pt_free", "pv_done", "pv_free"])
        logits_done, route, route_exp, combT_done, comb_hi, comb_lo = map(sem, [
            "logits_done", "route", "route_exp", "combT_done", "comb_hi", "comb_lo"])
        in_ln_c, ln_c_done, ln_c_out = map(sem, ["in_ln_c", "ln_c_done", "ln_c_out"])
        be2_split, choice_dve, last_choice = map(sem, ["be2_split", "choice_dve", "last_choice"])
        b1_done, b1_out, fc1_scaled = map(sem, ["b1_done", "b1_out", "fc1_scaled"])
        up0, silu0, glu0, cb0, scaled0, glu_hi_done, glu_lo_done, down0, acc0 = map(sem, [
            "up0", "silu0", "glu0", "cb0", "scaled0", "glu_hi_done", "glu_lo_done", "down0", "acc0"])
        A_hi_done, A_lo_done, lat_part = map(sem, ["A_hi_done", "A_lo_done", "lat_part"])
        w0_hi, w0_lo, x0_lo_done = map(sem, ["w0_hi", "w0_lo", "x0_lo_done"])
        fc_hi, fc_lo, x1_lo_done = map(sem, ["fc_hi", "fc_lo", "x1_lo_done"])
        aab_done, cost_mm, cost_step, cost_sqrt, sq_done = map(sem, [
            "aab_done", "cost_mm", "cost_step", "cost_sqrt", "sq_done"])
        choice_pool, al_used, vcol_out, away_done = map(sem, [
            "choice_pool", "al_used", "vcol_out", "away_done"])
        d_stored, d_loaded, v_stored, v_loaded = map(sem, ["d_stored", "d_loaded", "v_stored", "v_loaded"])
        dtw_init, row_done, pre_done, choice = map(sem, ["dtw_init", "row_done", "pre_done", "choice"])
        back, rises_step, vcol_done, mask_done, al_done = map(sem, ["back", "rises_step", "vcol_done", "mask_done", "al_done"])
        up1, gelu1, cb1, cbs1, gelu_hi_done, gelu_lo_done, down1, y1_used, acc1 = map(sem, [
            "up1", "gelu1", "cb1", "cbs1", "gelu_hi_done", "gelu_lo_done", "down1", "y1_used", "acc1"])
        stored = sem("stored")

        T_LAT, T_X1, T_E0, T_X2, T_DTW, T_G1, T_E1, T_OUT = range(8)

        block = ctx.enter_context(nc.Block())

        xv = a["x"].rearrange("b (c w) d -> (b c) w d", w=W)
        ov = out.rearrange("b (c w) d -> (b c) w d", w=W)

        N_ROWS_DMA = len(COL) + 1
        N_SMALL = 5
        N_CONSTS = 1 + 4 * B + 3

        COST_BANKS = [(0, 6), (6, 12), (12, 16)]
        B_GROUPS = [range(0, 4), range(4, 8), range(8, 10)]
        PT_BANKS = [0, 1, 7]

        COMB_BANKS = [2, 5, 6, 7]

        LN_CTX, LN_LAT, LN_E0, LN_DTW, LN_G1 = range(5)

        LN_BY_ACT = [w for w in range(W) if w % 3 == 1]
        LN_BY_DVE = [w for w in range(W) if w % 3 != 1]

        def ln_wait(eng, k, w=W - 1):
            if k == LN_LAT:
                eng.wait_ge(ln_dve, B + w + 1)
                return
            eng.wait_ge(ln_dve, B + W + len(LN_BY_DVE) * (k - LN_E0) + sum(q <= w for q in LN_BY_DVE))
            if w > 0:
                eng.wait_ge(ln_act, len(LN_BY_ACT) * (k - LN_E0) + sum(q <= w for q in LN_BY_ACT))

        SPLIT0 = [(w[:, :], w_hi[:, :], w_lo[:, :])
                  for w, w_hi, w_lo in ((ws1, ws1_hi, ws1_lo), (ws3, ws3_hi, ws3_lo), (ws2, ws2_hi, ws2_lo))]
        SPLIT0 += [(w[:, :, :], w_hi[:, :, :], w_lo[:, :, :])
                   for w, w_hi, w_lo in ((we1, we1_hi, we1_lo), (we3, we3_hi, we3_lo), (we2, we2_hi, we2_lo))]

        def prep_out(n, copy):
            k = 2 + n % 4
            if n == I_COLS:
                copy(cols[:, 0:NROWS], bank(k, NROWS))
                return copy(cols[:, NROWS:NROWS + E0], bank(k, E0, lo=NROWS))
            if n == I_CT:
                return copy(cT[:, :, :], bank(k, B * S).rearrange("p (b s) -> p b s", b=B))
            if n >= I_WQ and n < I_COLS:
                return copy(wqT[:, 512 * (n - I_WQ):512 * (n - I_WQ) + 512], bank(k))
            if n < I_V:
                return copy(kT[:, n - I_K, :], bank(k, B * S))
            if n < I_A:
                return copy(vT[:, n - I_V, :], bank(k, B * S))
            if n < I_B:
                dst, h = (A, n - I_A) if n < I_BT else (BT, n - I_BT)
                return copy(dst[:, :, S * h:S * h + S], bank(k, B * S).rearrange("p (b s) -> p b s", b=B))
            b, g = (n - I_B) // 3, (n - I_B) % 3
            src = PS[:, k, :].rearrange("p (k d) -> p k d", k=4)
            if g < 2:
                return copy(Bc[:, b, 4 * g:4 * g + 4, :], src)
            copy(Bc[:, b, 8, :], src[:, 0, :])
            return copy(Bc[0:KC[9], b, 9, :], src[0:KC[9], 1, :])

        def choices(eng, n, step, k, done):
            lo, hi = CHOICE[n]
            r = slice(lo, hi)
            eng.wait_ge(row_done, hi)
            eng.tensor_tensor(du[:, r, :], Rh[:, r, 1:1 + W], Rh[:, r, 0:W], ALU.subtract).then_inc(step, 1)
            eng.tensor_tensor(V[:, r, :], Rh[:, lo + 1:hi + 1, 0:W], mh[:, r, 0:W], ALU.subtract).then_inc(step, 1)
            eng.wait_ge(step, k + 2)
            eng.tensor_scalar(du[:, r, :], du[:, r, :], 0.0, None, ALU.is_lt).then_inc(step, 1)
            eng.tensor_scalar(V[:, r, :], V[:, r, :], 0.0, None, ALU.is_ge).then_inc(step, 1)
            eng.wait_ge(step, k + 4)
            eng.tensor_tensor(du[:, r, :], du[:, r, :], jj1[:, :].unsqueeze(1).to_broadcast([P, hi - lo, W]),
                              ALU.add).then_inc(step, 1)
            eng.wait_ge(step, k + 5)
            eng.tensor_tensor(V[:, r, :], V[:, r, :], du[:, r, :], ALU.mult).then_inc(done, 1)

        @block.sync
        def _(sp):
            sp.dma_start(cn[:, :, :], a["ctx_1024"].rearrange("b s d -> s b d")).then_inc(in_ctx, 16)
            for k, name in enumerate(("L0_xattn_ln_c_w", "L0_xattn_ln_c_b")):
                sp.dma_start(ln_c_rows[k:k + 1, :], a[name].rearrange("(o d) -> o d", o=1)).then_inc(in_ln_c, 16)
            sp.dma_start(wq, a["L0_xattn_Wq"]).then_inc(in_wq, 16)
            for name, src, n in (("ln_l_w", "L0_xattn_ln_l_w", 0), ("ln_l_b", "L0_xattn_ln_l_b", 0),
                                 ("bo", "L0_xattn_bo", 0), ("bs1", "L0_ffn_bs1", 0), ("bs2", "L0_ffn_bs2", 0),
                                 ("bs3", "L0_ffn_bs3", 0), ("be1", "L0_ffn_be1", 8), ("be3", "L0_ffn_be3", 8),
                                 ("ln_w", "L1_ffn_ln_w", 8), ("ln_b", "L1_ffn_ln_b", 8),
                                 ("fc2_b", "L1_ffn_fc2_b", 8), ("fc1_b", "L1_ffn_fc1_b", 32)):
                v = a[src]
                if n == 0:
                    v = v.rearrange("(o d) -> o d", o=1)
                elif name in ("be1", "be3"):
                    v = v.rearrange("(q e) i -> q (e i)", e=2)
                elif name == "fc1_b":
                    v = v.rearrange("e (f i) -> (e f) i", i=P)
                sp.dma_start(rows[COL[name]:COL[name] + max(n, 1), :], v).then_inc(in_rows, 16)
            sp.dma_start(gate_rows[:, :], a["L0_ffn_gate_w"]).then_inc(in_rows, 16)
            sp.dma_start(gains[:, 0:2], a["g_xattn"].partition_broadcast(P)).then_inc(in_small, 16)
            sp.dma_start(gains[:, 2:4], a["g_ffn"].partition_broadcast(P)).then_inc(in_small, 16)
            sp.dma_start(gate_b[:, :], a["L0_ffn_gate_b"].partition_broadcast(P)).then_inc(in_small, 16)
            sp.dma_start(alpha[:, :], a["L1_ffn_alpha"].partition_broadcast(P)).then_inc(in_small, 16)
            sp.dma_start(wg1[:, :], a["L1_ffn_Wg"]).then_inc(in_small, 16)
            sp.dma_start(we1[:, :, :], a["L0_ffn_We1"].rearrange("e d i -> d e i")).then_inc(in_e0, 16)
            sp.dma_start(we3[:, :, :], a["L0_ffn_We3"].rearrange("e d i -> d e i")).then_inc(in_e0, 16)
            sp.dma_start(we2[:, :, :], a["L0_ffn_We2"].rearrange("(q e) i d -> (e i) q d", e=2)).then_inc(in_e0, 16)
            for k in (0, LO):
                sp.dma_start(be2[k:k + E0, :], a["L0_ffn_be2"]).then_inc(in_e0, 16)
            sp.dma_start(ws1[:, :], a["L0_ffn_ws1"]).then_inc(in_e0, 16)
            sp.dma_start(ws2[:, :], a["L0_ffn_ws2"]).then_inc(in_e0, 16)
            sp.dma_start(ws3[:, :], a["L0_ffn_ws3"]).then_inc(in_e0, 16)
            sp.wait_ge(score_done, 3 * 4 * B)
            sp.dma_start(fc1, a["L1_ffn_fc1_w"].rearrange("e d f -> d e f")).then_inc(in_fc1, 16)
            sp.dma_start(fc2, a["L1_ffn_fc2_w"].rearrange("e (f i) d -> i e f d", i=P)).then_inc(in_fc2, 16)
            sp.wait_ge(dtw_init, 1)
            sp.dma_start(Dscr[:, 0:(C - 1) * ROWW], bigrow).then_inc(d_stored, 16)
            sp.dma_start(Dscr[:, (C - 1 + S) * ROWW:PADROWS * ROWW], bigrow).then_inc(d_stored, 16)
            sp.wait_ge(cost_sqrt, 1)
            sp.dma_start(Dscr[:, (C - 1) * ROWW:(C - 1 + S) * ROWW],
                         Dt.rearrange("p t w -> p (t w)")).then_inc(d_stored, 16)
            sp.wait_ge(d_stored, 48)
            sp.dma_start(Dsk.rearrange("p t w -> p (t w)"), Dskew).then_inc(d_loaded, 16)
            for n, (lo, hi) in enumerate(CHOICE):
                if n < len(CHOICE) - 1:
                    sp.wait_ge(choice, n + 1)
                else:
                    sp.wait_ge(last_choice, 1)
                sp.dma_start(Vscr[:, lo * W:hi * W], V[:, lo:hi, :].rearrange("p t w -> p (t w)")).then_inc(v_stored, 16)
            sp.wait_ge(v_stored, 16 * len(CHOICE))
            sp.dma_start(Vn_flat, Vskew).then_inc(v_loaded, 16)
            for g in range(4):
                sp.wait_ge(t_evac, 4 * T_OUT + g + 1)
                sp.dma_start(ov[:, 4 * g:4 * g + 4, :], X[:, 4 * g:4 * g + 4, :]).then_inc(stored, 16)
            sp.wait_ge(stored, 64)

        @block.gpsimd
        def _(g):
            g.memset(ident[:, :], 0.0).then_inc(const0, 1)
            g.memset(eps_col[:, :], EPS).then_inc(const0, 1)
            g.memset(ones[:, :], 1.0).then_inc(const0, 1)
            g.wait_ge(const0, 1)
            g.affine_select(out=ident[:, :], in_=ident[:, :], compare_op=ALU.not_equal, fill=1.0, base=0,
                            pattern=[[-1, P]], channel_multiplier=1).then_inc(consts, 1)
            g.memset(first[:, :], BIG).then_inc(const0, 1)
            g.memset(block_last[:, :], 0.0).then_inc(const0, 1)
            g.memset(sel0_words[:, :, :], 0.0).then_inc(const0, 1)
            g.memset(sel1_words[:, :, :], 0.0).then_inc(const0, 1)
            g.memset(low[:, :, :], 1.0).then_inc(const0, 1)
            g.memset(Bc[:, :, len(KC) - 1, :], 0.0).then_inc(const0, 1)
            g.memset(combT_words[:, :], 0.0).then_inc(const0, 1)
            g.memset(be2_hi_words[:, :], 0.0).then_inc(const0, 1)
            g.memset(be2_lo_words[:, :], 0.0).then_inc(const0, 1)
            g.wait_ge(const0, 12)
            for b in range(B):
                q = slice(C * b, C * b + C)
                g.wait_ge(consts, 1 + 4 * b)
                g.affine_select(out=first[q, :], in_=first[q, :], compare_op=ALU.not_equal, fill=0.0, base=0,
                                pattern=[[0, 1]], channel_multiplier=1).then_inc(consts, 1)
                g.wait_ge(consts, 2 + 4 * b)
                g.affine_select(out=block_last[q, :], in_=block_last[q, :], compare_op=ALU.not_equal, fill=BIG,
                                base=-(C - 1), pattern=[[0, 1]], channel_multiplier=1).then_inc(consts, 1)
                g.wait_ge(consts, 3 + 4 * b)
                g.iota(jj1[q, :], pattern=[[2, W]], base=1, channel_multiplier=2 * W,
                       allow_small_or_imprecise_dtypes=True).then_inc(consts, 1)
                g.wait_ge(consts, 4 + 4 * b)
                g.iota(jj2[q, :], pattern=[[2, W]], base=2, channel_multiplier=2 * W,
                       allow_small_or_imprecise_dtypes=True).then_inc(consts, 1)
            g.wait_ge(consts, 1 + 4 * B)
            g.iota(jrow[:, :], pattern=[[4, N]], base=4, channel_multiplier=0,
                   allow_small_or_imprecise_dtypes=True).then_inc(consts, 1)
            g.iota(iota_e[:, :], pattern=[[1, E0]], base=0, channel_multiplier=0,
                   allow_small_or_imprecise_dtypes=True).then_inc(consts, 1)
            g.affine_select(out=low[:, :, :], in_=low[:, :, :], compare_op=ALU.is_gt, fill=0.0, base=0,
                            pattern=[[1, 4], [-1, 4]], channel_multiplier=0).then_inc(consts, 1)
            for k in range(2):
                v = sel0_words[:, :, :].rearrange("k q (e i) -> k q e i", e=2)
                if k:
                    g.wait_ge(sel_ready, 2)
                g.affine_select(out=v, in_=v, compare_op=ALU.not_equal, fill=1.0, base=-LO * k,
                                pattern=[[-2, E0 // 2], [-1, 2], [0, F0]], channel_multiplier=1).then_inc(sel_ready, 1)
                g.affine_select(out=sel1_words[:, :, :], in_=sel1_words[:, :, :], compare_op=ALU.not_equal, fill=1.0,
                                base=-LO * k, pattern=[[-1, E1], [0, P]], channel_multiplier=1).then_inc(sel_ready, 1)


            def lat_copy(n, b, j):
                tokens = T1[:, 4 * j:4 * j + 4, bass.ds(b * C, C)]
                for into in (latb, latb_hi):
                    g.tensor_copy(into[:, j, :].rearrange("p (w c) -> p w c", c=C), tokens).then_inc(lat_part, 1)
                g.wait_ge(lat_part, 2 * n + 2)
                g.tensor_tensor(latb_lo[:, j, :], latb[:, j, :], latb_hi[:, j, :].bitcast(F32), ALU.subtract
                                ).then_inc(lat_slot, 1)

            def lat_step(n, b, j):
                g.wait_ge(score_done, 3 * (n - 3))
                lat_copy(n, b, j)

            def A_low(b):
                g.wait_ge(A_hi_done, b + 1)
                g.tensor_tensor(A_lo[:, b, :], A[:, b, :], A_hi[:, b, :].bitcast(F32), ALU.subtract).then_inc(A_lo_done, 1)

            for j in range(4):
                g.wait_ge(t_evac, 4 * T_LAT + max(j + 1, 2))
                lat_copy(j, 0, j)
            for b in range(B):
                A_low(b)
            for j in range(3):
                lat_step(4 + j, 1, j)
            g.wait_ge(prep_act, emptied(N_PREP - 1)[0])
            g.wait_ge(prep_dve, emptied(N_PREP - 1)[1])
            g.tensor_copy(Bs[:, :, :], Bc[:, 0, :, :]).then_inc(b_slot, 1)
            g.wait_ge(sel_ready, 4)
            for words, as_f32r in ((sel0_words, sel0), (sel1_words, sel1)):
                g.tensor_copy(as_f32r[:, :, :], words[:, :, :]).then_inc(sel_ready, 1)
            with g.Fori(0, B - 2) as b:
                lat_step(4 * b + 7, b + 1, 3)
                for j in range(3):
                    lat_step(4 * b + 8 + j, b + 2, j)
                g.wait_ge(pv_done, b + 2)
                g.tensor_copy(Bs[:, :, :], Bc[:, bass.ds(b + 1, 1), :, :].rearrange("p a k d -> p (a k) d")
                              ).then_inc(b_slot, 1)
            lat_step(4 * B - 1, B - 1, 3)
            for words, as_f32r in ((combT_words, combT), (be2_hi_words, be2_hi), (be2_lo_words, be2_lo)):
                g.tensor_copy(as_f32r[:, :], words[:, :]).then_inc(sel_ready, 1)
            g.wait_ge(pv_done, B)
            g.tensor_copy(Bs[:, :, :], Bc[:, B - 1, :, :]).then_inc(b_slot, 1)
            for n, (w, w_hi, w_lo) in enumerate(SPLIT0):
                g.wait_ge(w0_hi, n + 1)
                g.tensor_tensor(w_lo, w, w_hi.bitcast(F32), ALU.subtract).then_inc(w0_lo, 1)
            for k in range(4):
                r = slice(4 * k, 4 * k + 4)
                g.wait_ge(t_evac, 4 * T_E0 + k + 1)
                g.tensor_tensor(x0_lo[:, r, :], T1[:, r, :], x0_hi[:, r, :].bitcast(F32), ALU.subtract).then_inc(x0_lo_done, 1)
            g.wait_ge(be2_split, 2)
            g.wait_ge(sel_ready, 9)
            g.tensor_tensor(be2_lo[0:E0, :], be2[0:E0, :], be2_hi[0:E0, :].bitcast(F32), ALU.subtract).then_inc(be2_split, 1)
            g.wait_ge(b1_done, 1)
            for e in range(E1):
                g.tensor_scalar(fc1[:, e, :], fc1[:, e, :], cols[:, COL["ln_w"] + e:COL["ln_w"] + e + 1], 1.0,
                                ALU.mult, ALU.mult).then_inc(fc1_scaled, 1)

            for n in range(len(CHOICE) - 1):
                choices(g, n, choice_pool, 5 * n, choice)
            for e in range(E1):
                g.wait_ge(fc_hi, e + 1)
                g.tensor_tensor(fc1_lo[:, e, :], fc1[:, e, :], fc1_hi[:, e, :].bitcast(F32), ALU.subtract).then_inc(fc_lo, 1)
            for e in range(E1):
                g.wait_ge(fc_hi, E1 + e + 1)
                g.tensor_tensor(fc2_lo[:, e, :, :], fc2[:, e, :, :], fc2_hi[:, e, :, :].bitcast(F32),
                                ALU.subtract).then_inc(fc_lo, 1)
            for k in range(4):
                r = slice(4 * k, 4 * k + 4)
                g.wait_ge(t_evac, 4 * T_E1 + k + 1)
                g.tensor_tensor(x1_lo[:, r, :], T2[:, r, :], x1_hi[:, r, :].bitcast(F32), ALU.subtract).then_inc(x1_lo_done, 1)

        @block.vector
        def _(v):
            v.memset(vals[:, S:S + 1], 2.0 * N).then_inc(dve_consts, 1)
            v.memset(run_max[:, :, 0:1], 0.0).then_inc(dve_consts, 1)
            v.sem_inc(pv_free, 1)
            v.sem_inc(glu0, 3)
            v.sem_inc(gelu_lo_done, 4)
            v.sem_inc(y1_used, 2)

            def col(name, k=0):
                return cols[:, COL[name] + k:COL[name] + k + 1]

            m = [0]

            def ln_step(ins):
                ins.then_inc(ln_math, 1)
                m[0] += 1

            def ln_so_far():
                v.wait_ge(ln_math, m[0])

            def ln_statistics(k, src, n, ready, forms, parts=P):
                for w in range(n):
                    ready(w)
                    ins = v.bn_stats(stats[0:parts, w, :], src[:, w, :])
                ln_step(ins)
                ln_so_far()
                q = lnw[0:parts, :, 0:n]
                st = stats[0:parts, 0:n, :]
                v.tensor_tensor(q[:, 1, :], st[:, :, 1], st[:, :, 4], ALU.subtract)
                v.tensor_tensor(q[:, 0, :], st[:, :, 1], st[:, :, 4], ALU.add)
                ln_step(v.tensor_tensor(q[:, 2, :], st[:, :, 2], st[:, :, 5], ALU.add))
                ln_so_far()
                ln_step(v.scalar_tensor_tensor(out=q[:, 4, :], in0=q[:, 1, :], scalar=0.25, in1=q[:, 1, :],
                                               op0=ALU.mult, op1=ALU.mult))
                v.tensor_scalar(q[:, 3, :], q[:, 0, :], 0.5, None, ALU.mult)
                ln_so_far()
                ln_step(v.scalar_tensor_tensor(out=q[:, 5, :], in0=q[:, 2, :], scalar=1.0 / D, in1=q[:, 4, :],
                                               op0=ALU.mult, op1=ALU.add))
                ln_so_far()
                f = len(forms)
                for i, (scale, shift) in enumerate(forms):
                    ins = v.tensor_scalar(q[:, 6 + i, :], q[:, 5, :], scale, shift, ALU.mult, ALU.add)
                ins.then_inc(ln_var, 1)
                var, root, rstd = q[:, 6:6 + f, :], q[:, 8:8 + f, :], q[:, 10:10 + f, :]
                v.wait_ge(ln_sqrt, k + 1)
                ln_step(v.reciprocal(rstd, root))
                ln_so_far()
                ln_step(v.scalar_tensor_tensor(out=root, in0=rstd, scalar=-0.5, in1=var, op0=ALU.mult, op1=ALU.mult))
                ln_so_far()
                ln_step(v.tensor_tensor(root, root, rstd, ALU.mult))
                ln_so_far()
                ln_step(v.scalar_tensor_tensor(out=rstd, in0=root, scalar=1.5, in1=rstd, op0=ALU.add, op1=ALU.mult))
                ln_so_far()

            def ln_apply(src, dst, ws, i=0, parts=P):
                if ws is LN_BY_DVE:
                    v.scalar_tensor_tensor(out=lnw[:, 12, :], in0=lnw[:, 3, :], scalar=-1.0, in1=lnw[:, 10, :],
                                           op0=ALU.mult, op1=ALU.mult).then_inc(ln_shift, 1)
                for w in ws:
                    v.tensor_scalar(dst[:, w, :], src[:, w, :], lnw[0:parts, 3, w:w + 1],
                                    lnw[0:parts, 10 + i, w:w + 1], ALU.subtract, ALU.mult).then_inc(ln_dve, 1)

            ONE_NORM = [(1.0, EPS)]
            TWO_NORMS = [(1.0 + EPS, EPS * EPS)]

            def add_back(k):
                for g in range(4):
                    v.wait_ge(t_done, 4 * k + g + 1)
                    x4 = X[:, 4 * g:4 * g + 4, :]
                    v.tensor_tensor(x4, bank(g % 2).rearrange("p (w d) -> p w d", w=4), x4, ALU.add).then_inc(t_evac, 1)

            v.wait_ge(in_ctx, 16)
            ln_statistics(LN_CTX, cn[:, :, :], B, lambda w: None, ONE_NORM, S)
            ln_apply(cn[:, :, :], cln, range(B), parts=S)
            v.wait_ge(in_x, 16)
            ln_statistics(LN_LAT, X, W, lambda w: None, TWO_NORMS)
            ln_apply(X, Y, range(W))
            v.wait_ge(prep_act, I_COLS + 1)
            for g in range(4):
                v.wait_ge(t_done, 4 * T_LAT + g + 1)
                v.tensor_scalar(T1[:, 4 * g:4 * g + 4, :], bank(g % 2).rearrange("p (w n) -> p w n", w=4),
                                col("ln_l_w"), col("ln_l_b"), ALU.mult, ALU.add).then_inc(t_evac, 1)
            for n in range(I_A, N_PREP):
                if not BY_ACT[n]:
                    v.wait_ge(prep_done, n + 1)
                    prep_out(n, lambda o, i: v.tensor_copy(o, i)).then_inc(prep_dve, 1)
            v.wait_ge(misc_act, 2)
            v.tensor_tensor(bs2g[:, :], col("bs2"), tg[:, 2:3], ALU.mult).then_inc(misc_dve, 1)

            def softmax(n, j):
                e = Et[:, j, :]
                eh = e.rearrange("p (h s) -> p h s", h=H)
                v.wait_ge(exp_done, 3 * n + 3)
                v.tensor_scalar(e, e, E_HI, E_LO, ALU.min, ALU.max).then_inc(softmax_step, 1)
                v.wait_ge(softmax_step, 4 * n + 1)
                v.tensor_reduce(sums[:, 0, :], eh, AX.X, ALU.add).then_inc(softmax_step, 1)
                v.wait_ge(softmax_step, 4 * n + 2)
                v.reciprocal(sums[:, 1, :], sums[:, 0, :]).then_inc(softmax_step, 1)
                v.wait_ge(softmax_step, 4 * n + 3)
                v.tensor_tensor(eh, eh, sums[:, 1, :].unsqueeze(2).to_broadcast([P, H, S]), ALU.mult
                                ).then_inc(softmax_step, 1)

            def attention(b, last):
                softmax(4 * b + 2, 2)
                softmax(4 * b + 3, 3)
                if not last:
                    softmax(4 * b + 4, 0)
                    softmax(4 * b + 5, 1)
                v.wait_ge(pv_done, b + 2)
                v.tensor_scalar(T2[:, :, bass.ds(b * C, C)], bank(6).rearrange("p (w c) -> p w c", w=W),
                                col("bo"), tg[:, 0:1], ALU.add, ALU.mult).then_inc(pv_free, 1)

            softmax(0, 0)
            softmax(1, 1)
            with v.Fori(0, B - 1) as b:
                attention(b, False)
            attention(B - 1, True)
            add_back(T_X1)

            ln_statistics(LN_E0, X, W, lambda w: v.wait_ge(t_evac, 4 * T_X1 + w // 4 + 1), ONE_NORM)
            ln_apply(X, Y, LN_BY_DVE)
            r = [0]

            def did(ins):
                ins.then_inc(route, 1)
                r[0] += 1

            def so_far():
                v.wait_ge(route, r[0])

            def per_token(x, n):
                return x.unsqueeze(2).to_broadcast([P, W, n])

            def top_two(values, n):
                for w in range(W):
                    ins = v.max(top[:, w, :], values[:, w, :])
                did(ins)
                so_far()
                for w in range(W):
                    ins = v.max_index(topi[:, w, :], top[:, w, :], values[:, w, :])
                did(ins)
                so_far()
                did(v.tensor_copy(topf, topi))
                so_far()
                ie = iota_e[:, 0:n].unsqueeze(1).to_broadcast([P, W, n])
                v.tensor_tensor(oh1[:, :, 0:n], ie, per_token(topf[:, :, 0], n), ALU.is_equal)
                did(v.tensor_tensor(oh2[:, :, 0:n], ie, per_token(topf[:, :, 1], n), ALU.is_equal))
                so_far()

            def comb_low(layer, n):
                for g, k in enumerate(COMB_BANKS):
                    v.wait_ge(comb_hi, 4 * layer + g + 1)
                    r = slice(N * g, N * g + N)
                    v.tensor_tensor(combT[LO:LO + n, r], bank(k, parts=n), combT[0:n, r].bitcast(F32), ALU.subtract
                                    ).then_inc(comb_lo, 1)

            v.wait_ge(consts, N_CONSTS)
            v.wait_ge(in_small, 16 * N_SMALL)
            v.wait_ge(logits_done, 1)
            lg = bank(7, W * E0).rearrange("p (w e) -> p w e", w=W)
            did(v.tensor_reduce(small[:, 0, :], lg, AX.X, ALU.max))
            so_far()
            did(v.tensor_tensor(scr, lg, per_token(small[:, 0, :], E0), ALU.subtract))
            v.wait_ge(route_exp, 1)
            did(v.tensor_reduce(small[:, 1, :], pr, AX.X, ALU.add))
            so_far()
            did(v.reciprocal(small[:, 2, :], small[:, 1, :]))
            so_far()
            did(v.tensor_tensor(pr, pr, per_token(small[:, 2, :], E0), ALU.mult))
            so_far()
            did(v.tensor_tensor(scr, pr, gate_b[:, :].unsqueeze(1).to_broadcast([P, W, E0]), ALU.add))
            so_far()
            q4 = scr.rearrange("p w (g k) -> p (w g) k", k=4)
            hi1, lo1, hi2, lo2, m1, mlo, mhi, m2, gs = (t4[:, k, :] for k in range(9))
            v.tensor_tensor(hi1, q4[:, :, 0], q4[:, :, 1], ALU.max)
            v.tensor_tensor(lo1, q4[:, :, 0], q4[:, :, 1], ALU.min)
            v.tensor_tensor(hi2, q4[:, :, 2], q4[:, :, 3], ALU.max)
            did(v.tensor_tensor(lo2, q4[:, :, 2], q4[:, :, 3], ALU.min))
            so_far()
            v.tensor_tensor(m1, hi1, hi2, ALU.max)
            v.tensor_tensor(mlo, hi1, hi2, ALU.min)
            did(v.tensor_tensor(mhi, lo1, lo2, ALU.max))
            so_far()
            did(v.tensor_tensor(m2, mlo, mhi, ALU.max))
            so_far()
            did(v.tensor_tensor(gs, m1, m2, ALU.add))
            so_far()
            gw = gs.rearrange("p (w g) -> p w g", g=4)
            mine = gw.unsqueeze(3).to_broadcast([P, W, 4, 4])
            other = gw.unsqueeze(2).to_broadcast([P, W, 4, 4])
            v.tensor_tensor(beat, other, mine, ALU.is_gt)
            did(v.tensor_tensor(beat2, other, mine, ALU.is_equal))
            so_far()
            did(v.tensor_tensor(beat2, beat2, low[:, :, :].unsqueeze(1).to_broadcast([P, W, 4, 4]), ALU.mult))
            so_far()
            did(v.tensor_tensor(beat, beat, beat2, ALU.add))
            so_far()
            did(v.tensor_reduce(hi1, beat.rearrange("p w g o -> p (w g) o"), AX.X, ALU.add))
            so_far()
            did(v.tensor_scalar(lo1, hi1, 2.0, -BIG, ALU.is_ge, ALU.mult))
            so_far()
            did(v.tensor_tensor(q4, q4, lo1.unsqueeze(2).to_broadcast([P, W * 4, 4]), ALU.add))
            so_far()
            top_two(scr, E0)
            did(v.tensor_tensor(oh1, oh1, oh2, ALU.add))
            so_far()
            did(v.tensor_tensor(comb, oh1, pr, ALU.mult))
            comb_low(0, E0)

            def glu_unit(b, u):
                n = 9 * b + u
                u = u % 9
                v.wait_ge(silu0, n + 1)
                v.scalar_tensor_tensor(out=glu[:, u % 3, :], in0=bank(3 + u % 3),
                                       scalar=col("be3", u - 1) if u else col("bs3"), in1=silu[:, u % 3, :],
                                       op0=ALU.add, op1=ALU.mult).then_inc(glu0, 1)

            def block0(b, last):
                for u in range(9):
                    if u:
                        v.wait_ge(cb0, 8 * b + u)
                        v.wait_ge(glu0, 9 * b + u + 4)
                        v.tensor_tensor(glu[:, u % 3, :], glu[:, u % 3, :], bank(7), ALU.mult).then_inc(scaled0, 1)
                    if not (last and u == 8):
                        glu_unit(b, u + 1)
                    v.wait_ge(glu_hi_done, 9 * b + u + 1)
                    v.tensor_tensor(glu_lo[:, u % 3, :], glu[:, u % 3, :], glu_hi[:, u % 3, :].bitcast(F32),
                                    ALU.subtract).then_inc(glu_lo_done, 1)

            glu_unit(0, 0)
            with v.Fori(0, B - 1) as b:
                block0(b, False)
            block0(B - 1, True)
            add_back(T_X2)
            v.memset(mh[:, :, W:ROWW], BIG)
            v.memset(Rh[:, 0, :], BIG)
            v.memset(Rh[:, 1, 0:1], BIG)
            v.memset(bigrow, BIG).then_inc(dtw_init, 1)

            ln_statistics(LN_DTW, X, W, lambda w: v.wait_ge(t_evac, 4 * T_X2 + w // 4 + 1), ONE_NORM)
            ln_apply(X, Y, LN_BY_DVE)
            v.wait_ge(aab_done, 1)
            v.tensor_copy(aab, bank(5, S)).then_inc(cost_step, 1)
            v.wait_ge(sq_done, 1)
            v.tensor_reduce(bb, Y2[:, :, :], AX.X, ALU.add).then_inc(cost_step, 1)
            v.wait_ge(cost_step, 2)
            v.tensor_tensor(base, aab.unsqueeze(1).to_broadcast([P, W, S]), bb.unsqueeze(2).to_broadcast([P, W, S]),
                            ALU.add).then_inc(cost_step, 1)
            v.wait_ge(cost_step, 3)
            v.tensor_copy(Dt[:, :, W:ROWW], block_last[:, :].unsqueeze(1).to_broadcast([P, S, 1]))
            for k, (lo, hi) in enumerate(COST_BANKS):
                v.wait_ge(cost_mm, k + 1)
                v.scalar_tensor_tensor(out=Dt[:, :, lo:hi].rearrange("p i w -> p w i"),
                                       in0=bank(2 + k, (hi - lo) * S).rearrange("p (w i) -> p w i", i=S), scalar=-2.0,
                                       in1=base[:, lo:hi, :], op0=ALU.mult, op1=ALU.add).then_inc(cost_step, 1)
            v.wait_ge(cost_step, 6)
            v.tensor_scalar(Dt[:, :, 0:W], Dt[:, :, 0:W], 0.0, None, ALU.max).then_inc(cost_step, 1)

            v.wait_ge(dve_consts, 2)
            v.wait_ge(dtw_init, 1)
            v.wait_ge(d_loaded, 16)
            shift = [C - 1] + list(range(C - 1))
            for t in range(STEPS):
                if t:
                    v.wait_ge(row_done, t)
                    v.stream_shuffle(Rh[:, t + 1, 0:1], Rh[:, t, W + 1:W + 2], shift)
                v.tensor_tensor(mh[:, t, 0:W], Rh[:, t, 1:1 + W], Rh[:, t, 0:W], ALU.min).then_inc(pre_done, 1)
                v.wait_ge(pre_done, t + 1)
                v.tensor_tensor_scan(Rh[:, t + 1, 1:2 + W], mh[:, t, :], Dsk[:, t, :],
                                     Rh[:, t + 1, 0:1] if t else first[:, :], ALU.min, ALU.add).then_inc(row_done, 1)

            choices(v, len(CHOICE) - 1, choice_dve, 0, last_choice)
            v.wait_ge(b1_done, 1)
            v.tensor_tensor(b1c[:, :], bank(7, 32), cols[:, COL["fc1_b"]:COL["fc1_b"] + 32], ALU.add
                            ).then_inc(b1_out, 1)

            v.wait_ge(v_loaded, 16)
            def running_max(n):
                vn = Vn[:, S - 1 - n, :]
                v.tensor_tensor_scan(run_max[:, n % 2, 1:1 + W], vn, vn, 0.0, ALU.max, ALU.max).then_inc(rises_step, 1)

            def rises_of(n):
                v.tensor_tensor(rises[:, n % 2, :], run_max[:, n % 2, 1:1 + W], run_max[:, n % 2, 0:W], ALU.subtract
                                ).then_inc(rises_step, 1)

            running_max(0)
            running_max(1)
            v.wait_ge(rises_step, 2)
            rises_of(0)
            rises_of(1)
            v.wait_ge(rises_step, 3)
            for n, i in enumerate(range(S - 1, -1, -1)):
                v.scalar_tensor_tensor(out=pick[:, :], in0=jj2[:, :], scalar=vals[:, i + 1:i + 2],
                                       in1=rises[:, n % 2, :], op0=ALU.is_le, op1=ALU.mult, accum_out=pickm[:, :]
                                       ).then_inc(back, 1)
                if n + 2 < S:
                    running_max(n + 2)
                v.wait_ge(back, 2 * n + 1)
                v.tensor_reduce(vals[:, i:i + 1], pickm[:, :].to_broadcast([P, C]), AX.X, ALU.max,
                                apply_transpose=True).then_inc(back, 1)
                if n + 2 < S:
                    v.wait_ge(rises_step, 2 * n + 5)
                    rises_of(n + 2)
                else:
                    v.wait_ge(rises_step, 2 * S)
                v.wait_ge(back, 2 * n + 2)
            v.wait_ge(vcol_done, 1)
            ends = bank(2, 2 * P, S).rearrange("p (k b c) -> p k b c", k=2, b=B)
            v.tensor_copy(vcol[:, :, :], ends[:, :, :, 0]).then_inc(vcol_out, 1)
            v.wait_ge(vcol_out, 1)
            v.scalar_tensor_tensor(out=span[:, 0, :], in0=vcol[:, 0, :], scalar=-1.0, in1=vcol[:, 1, :],
                                   op0=ALU.mult, op1=ALU.subtract).then_inc(vcol_out, 1)
            v.tensor_tensor(span[:, 1, :], vcol[:, 1, :], vcol[:, 0, :], ALU.subtract).then_inc(vcol_out, 1)
            v.wait_ge(vcol_out, 3)
            for b in range(B):
                v.wait_ge(away_done, b + 1)
                v.tensor_scalar(Mb[:, b, :], away[:, b, :], span[:, 1, b:b + 1], None, ALU.is_le).then_inc(mask_done, 1)
            for k in range(4):
                v.wait_ge(al_done, k + 1)
                x4 = X[:, 4 * k:4 * k + 4, :]
                v.scalar_tensor_tensor(out=x4, in0=bank(3 + k).rearrange("p (w d) -> p w d", w=4), scalar=tg[:, 1:2],
                                       in1=x4, op0=ALU.mult, op1=ALU.add).then_inc(al_used, 1)

            ln_statistics(LN_G1, X, W, lambda w: v.wait_ge(al_used, w // 4 + 1), ONE_NORM + TWO_NORMS)
            ln_apply(X, Y, LN_BY_DVE)
            ln_apply(X, Y2, range(W), 1)
            v.wait_ge(logits_done, 2)
            lg1 = scr[:, :, 0:E1]
            did(v.tensor_copy(lg1, bank(7, W * E1).rearrange("p (w e) -> p w e", w=W)))
            so_far()
            top_two(lg1, E1)
            did(v.tensor_tensor(small[:, 0, :], top[:, :, 1], top[:, :, 0], ALU.subtract))
            v.wait_ge(route_exp, 2)
            did(v.tensor_scalar(small[:, 2, :], small[:, 1, :], 1.0, None, ALU.add))
            so_far()
            did(v.reciprocal(small[:, 3, :], small[:, 2, :]))
            so_far()
            did(v.tensor_tensor(small[:, 4, :], small[:, 1, :], small[:, 3, :], ALU.mult))
            so_far()
            v.tensor_tensor(oh1[:, :, 0:E1], oh1[:, :, 0:E1], per_token(small[:, 3, :], E1), ALU.mult)
            did(v.tensor_tensor(oh2[:, :, 0:E1], oh2[:, :, 0:E1], per_token(small[:, 4, :], E1), ALU.mult))
            so_far()
            did(v.tensor_tensor(oh1[:, :, 0:E1], oh1[:, :, 0:E1], oh2[:, :, 0:E1], ALU.add))
            so_far()
            did(v.tensor_tensor(comb[:, :, 0:E1], oh1[:, :, 0:E1],
                                alpha[:, :].unsqueeze(1).to_broadcast([P, W, E1]), ALU.mult))
            assert r[0] == R_COMB0 + R_L1, r[0]
            comb_low(1, E1)

            def gelu_low(b, u):
                n = 32 * b + u
                v.wait_ge(gelu_hi_done, n + 1)
                v.tensor_tensor(gelu_lo[:, u % 4, :], gelu[:, u % 4, :], gelu_hi[:, u % 4, :].bitcast(F32),
                                ALU.subtract).then_inc(gelu_lo_done, 1)

            def block1(b, last):
                acc = T1[:, bass.ds(4 * b, 4), :].rearrange("p w n -> p (w n)")
                for u in range(3, 35):
                    if not (last and u > 31):
                        gelu_low(b, u)
                    e, step = (u - 4) // 4, u % 4
                    n = E1 * b + e
                    if last and u > 31 and u < 34:
                        block_out(u - 32)
                    if u > 3 and step == 0:
                        v.wait_ge(cb1, n + 1)
                        v.tensor_copy(cbs[:, e % 2, :], bank(6 + e % 2)).then_inc(cbs1, 1)
                    if u > 3 and step == 1:
                        v.wait_ge(cbs1, n + 1)
                        v.wait_ge(down1, 4 * n + 8)
                        v.scalar_tensor_tensor(out=yt[:, e % 2, :] if e else acc, in0=bank(4 + e % 2),
                                               scalar=col("fc2_b", e), in1=cbs[:, e % 2, :],
                                               op0=ALU.add, op1=ALU.mult).then_inc(y1_used, 1)
                    if step == 2 and e:
                        v.wait_ge(y1_used, n + 3)
                        if e > 1:
                            v.wait_ge(acc1, 7 * b + e - 1)
                        v.tensor_tensor(acc, acc, yt[:, e % 2, :], ALU.add).then_inc(acc1, 1)

            def block_out(g):
                v.wait_ge(t_done, 4 * T_OUT + g + 1)
                x4 = X[:, 4 * g:4 * g + 4, :]
                v.scalar_tensor_tensor(out=x4, in0=bank(g).rearrange("p (w d) -> p w d", w=4), scalar=tg[:, 3:4],
                                       in1=x4, op0=ALU.mult, op1=ALU.add).then_inc(t_evac, 1)

            for u in range(3):
                gelu_low(0, u)
            with v.Fori(0, B - 1) as b:
                block1(b, False)
            block1(B - 1, True)
            block_out(2)
            block_out(3)

        @block.scalar
        def _(s):
            s.dma_start(X[:, :, :], xv).then_inc(in_x, 16)
            s.dma_start(wkv, a["L0_xattn_Wkv"]).then_inc(in_wkv, 16)
            s.sem_inc(pt_free, 3)
            s.sem_inc(acc0, 1)
            s.sem_inc(gelu1, 4)

            def col(name, k=0):
                return cols[:, COL[name] + k:COL[name] + k + 1]

            s.wait_ge(const0, 3)

            brought = []

            def bring(function):
                k = len(brought)
                brought.append(function)
                s.activation(unused[:, k:k + 1], eps_col[:, :], function)

            def ln_root(k, f=1, n=W, parts=P):
                s.wait_ge(ln_var, k + 1)
                s.activation(lnw[0:parts, 8:8 + f, 0:n], lnw[0:parts, 6:6 + f, 0:n], ACT.Sqrt).then_inc(ln_sqrt, 1)

            def ln_apply(k, src, dst):
                s.wait_ge(ln_shift, k - LN_LAT)
                for w in LN_BY_ACT:
                    s.activation(dst[:, w, :], src[:, w, :], ACT.Identity, bias=lnw[:, 12, w:w + 1],
                                 scale=lnw[:, 10, w:w + 1]).then_inc(ln_act, 1)

            bring(ACT.Sqrt)
            ln_root(LN_CTX, n=B, parts=S)
            s.dma_start(wo[:, :, :], a["L0_xattn_Wo"].rearrange("(q i) d -> i q d", i=P)).then_inc(in_wo, 16)
            s.wait_ge(ln_c_done, 1)
            s.activation(ln_c[:, :], bank(6, 2), ACT.Copy).then_inc(ln_c_out, 1)
            for n in range(N_PREP):
                if BY_ACT[n]:
                    s.wait_ge(prep_done, n + 1)
                    if n == I_CLT:
                        s.wait_ge(ln_c_out, 1)
                        s.activation(clT, bank(2 + n % 4, B * S), ACT.Identity, bias=ln_c[:, 1:2],
                                     scale=ln_c[:, 0:1]).then_inc(prep_act, 1)
                    else:
                        prep_out(n, lambda o, i: s.activation(o, i, ACT.Copy)).then_inc(prep_act, 1)
                if n == I_K:
                    ln_root(LN_LAT)
                b = (n - I_BT) // 3
                if n >= I_BT and n < I_B and (n - I_BT) % 3 == 2 and b < B:
                    if b == 0:
                        s.wait_ge(prep_act, emptied(I_BT - 1)[0])
                        s.wait_ge(prep_dve, emptied(I_BT - 1)[1])
                    s.activation(A_hi[:, b, :], A[:, b, :], ACT.Copy).then_inc(A_hi_done, 1)
                if n == I_K + 5:
                    s.wait_ge(prep_act, I_CT + 1)
                    s.activation(csq[:, :, :], cT[:, :, :], ACT.Square).then_inc(misc_act, 1)
            s.wait_ge(in_small, 16 * N_SMALL)
            s.activation(tg[:, :], gains[:, :], ACT.Tanh).then_inc(misc_act, 1)
            bring(ACT.Exp)

            def exps(n, jj):
                s.wait_ge(pt_done, 3 * n + 3)
                h0 = 0
                for k, nh in enumerate(SCORE_HEADS):
                    s.wait_ge(score_done, 3 * n + k + 1)
                    s.activation(Et[:, jj % 4, h0 * S:(h0 + nh) * S], bank(2 + (3 * jj + k) % 4, nh * S), ACT.Exp,
                                 scale=DH ** -0.5).then_inc(exp_done, 1)
                    h0 += nh

            def weights_out(n, b, j):
                for g in range(3):
                    s.wait_ge(pt_done, 12 + 3 * n + g + 1)
                    if j == 0 and g == 0:
                        s.wait_ge(pv_done, b + 1)
                    k0 = 4 * g
                    src = PS[:, PT_BANKS[g], :].rearrange("p (k n) -> p k n", k=4)
                    if g < 2:
                        s.activation(PT[:, k0:k0 + 4, P * j:P * j + P], src, ACT.Copy).then_inc(pt_free, 1)
                    else:
                        s.activation(PT[:, 8, P * j:P * j + P], src[:, 0, :], ACT.Copy)
                        s.activation(PT[0:KC[9], 9, P * j:P * j + P], src[0:KC[9], 1, :], ACT.Copy).then_inc(pt_free, 1)

            exps(0, 0)
            exps(1, 1)

            def attention(b, last):
                for j in range(4):
                    if not (last and j > 1):
                        exps(4 * b + j + 2, j + 2)
                    weights_out(4 * b + j, b, j)

            with s.Fori(0, B - 1) as b:
                attention(b, False)
            attention(B - 1, True)

            def t_copy(k, dst):
                for g in range(4):
                    s.wait_ge(t_done, 4 * k + g + 1)
                    s.activation(dst[:, 4 * g:4 * g + 4, :], bank(g % 2).rearrange("p (w n) -> p w n", w=4),
                                 ACT.Copy).then_inc(t_evac, 1)

            s.wait_ge(in_e0, 16 * 8)
            for w, w_hi, _ in SPLIT0:
                s.activation(w_hi, w, ACT.Copy).then_inc(w0_hi, 1)
            s.wait_ge(sel_ready, 9)
            for k in (0, LO):
                s.activation(be2_hi[k:k + E0, :], be2[k:k + E0, :], ACT.Copy).then_inc(be2_split, 1)
            bring(ACT.Sqrt)
            ln_root(LN_E0)
            ln_apply(LN_E0, X, Y)

            def t_copy_split(k, full, high):
                for g in range(4):
                    s.wait_ge(t_done, 4 * k + g + 1)
                    src = bank(g % 2).rearrange("p (w n) -> p w n", w=4)
                    s.activation(full[:, 4 * g:4 * g + 4, :], src, ACT.Copy)
                    s.activation(high[:, 4 * g:4 * g + 4, :], src, ACT.Copy).then_inc(t_evac, 1)

            def comb_high(layer, n):
                for g, k in enumerate(COMB_BANKS):
                    s.wait_ge(combT_done, 4 * layer + g + 1)
                    s.activation(combT[0:n, N * g:N * g + N], bank(k, parts=n), ACT.Copy).then_inc(comb_hi, 1)

            s.wait_ge(b_slot, B)
            t_copy_split(T_E0, T1, x0_hi)
            bring(ACT.Exp)
            s.wait_ge(route, 2)
            s.activation(pr, scr, ACT.Exp).then_inc(route_exp, 1)
            bring(ACT.Silu)
            comb_high(0, E0)

            def silu_unit(b, u):
                s.wait_ge(up0, 9 * b + u + 1)
                u = u % 9
                s.activation(silu[:, u % 3, :], bank(u % 3), ACT.Silu,
                             bias=col("be1", u - 1) if u else col("bs1")).then_inc(silu0, 1)

            def glu_high(b, u):
                n = 9 * b + u
                if u % 9:
                    s.wait_ge(scaled0, 8 * b + u)
                else:
                    s.wait_ge(glu0, n + 4)
                s.wait_ge(down0, n + 1)
                s.activation(glu_hi[:, u % 3, :], glu[:, u % 3, :], ACT.Copy).then_inc(glu_hi_done, 1)

            def block0(b, last):
                for u in range(1, 9):
                    if not (last and u == 8):
                        silu_unit(b, u + 1)
                    glu_high(b, u)
                if not last:
                    silu_unit(b, 10)
                s.wait_ge(down0, 9 * b + 12)
                s.activation(T2[:, bass.ds(4 * b, 4), :], bank(6).rearrange("p (w n) -> p w n", w=4), ACT.Identity,
                             bias=bs2g[:, :], scale=tg[:, 2:3]).then_inc(acc0, 1)
                if not last:
                    glu_high(b, 9)

            s.wait_ge(misc_dve, 1)
            silu_unit(0, 0)
            silu_unit(0, 1)
            glu_high(0, 0)
            with s.Fori(0, B - 1) as b:
                block0(b, False)
            block0(B - 1, True)

            bring(ACT.Sqrt)
            ln_root(LN_DTW)
            ln_apply(LN_DTW, X, Y)
            t_copy(T_DTW, T1)
            ln_wait(s, LN_DTW)
            s.activation(Y2[:, :, :], Y[:, :, :], ACT.Square).then_inc(sq_done, 1)
            s.wait_ge(cost_step, 7)
            s.activation(Dt[:, :, 0:W], Dt[:, :, 0:W], ACT.Sqrt).then_inc(cost_sqrt, 1)

            for e in range(E1):
                s.wait_ge(fc1_scaled, e + 1)
                s.activation(fc1_hi[:, e, :], fc1[:, e, :], ACT.Copy).then_inc(fc_hi, 1)
            s.wait_ge(in_fc2, 16)
            s.wait_ge(choice, len(CHOICE) - 1)
            s.wait_ge(last_choice, 1)
            for e in range(E1):
                s.activation(fc2_hi[:, e, :, :], fc2[:, e, :, :], ACT.Copy).then_inc(fc_hi, 1)
            for b in range(B):
                s.wait_ge(vcol_out, 3)
                s.activation(away[:, b, :], jrow[:, :], ACT.Abs, bias=span[:, 0, b:b + 1]).then_inc(away_done, 1)
            bring(ACT.Sqrt)
            ln_root(LN_G1, 2)
            ln_apply(LN_G1, X, Y)
            t_copy(T_G1, T1)
            t_copy_split(T_E1, T2, x1_hi)
            bring(ACT.Exp)
            s.wait_ge(route, R_COMB0 + R_EXP1)
            s.activation(small[:, 1, :], small[:, 0, :], ACT.Exp).then_inc(route_exp, 1)
            bring(ACT.Gelu_apprx_tanh)
            comb_high(1, E1)

            def gelu_unit(b, u):
                n = 32 * b + u
                s.wait_ge(up1, n + 1)
                s.wait_ge(gelu_lo_done, n + 1)
                s.activation(gelu[:, u % 4, :], bank(u % 4), ACT.Gelu_apprx_tanh, bias=b1c[:, u:u + 1]).then_inc(gelu1, 1)

            def gelu_high(b, u):
                n = 32 * b + u
                s.wait_ge(gelu1, n + 5)
                s.wait_ge(down1, n + 1)
                s.activation(gelu_hi[:, u % 4, :], gelu[:, u % 4, :], ACT.Copy).then_inc(gelu_hi_done, 1)

            s.wait_ge(b1_out, 1)
            with s.Fori(0, B) as b:
                for u in range(32):
                    gelu_unit(b, u)
                    gelu_high(b, u)

        @block.tensor
        def _(pe):
            pe.sem_inc(pt_done, 12)
            pe.sem_inc(pv_done, 1)
            pe.sem_inc(down0, 3)
            pe.sem_inc(down1, 4)

            def t_set(k, src, ready, after=None):
                for g in range(4):
                    n = 4 * k + g
                    if n > 1:
                        pe.wait_ge(t_evac, n - 1)
                    for w in range(4 * g, 4 * g + 4):
                        ready(w)
                        ins = pe.transpose(bank(g % 2, P, lo=P * (w % 4)), src[:, w, :], ident[:, :])
                    ins.then_inc(t_done, 1)
                    if after and g:
                        after(g - 1)
                if after:
                    after(3)

            def warm(n, k=7):
                for _ in range(n):
                    pe.matmul(bank(k, P), ident[:, :], ident[:, :], start=True, stop=True)

            def normed(k):
                return lambda w: ln_wait(pe, k, w)

            def logits(k, weights, n):
                def group(g):
                    pe.wait_ge(t_evac, 4 * k + g + 1)
                    for w in range(4 * g, 4 * g + 4):
                        ins = pe.matmul(bank(7, n, lo=n * w), T1[:, w, :], weights, start=True, stop=True)
                    if g == 3:
                        ins.then_inc(logits_done, 1)
                return group

            def transpose_comb(n):
                for g, k in enumerate(COMB_BANKS):
                    for q in range(4):
                        ins = pe.transpose(bank(k, P, n, P * q), comb[:, 4 * g + q, 0:n], ident[:, :])
                    ins.then_inc(combT_done, 1)

            def item(n):
                if n >= 4:
                    q = emptied(n - 4)
                    pe.wait_ge(prep_act if BY_ACT[n - 4] else prep_dve, q[0] if BY_ACT[n - 4] else q[1])
                return 2 + n % 4

            def have(n):
                q = emptied(n)
                pe.wait_ge(prep_act, q[0])
                if q[1]:
                    pe.wait_ge(prep_dve, q[1])

            pe.wait_ge(consts, 1)
            warm(14)
            pe.wait_ge(in_ctx, 16)
            for b in range(B):
                ins = pe.transpose(bank(2, S, lo=S * b), cn[:, b, :], ident[0:S, 0:S])
            ins.then_inc(prep_done, 1)
            pe.wait_ge(in_ln_c, 32)
            pe.transpose(bank(6, 2), ln_c_rows[:, :], ident[0:2, 0:2]).then_inc(ln_c_done, 1)
            pe.wait_ge(ln_dve, B)
            for b in range(B):
                ins = pe.transpose(bank(3, S, lo=S * b), cln[:, b, :], ident[0:S, 0:S])
            ins.then_inc(prep_done, 1)
            pe.wait_ge(in_wkv, 16)
            have(I_CLT)
            for q in range(16):
                k = item(I_K + q)
                pe.matmul(bank(k, B * S), wkv[:, P * q:P * q + P], clT, start=True, stop=True).then_inc(prep_done, 1)
            pe.wait_ge(in_wq, 16)
            for g in range(2):
                k = item(I_WQ + g)
                for q in range(4):
                    ins = pe.transpose(bank(k, P, lo=P * q), wq[:, P * (4 * g + q):P * (4 * g + q + 1)], ident[:, :])
                ins.then_inc(prep_done, 1)
            pe.wait_ge(in_rows, 16 * N_ROWS_DMA)
            k = item(I_COLS)
            pe.transpose(bank(k, NROWS), rows[:, :], ident[0:NROWS, 0:NROWS])
            pe.transpose(bank(k, E0, lo=NROWS), gate_rows[:, :], ident[0:E0, 0:E0]).then_inc(prep_done, 1)
            t_set(T_LAT, Y, normed(LN_LAT))
            have(I_COLS)
            for h in range(H):
                k = item(I_A + h)
                r = slice(DH * (h % 2), DH * (h % 2) + DH)
                pe.matmul(bank(k, B * S), wqT[r, P * (h // 2):P * (h // 2) + P], kT[r, h // 2, :],
                          start=True, stop=True).then_inc(prep_done, 1)
            pe.wait_ge(in_wo, 16)
            have(I_A - 1)
            for h in range(H):
                k = item(I_BT + h)
                r = slice(DH * (h % 2), DH * (h % 2) + DH)
                pe.matmul(bank(k, B * S), wo[r, h // 2, :], vT[r, h // 2, :], start=True, stop=True).then_inc(prep_done, 1)
            have(I_B - 1)
            pe.wait_ge(const0, 12)
            for b in range(B):
                for g, ks in enumerate(B_GROUPS):
                    k = item(I_B + 3 * b + g)
                    for q in ks:
                        ins = pe.transpose(bank(k, P, KC[q], P * (q % 4)), BT[:, b, P * q:P * q + KC[q]], ident[:, :])
                    ins.then_inc(prep_done, 1)
            have(N_PREP - 1)

            def split_product(dst, w_hi, w_lo, x_hi, x_lo, start=True, stop=True, before_last=None):
                pe.matmul(dst, w_lo, x_hi, start=start, stop=False)
                pe.matmul(dst, w_hi, x_lo, start=False, stop=False)
                if before_last is not None:
                    pe.wait_ge(*before_last)
                return pe.matmul(dst, w_hi, x_hi, start=False, stop=stop)

            def scores(n, b, jj):
                pe.wait_ge(lat_slot, n + 1)
                h0 = 0
                for k, nh in enumerate(SCORE_HEADS):
                    m = 3 * jj + k
                    if jj >= 3:
                        pe.wait_ge(exp_done, 3 * n + k - 3)
                    elif m >= 4:
                        pe.wait_ge(exp_done, m - 3)
                    a_hi, a_lo = (q[:, bass.ds(b, 1), h0 * S:(h0 + nh) * S].rearrange("p b n -> p (b n)")
                                  for q in (A_hi, A_lo))
                    split_product(bank(2 + m % 4, nh * S), latb_hi[:, jj % 4, :], latb_lo[:, jj % 4, :], a_hi, a_lo
                                  ).then_inc(score_done, 1)
                    h0 += nh

            def transpose_weights(n, j):
                pe.wait_ge(softmax_step, 4 * n + 4)
                for g, ks in enumerate(B_GROUPS):
                    pe.wait_ge(pt_free, 3 * n + g + 1)
                    for q in ks:
                        ins = pe.transpose(bank(PT_BANKS[g], P, KC[q], P * (q % 4)),
                                           Et[:, j, P * q:P * q + KC[q]], ident[:, :])
                    ins.then_inc(pt_done, 1)

            def attention(b, last):
                for j in range(4):
                    transpose_weights(4 * b + j, j)
                    if not (last and j > 0):
                        scores(4 * b + j + 3, b if j < 1 else b + 1, j + 3)
                pe.wait_ge(b_slot, b + 1)
                pe.wait_ge(pv_free, b + 1)
                pe.wait_ge(pt_free, 3 + 3 * (4 * b + 3) + 3)
                for q, kc in enumerate(KC):
                    ins = pe.matmul(bank(6), Bs[0:kc, q, :], PT[0:kc, q, :], start=(q == 0), stop=(q == len(KC) - 1))
                ins.then_inc(pv_done, 1)

            pe.wait_ge(t_evac, 4 * T_LAT + 4)
            pe.wait_ge(A_lo_done, B)
            for n in range(3):
                scores(n, 0, n)
            with pe.Fori(0, B - 1) as b:
                attention(b, False)
            attention(B - 1, True)
            pe.wait_ge(pv_free, 1 + B)
            t_set(T_X1, T2, lambda w: None)
            warm(24)

            t_set(T_E0, Y, normed(LN_E0), logits(T_E0, cols[:, NROWS:NROWS + E0], E0))

            def up_unit0(b, u, before_last=None):
                n = 9 * b + u
                if u > 8:
                    b, u = b + 1, u - 9
                x_hi, x_lo = (q[:, bass.ds(4 * b, 4), :].rearrange("p w n -> p (w n)") for q in (x0_hi, x0_lo))
                pe.wait_ge(glu0, n + 1)
                w1_hi, w1_lo, w3_hi, w3_lo = (
                    (q[:, 2 * u - 2:2 * u, :].rearrange("p e i -> p (e i)") if u else shared[:, :])
                    for q, shared in ((we1_hi, ws1_hi), (we1_lo, ws1_lo), (we3_hi, ws3_hi), (we3_lo, ws3_lo)))
                split_product(bank(3 + u % 3), w3_hi, w3_lo, x_hi, x_lo)
                split_product(bank(u % 3), w1_hi, w1_lo, x_hi, x_lo, before_last=before_last).then_inc(up0, 1)

            def block0(b, last):
                cols_b = bass.ds(b * N, N)
                for u in range(9):
                    free = (acc0, b + 1) if u == 0 else (scaled0, 8 * b + u)
                    if not (last and u > 6):
                        up_unit0(b, u + 2, free)
                    if u == 0:
                        pe.wait_ge(comb_lo, 4)
                        pe.matmul(bank(6), be2_lo[:, :], combT[:, cols_b], start=True, stop=False)
                        pe.matmul(bank(6), be2_hi[:, :], combT[:, cols_b], start=False, stop=False)
                    if u < 8:
                        if last and u == 7:
                            pe.wait_ge(scaled0, 8 * B - 1)
                        pe.matmul(bank(7), sel0[:, u, :], combT[:, cols_b], start=True, stop=True).then_inc(cb0, 1)
                    pe.wait_ge(glu_lo_done, 9 * b + u + 1)
                    split_product(bank(6), *((we2_hi[:, u - 1, :], we2_lo[:, u - 1, :]) if u else (ws2_hi[:, :], ws2_lo[:, :])),
                                  glu_hi[:, u % 3, :], glu_lo[:, u % 3, :], start=False, stop=(u == 8)).then_inc(down0, 1)

            pe.wait_ge(w0_lo, len(SPLIT0))
            pe.wait_ge(x0_lo_done, 1)
            pe.wait_ge(t_evac, 4 * T_E0 + 3)
            up_unit0(0, 0)
            pe.wait_ge(t_evac, 4 * T_E0 + 4)
            up_unit0(0, 1)
            warm(28, 2)
            pe.wait_ge(route, R_COMB0)
            pe.wait_ge(sel_ready, 9)
            transpose_comb(E0)
            pe.wait_ge(comb_lo, 2)
            pe.wait_ge(x0_lo_done, 4)
            pe.wait_ge(be2_split, 3)
            with pe.Fori(0, B - 1) as b:
                block0(b, False)
            block0(B - 1, True)
            pe.wait_ge(acc0, 1 + B)
            t_set(T_X2, T2, lambda w: None)
            warm(32)

            pe.wait_ge(misc_act, 2)
            for b in range(B):
                ins = pe.matmul(PS[C * b:C * b + C, 5, 0:S], ones[:, :], csq[:, b, :], start=True, stop=True)
            ins.then_inc(aab_done, 1)
            t_set(T_DTW, Y, normed(LN_DTW))
            pe.wait_ge(t_evac, 4 * T_DTW + 4)
            for k, (lo, hi) in enumerate(COST_BANKS):
                for w in range(lo, hi):
                    for b in range(B):
                        ins = pe.matmul(PS[C * b:C * b + C, 2 + k, S * (w - lo):S * (w - lo) + S],
                                        T1[:, w, C * b:C * b + C], cT[:, b, :], start=True, stop=True)
                ins.then_inc(cost_mm, 1)
            pe.wait_ge(in_fc1, 16)
            for e in range(E1):
                for f in range(4):
                    ins = pe.matmul(bank(7, 1, lo=4 * e + f), fc1[:, e, P * f:P * f + P],
                                    cols[:, COL["ln_b"] + e:COL["ln_b"] + e + 1], start=True, stop=True)
            ins.then_inc(b1_done, 1)

            pe.wait_ge(back, 2 * (S - 9))
            warm(14)
            pe.wait_ge(back, 2 * S)
            pe.wait_ge(dve_consts, 2)
            pe.transpose(bank(2, P, S), vals[:, 0:S], ident[:, :])
            pe.transpose(bank(2, P, S, P), vals[:, 1:S + 1], ident[:, :]).then_inc(vcol_done, 1)
            warm(6)
            for b in range(B):
                pe.wait_ge(mask_done, b + 1)
                for w in range(W):
                    mask = Mb[:, b, :].rearrange("p (c w) -> p c w", w=W)[:, :, w]
                    ins = pe.matmul(PS[C * b:C * b + C, 3 + w // 4, P * (w % 4):P * (w % 4) + P], mask, cn[:, b, :],
                                    start=True, stop=True)
                    if b == B - 1 and w % 4 == 3:
                        ins.then_inc(al_done, 1)
            warm(24)

            t_set(T_G1, Y, normed(LN_G1), logits(T_G1, wg1[:, :], E1))
            t_set(T_E1, Y2, lambda w: pe.wait_ge(ln_dve, B + W + 3 * len(LN_BY_DVE) + w + 1))
            pe.wait_ge(fc_lo, 2 * E1)
            pe.wait_ge(x1_lo_done, 1)

            def up_unit1(b, u, before_last=None):
                n = 32 * b + u
                if u > 31:
                    b, u = b + 1, u - 32
                e, f = u // 4, slice(P * (u % 4), P * (u % 4) + P)
                x_hi, x_lo = (q[:, bass.ds(4 * b, 4), :].rearrange("p w n -> p (w n)") for q in (x1_hi, x1_lo))
                pe.wait_ge(gelu1, n + 1)
                split_product(bank(u % 4), fc1_hi[:, e, f], fc1_lo[:, e, f], x_hi, x_lo, before_last=before_last
                              ).then_inc(up1, 1)

            def transpose_out(g):
                pe.wait_ge(gelu1, 32 * B + g + 1)
                for w in range(4 * g, 4 * g + 4):
                    ins = pe.transpose(bank(g, P, lo=P * (w % 4)), T1[:, w, :], ident[:, :])
                ins.then_inc(t_done, 1)

            def block1(b, last):
                for u in range(32):
                    e, f = u // 4, u % 4
                    if last and u > 29:
                        transpose_out(u - 30)
                    free = (y1_used, E1 * b + e + 1) if f == 0 else None
                    if not (last and u > 29):
                        up_unit1(b, u + 2, free)
                    if e < 2 and f == 0:
                        pe.wait_ge(comb_lo, 8 if e else 7)
                    if f == 0:
                        pe.matmul(bank(6 + e % 2), sel1[:, e, :], combT[:, bass.ds(b * N, N)],
                                  start=True, stop=True).then_inc(cb1, 1)
                    pe.wait_ge(gelu_lo_done, 32 * b + u + 5)
                    split_product(bank(4 + e % 2), fc2_hi[:, e, f, :], fc2_lo[:, e, f, :], gelu_hi[:, f, :],
                                  gelu_lo[:, f, :], start=(f == 0), stop=(f == 3)).then_inc(down1, 1)

            pe.wait_ge(t_evac, 4 * T_E1 + 3)
            up_unit1(0, 0)
            pe.wait_ge(t_evac, 4 * T_E1 + 4)
            up_unit1(0, 1)
            pe.wait_ge(route, R_COMB0 + R_L1)
            transpose_comb(E1)
            pe.wait_ge(comb_lo, 5)
            pe.wait_ge(x1_lo_done, 4)
            with pe.Fori(0, B - 1) as b:
                block1(b, False)
            block1(B - 1, True)
            transpose_out(2)
            pe.wait_ge(acc1, 7 * B)
            transpose_out(3)


_INS = ["x", "ctx_1024", "g_xattn", "g_ffn",
        "L0_xattn_ln_l_w", "L0_xattn_ln_l_b", "L0_xattn_ln_c_w", "L0_xattn_ln_c_b", "L0_xattn_Wq", "L0_xattn_Wkv",
        "L0_xattn_Wo", "L0_xattn_bo", "L0_ffn_gate_w", "L0_ffn_gate_b", "L0_ffn_We1", "L0_ffn_be1", "L0_ffn_We2",
        "L0_ffn_be2", "L0_ffn_We3", "L0_ffn_be3", "L0_ffn_ws1", "L0_ffn_bs1", "L0_ffn_ws2", "L0_ffn_bs2",
        "L0_ffn_ws3", "L0_ffn_bs3", "L1_ffn_Wg", "L1_ffn_alpha", "L1_ffn_ln_w", "L1_ffn_ln_b", "L1_ffn_fc1_w",
        "L1_ffn_fc1_b", "L1_ffn_fc2_w", "L1_ffn_fc2_b"]


def kernel(**inputs):
    import numpy as _np
    import concourse.bacc as _bacc
    from concourse import mybir as _mybir
    from concourse.bass_utils import run_bass_kernel_spmd as _run

    nc = _bacc.Bacc("TRN2", target_bir_lowering=False, num_devices=1)
    arrays, args = {}, {}
    for name in _INS:
        v = _np.ascontiguousarray(inputs[name])
        arrays[f"in_{name}"] = v
        args[name] = nc.dram_tensor(f"in_{name}", v.shape, _mybir.dt.from_np(v.dtype), kind="ExternalInput").ap()
    out = nc.dram_tensor("out_0", (B, N, D), F32, kind="ExternalOutput").ap()
    build(nc, args, out)
    r = _run(nc, [arrays], core_ids=[0])
    return r.results[0]["out_0"]
```
